# Optimizing a Trainium2 kernel written in Bass

```python
import numpy as np
import jax
import jax.numpy as jnp

def _softmax(x, axis=-1):
    return jax.nn.softmax(x, axis=axis)

def _gelu(x):
    return jax.nn.gelu(x, approximate=True)

def _silu(x):
    return jax.nn.silu(x)

def _sigmoid(x):
    return jax.nn.sigmoid(x)

def _layernorm(x, axis=-1, eps=1e-05):
    m = jnp.mean(x, axis=axis, keepdims=True)
    v = jnp.var(x, axis=axis, keepdims=True)
    return (x - m) / jnp.sqrt(v + eps)

def _scatter_add(tgt, idx, src, axis=0):
    return tgt.at[idx].add(src)

def _segment_sum(src, seg, n):
    return jax.ops.segment_sum(src, seg, n)
kernel_name = 'mk_gnn_ffn_d1_gnn_r8_639efb'

def setup_inputs(seed: int=0):
    np.random.seed(seed)
    _w = jnp.asarray

    def _rec_inputs():
        import jax
        import jax.numpy as jnp
        _gk = jax.random.key(seed)
        x = -0.000202 + 1 * jax.random.normal(jax.random.fold_in(_gk, 1), (6250, 256), jnp.float32)
        src = jax.random.randint(jax.random.fold_in(_gk, 2), (100000,), 0, 6250, jnp.int32)
        dst = jax.random.randint(jax.random.fold_in(_gk, 3), (100000,), 0, 6250, jnp.int32)
        _o = jnp.argsort(dst, stable=True)
        src = src[_o]
        dst = dst[_o]
        return (x, src, dst)
    x, src, dst = _rec_inputs()

    def _L0_gnn_setup():
        import jax, jax.numpy as jnp
        import numpy as np
        N_NODES = 3125
        N_EDGES = 50000
        D = 256
        key = jax.random.key(seed)
        k1, k2, k3, k4, k5 = jax.random.split(key, 5)
        feat = jax.random.normal(k1, (N_NODES, D), dtype=jnp.float32)
        src = jax.random.randint(k2, (N_EDGES,), 0, N_NODES, dtype=jnp.int32)
        dst = jax.random.randint(k3, (N_EDGES,), 0, N_NODES, dtype=jnp.int32)
        a = float(np.sqrt(6.0 / (D + D)))
        W1 = jax.random.uniform(k4, (D, D), minval=-a, maxval=a, dtype=jnp.float32)
        W2 = jax.random.uniform(k5, (D, D), minval=-a, maxval=a, dtype=jnp.float32)
        b = jnp.zeros((D,), dtype=jnp.float32)
        return {'feat': feat, 'W1': W1, 'W2': W2, 'b': b, 'src': src, 'dst': dst}
    _L0_gnn_all = _L0_gnn_setup()
    _L0_gnn_in = {k: v for k, v in _L0_gnn_all.items() if k in ('W1', 'W2', 'b')}
    del _L0_gnn_all

    def _L0_ffn_setup():
        import jax, jax.numpy as jnp
        import numpy as np
        C = 256
        HID = 1024
        E = 8
        TEMP = 1.0
        key = jax.random.key(seed)
        ks = jax.random.split(key, 7)
        x = jax.random.normal(ks[0], (8, 2048, C), dtype=jnp.float32)
        W1 = jax.random.normal(ks[1], (C, HID), dtype=jnp.float32) * 0.02
        b1 = jnp.zeros((HID,), dtype=jnp.float32)
        Wg = jax.random.normal(ks[2], (HID, E), dtype=jnp.float32) * 0.02
        bg = jnp.zeros((E,), dtype=jnp.float32)
        Wd = jax.random.normal(ks[3], (E, HID, C), dtype=jnp.float32) * 0.02
        bd = jnp.zeros((E, C), dtype=jnp.float32)
        return {'x': x, 'W1': W1, 'b1': b1, 'Wg': Wg, 'bg': bg, 'Wd': Wd, 'bd': bd}
    _L0_ffn_all = _L0_ffn_setup()
    _L0_ffn_in = {k: v for k, v in _L0_ffn_all.items() if k in ('W1', 'b1', 'Wg', 'bg', 'Wd', 'bd')}
    del _L0_ffn_all
    return {'x': x, 'src': src, 'dst': dst, 'L0_gnn_W1': _L0_gnn_in['W1'], 'L0_gnn_W2': _L0_gnn_in['W2'], 'L0_gnn_b': _L0_gnn_in['b'], 'L0_ffn_W1': _L0_ffn_in['W1'], 'L0_ffn_b1': _L0_ffn_in['b1'], 'L0_ffn_Wg': _L0_ffn_in['Wg'], 'L0_ffn_bg': _L0_ffn_in['bg'], 'L0_ffn_Wd': _L0_ffn_in['Wd'], 'L0_ffn_bd': _L0_ffn_in['bd']}

def reference(x, src, dst, L0_gnn_W1, L0_gnn_W2, L0_gnn_b, L0_ffn_W1, L0_ffn_b1, L0_ffn_Wg, L0_ffn_bg, L0_ffn_Wd, L0_ffn_bd):
    import jax
    import jax.numpy as jnp

    def _L0_gnn_ref(feat, W1, W2, b, src, dst):
        import jax, jax.numpy as jnp
        import numpy as np
        N_NODES = 3125
        N_EDGES = 50000
        D = 256
        n = feat.shape[0]
        ones = jnp.ones(src.shape[0], dtype=feat.dtype)
        out_deg = jnp.maximum(jax.ops.segment_sum(ones, src, num_segments=n), 1.0)
        in_cnt = jax.ops.segment_sum(ones, dst, num_segments=n)
        t1 = feat @ W1
        msg = t1[src] + feat[src] * feat[dst] @ W2
        scale = jnp.sqrt(out_deg[src]) * jnp.sqrt(out_deg[dst])
        msg = msg / scale[:, None]
        agg = jax.ops.segment_sum(msg, dst, num_segments=n)
        embed = jnp.where(in_cnt[:, None] > 0, t1 + agg, jnp.zeros_like(t1))
        embed = embed + b
        embed = jax.nn.leaky_relu(embed, negative_slope=0.01)
        norm = jnp.linalg.norm(embed, axis=1, keepdims=True)
        embed = embed / jnp.maximum(norm, 1e-12)
        return embed

    def _L0_ffn_ref(x, W1, b1, Wg, bg, Wd, bd):
        import jax, jax.numpy as jnp
        import numpy as np
        C = 256
        HID = 1024
        E = 8
        TEMP = 1.0
        orig_shape = x.shape
        xf = x.reshape(-1, orig_shape[-1])
        H = jax.nn.gelu(xf @ W1 + b1, approximate=False)
        probs = jax.nn.softmax((H @ Wg + bg) / TEMP, axis=-1)
        assign = jnp.argmax(probs, axis=-1)
        out = jnp.zeros_like(xf)
        for e in range(Wd.shape[0]):
            y = H @ Wd[e] + bd[e]
            sel = (assign == e)[:, None]
            out = out + jnp.where(sel, probs[:, e:e + 1] * y, 0.0)
        return out.reshape(orig_shape)
    x = x + _L0_gnn_ref(_layernorm(x, axis=-1), L0_gnn_W1, L0_gnn_W2, L0_gnn_b, src, dst)
    x = x + _L0_ffn_ref(_layernorm(x, axis=-1)[None], L0_ffn_W1, L0_ffn_b1, L0_ffn_Wg, L0_ffn_bg, L0_ffn_Wd, L0_ffn_bd)[0]
    return x

_drawn_inputs = setup_inputs


def setup_inputs(seed=0):
    import zlib

    import numpy as np

    out = dict(_drawn_inputs(seed))
    spreads = {'L0_gnn_b': (0.0, 0.8),
     'L0_ffn_b1': (0.0, 0.567),
     'L0_ffn_bg': (0.0, 0.394),
     'L0_ffn_bd': (0.0, 0.562)}
    factors = {'L0_gnn_W2': 3.847, 'L0_ffn_Wg': 2.843, 'L0_ffn_Wd': 3.247}
    for name, (base, spread) in spreads.items():
        noise = np.random.default_rng([zlib.crc32(name.encode()), seed]).standard_normal(out[name].shape)
        drawn = base * np.exp(spread * noise) if base else spread * noise
        out[name] = jnp.asarray(drawn.astype(out[name].dtype))
    for name, factor in factors.items():
        out[name] = (out[name] * factor).astype(out[name].dtype)
    return out
```

```python
from contextlib import ExitStack

import concourse.bass as bass
from concourse import mybir

F32 = mybir.dt.float32
BF16 = mybir.dt.bfloat16
I32 = mybir.dt.int32
ALU = mybir.AluOpType
ACT = mybir.ActivationFunctionType
AX = mybir.AxisListType

P = 128
N = 6250
D = 256
NE = 100000
HID = 1024
EX = 8
KD = D // P
KH = HID // P
NT = (N + P - 1) // P
LASTN = N - (NT - 1) * P
ET = 4
GE = ET * P
NG = -(-NE // GE)
NET = NG * ET
WIN = 64
PER = 4
NI = NG // PER
LATE = 2
assert NI == NT and NI * PER == NG
SW = 512
NSW = -(-(N + WIN) // SW)
ACCW = NSW * SW
NB = 7
BR = NET // NB
FULLR = NE // P
RESTE = NE - FULLR * P
NJ = (N + EX * (P - 1)) // P
UN = 4
assert NJ % UN == 0
EPS = 1e-5
FAR = 100000.0


class Chain:

    def __init__(self, eng, sem):
        self.eng, self.sem, self.base, self.k = eng, sem, 0, 0

    def __call__(self, ins):
        ins.then_inc(self.sem, 1)
        self.k += 1
        self.eng.wait_ge(self.sem, self.base + self.k)

    def at(self, base):
        self.base, self.k = base, 0

    def count(self):
        return self.base + self.k


def build(nc, x, src, dst, gnn_w1, gnn_w2, gnn_b, w1, b1, wg, bg, wd, bd, out):
    ctx = ExitStack()
    with ctx:
        ctx.enter_context(nc.allow_non_contiguous_dma("small transposed bias loads"))

        def sb(name, shape, dt=F32):
            return ctx.enter_context(nc.sbuf_tensor(name, shape, dt))

        def bank(name):
            return ctx.enter_context(nc.psum_tensor(name, [P, 512], F32))

        def sem(name):
            return ctx.enter_context(nc.semaphore(name))

        g_dram = nc.dram_tensor("g_scratch", (NT * P, D), F32, kind="Internal").ap()
        tok_dram = nc.dram_tensor("tok_scratch", (NT * P, 2 * D), F32, kind="Internal").ap()

        accT = sb("accT", [P, KD, ACCW])
        big = sb("big", [P, EX * KH * D])
        wd_sb = big[:, :].rearrange("p (e c n) -> p (e c) n", e=EX, c=KH)
        xs = big[:, 0:NT * D].rearrange("p (t d) -> p t d", d=D)
        slow_oh = big[:, 0:ET * SW].rearrange("p (j w) -> p j w", j=ET)
        slow_iota = big[:, ET * SW:ET * SW + SW]
        SO = NT * D
        slo = big[:, SO:SO + NET]
        shi = big[:, SO + NET:SO + 2 * NET]
        rows = sb("rows", [P, PER, ET * D])
        w1_sb = sb("w1_sb", [P, KD, HID])
        gw_sb = sb("gw_sb", [P, 2 * KD, D])
        gb_sb = sb("gb_sb", [P, D])
        b1_sb = sb("b1_sb", [P, KH])
        wg_sb = sb("wg_sb", [P, KH, EX])
        bg_sb = sb("bg_sb", [P, EX])
        src_idx = sb("src_idx", [P, NET], I32)
        dstf = sb("dstf", [P, NET + ET])
        dlo = sb("dlo", [P, NET + ET])
        dhi = sb("dhi", [P, NET + ET])
        rel = sb("rel", [P, NET + ET])
        acc0 = accT[:, 0, :]
        acc1 = accT[:, 1, :]
        nat_i = [acc0[0:BR, k * NB * P:(k + 1) * NB * P].bitcast(I32).rearrange("p (b c) -> p b c", b=NB) for k in (0, 1)]
        nat_f = [acc0[0:BR, (2 + k) * NB * P:(3 + k) * NB * P].rearrange("p (b c) -> p b c", b=NB) for k in (0, 1)]
        raw_i = acc1[:, 0:NET].bitcast(I32)
        part_i = acc1[:, NET:2 * NET].bitcast(I32)
        part2_i = acc1[:, 2 * NET:3 * NET].bitcast(I32)
        viol = acc1[:, 3 * NET:4 * NET]
        viol2 = acc1[:, 4 * NET:5 * NET]
        NJUNK = 8
        junk = [acc1[:, 5 * NET + q * D:5 * NET + (q + 1) * D] for q in range(NJUNK)]

        ident = sb("ident", [P, P])
        ones = sb("ones", [P, P])
        row0 = sb("row0", [P, P])
        upper = sb("upper", [P, P], BF16)
        ones_h = sb("ones_h", [P, P], BF16)
        iota_i = sb("iota_i", [P, SW], I32)
        iota_f = sb("iota_f", [P, P])
        iota_h = sb("iota_h", [P, P], BF16)
        lim_i = sb("lim_i", [P, NG], I32)
        limf = sb("limf", [P, NG])
        basef = sb("basef", [P, NG])
        base_i = sb("base_i", [1, NG], I32)
        flag_i = sb("flag_i", [1, 1], I32)
        small = sb("small", [P, 8])
        idx = sb("idx", [P, PER, ET], I32)
        hoh = sb("hoh", [P, 2, 8, 2 * P], BF16)
        woh = sb("woh", [P, 2, ET, WIN])
        ssum = sb("ssum", [P, NT])
        nmean = sb("nmean", [P, NT])
        ssq = sb("ssq", [P, NT])
        rstd = sb("rstd", [P, NT])
        nb = sb("nb", [P, NT])
        deg = sb("deg", [P, NT])
        rs = sb("rs", [P, NT])
        gsc = sb("gsc", [P, NT])
        gsb = sb("gsb", [P, NT])
        usc = sb("usc", [P, NT])
        usb = sb("usb", [P, NT])

        xin = sb("xin", [P, D])
        fu = sb("fu", [P, 2, D])
        lT = sb("lT", [P, 2 * KD, P])
        emb = sb("emb", [P, D])
        emb2 = sb("emb2", [P, D])
        sqj = sb("sqj", [P, D])
        xcat = sb("xcat", [P, 2 * D])
        xT = sb("xT", [P, 2, KD, P])
        hT = sb("hT", [P, 2, KH, P])
        reff = sb("reff", [P, 1])
        ss = sb("ss", [P, 1])
        rn = sb("rn", [P, 1])
        nrm = sb("nrm", [P, 1])
        sd = sb("sd", [P, 1])
        eps_t = sb("eps_t", [P, 1])
        st6 = sb("st6", [P, 6])
        mv = sb("mv", [P, 2])
        rstd2 = sb("rstd2", [P, 1])
        logits = sb("logits", [P, NT, EX])

        bd_sb = acc1[:, 0:EX * D]
        LE = NT * EX
        carved = [0]

        def carve(n, dt=F32):
            at = carved[0]
            carved[0] += n
            assert carved[0] <= ACCW
            return acc0[:, at:at + n] if dt == F32 else acc0[:, at:at + n].bitcast(dt)

        te_view = lambda a: a.rearrange("p (t e) -> p t e", e=EX)
        et_view = lambda a: a.rearrange("p (e t) -> p e t", e=EX)
        ra, rb, oneh = te_view(carve(LE)), te_view(carve(LE)), te_view(carve(LE))
        oneh_h = sb("oneh_h", [P, NT, EX], BF16)
        tot, cum, keep = et_view(carve(LE)), et_view(carve(LE)), et_view(carve(LE))
        mx, prob, pos, plo, phi, valid = (carve(NT) for _ in range(6))
        pos_i, plo_i = carve(NT, I32), carve(NT, I32)
        tid_i = sb("tid_i", [P, NT], I32)
        tid = sb("tid", [P, NT])
        rank8_i = sb("rank8_i", [P, EX], I32)
        rank8 = sb("rank8", [P, EX])
        te, tinc, tstart = carve(EX), carve(EX), carve(EX)
        te_i = carve(EX, I32)
        one8 = sb("one8", [P, EX])
        zeros_h = sb("zeros_h", [P, P], BF16)
        jx = carve(NJ * EX)[0:1, :].rearrange("p (j e) -> p j e", e=EX)
        jexp = carve(NJ)[0:1, :]
        jexp_i = carve(NJ, I32)[0:1, :]
        ploh = carve(2 * P).rearrange("p (b n) -> p b n", b=2)
        phoh = carve(4 * NJ).rearrange("p (b a j) -> p b a j", b=2, a=2)
        slot = carve(2 * NJ).rearrange("p (a j) -> p a j", a=2)
        gidx, sidx = carve(NJ, I32), carve(NJ, I32)
        sidf = carve(NJ)
        gring = sb("gring", [P, UN], I32)
        sring = sb("sring", [P, UN], I32)
        trow = [rows[:, s, 0:2 * D] for s in range(UN)]
        obuf = [rows[:, s, 2 * D:3 * D] for s in range(UN)]
        yb = rows[:, 0, 3 * D:4 * D]

        bkA = [bank("bkA0"), bank("bkA1")]
        bkC = bank("bkC")
        bkT = bank("bkT")
        bkE = bank("bkE")
        bkH = [bank("bkH0"), bank("bkH1")]
        bkL = bank("bkL")
        bkT2 = (bkT, bkL)
        bkY = (bkE, bkC)
        segp = [b[:, 0:KD * WIN].rearrange("p (h w) -> p h w", h=KD) for b in bkA]

        pads_set = sem("pads_set"); edges_in = sem("edges_in"); x_in = sem("x_in"); weights_in = sem("weights_in")
        consts = sem("consts"); pool_own = sem("pool_own"); dve_own = sem("dve_own")
        nat_ready = sem("nat_ready"); tables_t = sem("tables_t"); tables_read = sem("tables_read")
        sums_done = sem("sums_done"); mean_ready = sem("mean_ready"); ssq_done = sem("ssq_done"); scales = sem("scales")
        hist_oh = sem("hist_oh"); hist_used = sem("hist_used"); hist_done = sem("hist_done"); cnt_zero = sem("cnt_zero")
        deg_read = sem("deg_read"); slow_own = sem("slow_own"); act_own = sem("act_own"); edge_own = sem("edge_own")
        g_act = sem("g_act"); g_dve = sem("g_dve"); g_stored = sem("g_stored"); acc_zero = sem("acc_zero")
        dst_ready = sem("dst_ready"); base_bc = sem("base_bc"); viol_ready = sem("viol_ready"); viol_sum = sem("viol_sum")
        flag_ready = sem("flag_ready")
        slow_idx = sem("slow_idx"); slow_landed = sem("slow_landed"); slow_oh_ready = sem("slow_oh_ready")
        slow_sum = sem("slow_sum"); slow_added = sem("slow_added"); slow_hist = sem("slow_hist")
        slow_hist_used = sem("slow_hist_used")
        idx_in = [sem(f"idx_in{s}") for s in range(PER)]
        landed = [sem(f"landed{s}") for s in range(PER)]
        oh_ready = sem("oh_ready"); seg_done = sem("seg_done"); seg_added = sem("seg_added")
        ehist_oh = sem("ehist_oh"); ehist_done = sem("ehist_done"); cnt_read = sem("cnt_read")
        xt_in = sem("xt_in"); fu_ready = sem("fu_ready"); fu_t = sem("fu_t"); l_ready = sem("l_ready")
        e_done = sem("e_done"); e_ready = sem("e_ready"); ss_ready = sem("ss_ready"); nrm_ready = sem("nrm_ready"); var_ready = sem("var_ready"); sd_ready = sem("sd_ready"); roots = sem("roots"); x2_ready = sem("x2_ready")
        xn_ready = sem("xn_ready"); xn_t = sem("xn_t"); xt_ready = sem("xt_ready")
        h_done = [sem("h_done0"), sem("h_done1")]; gelu_done = sem("gelu_done")
        lg_done = sem("lg_done"); lg_read = sem("lg_read"); tok_stored = sem("tok_stored"); wd_in = sem("wd_in"); bd_in = sem("bd_in")
        exp_in = sem("exp_in"); exp_done = sem("exp_done"); oneh_ready = sem("oneh_ready"); ranks = sem("ranks")
        pm_oh = sem("pm_oh"); pm_used = sem("pm_used"); slots_ready = sem("slots_ready")
        gi_in = [sem(f"gi_in{s}") for s in range(UN)]
        si_in = [sem(f"si_in{s}") for s in range(UN)]
        tok_in = [sem(f"tok_in{s}") for s in range(UN)]
        stored = [sem(f"stored{s}") for s in range(UN)]
        t2_done = sem("t2_done"); t2_read = sem("t2_read"); h2_done = sem("h2_done"); gelu2 = sem("gelu2")
        y_done = sem("y_done"); y_read = sem("y_read"); o_ready = sem("o_ready"); slots_used = sem("slots_used")

        ticks = sem("ticks")

        def wait_count(eng, s, value):
            eng.wait_ge(s, value)
            if not isinstance(value, int):
                eng.sem_inc(ticks, 1)

        block = ctx.enter_context(nc.Block())

        SEG1 = LATE + 1

        def edge_loop(eng, body):
            for i in range(SEG1):
                body(i)
            with eng.Fori(SEG1, NI) as i:
                body(i)

        @block.sync
        def _(sp):
            sp.wait_ge(pads_set, 3)
            for k, e in enumerate((src, dst)):
                full = (NB - 1) * BR
                sp.dma_start(nat_i[k][:, 0:NB - 1, :],
                             e[0:full * P].rearrange("(b p c) -> p b c", p=BR, c=P)).then_inc(edges_in, 16)
                sp.dma_start(nat_i[k][0:FULLR - full, NB - 1, :],
                             e[full * P:FULLR * P].rearrange("(p c) -> p c", c=P)).then_inc(edges_in, 16)
                sp.dma_start(nat_i[k][FULLR - full:FULLR - full + 1, NB - 1, 0:RESTE],
                             e[FULLR * P:NE].rearrange("(p c) -> p c", p=1)).then_inc(edges_in, 16)
            for c in range(6):
                sp.dma_start(xs[:, 8 * c:8 * c + 8, :],
                             x[8 * c * P:8 * (c + 1) * P, :].rearrange("(t p) d -> p t d", p=P)).then_inc(x_in, 16)
            sp.dma_start(xs[0:LASTN, NT - 1, :], x[(NT - 1) * P:N, :]).then_inc(x_in, 16)

            for c in range(7):
                if c < 3:
                    sp.wait_ge(g_act, c + 1)
                else:
                    sp.wait_ge(g_dve, c - 2)
                sp.dma_start(g_dram[7 * c * P:7 * (c + 1) * P, :].rearrange("(t p) d -> p t d", p=P),
                             xs[:, 7 * c:7 * c + 7, :]).then_inc(g_stored, 16)

            sp.wait_ge(flag_ready, 1)
            general = sp.value_load(flag_i[0:1, 0:1], min_val=0, max_val=1)
            with sp.If(general != 0):
                with sp.Fori(0, NG) as n:
                    sp.wait_ge(slow_sum, n * NSW + 1)
                    sp.dma_start(idx[:, 0, :], src_idx[:, bass.ds(n * ET, ET)]).then_inc(slow_idx, 16)
                sp.wait_ge(slow_landed, NG * ET * 16)

            for s in range(PER):
                sp.dma_start(idx[:, s, :], src_idx[:, s * ET:(s + 1) * ET]).then_inc(idx_in[s], 16)
            sp.dma_start(xin[:, :], x[0:P, :]).then_inc(xt_in, 16)
            sp.wait_ge(g_stored, 7 * 16)
            sp.wait_ge(acc_zero, 2)
            sp.dma_start(wd_sb, wd.rearrange("e (c p) n -> p (e c) n", p=P)).then_inc(wd_in, 16)

            def ahead(i, last):
                for s in range(PER):
                    if not last:
                        sp.wait_ge(landed[s], (i + 1) * (ET * 16))
                        sp.dma_start(idx[:, s, :], src_idx[:, bass.ds((i + 1) * (PER * ET) + s * ET, ET)])\
                          .then_inc(idx_in[s], 16)
                    if s == 2:
                        store(i)

            def store(i):
                if isinstance(i, int) and i < LATE:
                    return
                t = i - LATE
                sp.wait_ge(x2_ready, t + 1)
                sp.dma_start(xin[:, :], x[bass.ds((t + 1) * P, P), :]).then_inc(xt_in, 16)
                sp.wait_ge(xn_ready, t + 1)
                sp.dma_start(tok_dram[bass.ds(t * P, P), :], xcat[:, :]).then_inc(tok_stored, 16)

            for i in range(SEG1):
                ahead(i, False)
            with sp.Fori(SEG1, NI - 1) as i:
                ahead(i, False)
            ahead(NI - 1, True)
            t = NT - 2
            sp.wait_ge(x2_ready, t + 1)
            sp.dma_start(xin[0:LASTN, :], x[(NT - 1) * P:N, :]).then_inc(xt_in, 16)
            for t in (NT - 2, NT - 1):
                sp.wait_ge(xn_ready, t + 1)
                sp.dma_start(tok_dram[t * P:(t + 1) * P, :], xcat[:, :]).then_inc(tok_stored, 16)

            sp.dma_start(bd_sb, bd.rearrange("e n -> (e n)").partition_broadcast(P)).then_inc(bd_in, 16)

            sp.wait_ge(slots_ready, 1)

            def rings(u, s, first):
                j = u * UN + s
                if not first:
                    sp.wait_ge(tok_in[s], u * 16)
                sp.dma_start(gring[:, s:s + 1], gidx[:, bass.ds(j, 1)]).then_inc(gi_in[s], 16)
                if not first:
                    sp.wait_ge(stored[s], u * 16)
                sp.dma_start(sring[:, s:s + 1], sidx[:, bass.ds(j, 1)]).then_inc(si_in[s], 16)

            for s in range(UN):
                rings(0, s, True)
            with sp.Fori(1, NJ // UN) as u:
                for s in range(UN):
                    rings(u, s, False)

        @block.gpsimd
        def _(pool):
            own = Chain(pool, pool_own)
            pool.memset(nat_i[0][:, NB - 1, :], -1).then_inc(pads_set, 1)
            pool.memset(nat_i[1][:, NB - 1, :], -1).then_inc(pads_set, 1)
            pool.memset(xs[:, NT - 1, :], 0.0).then_inc(pads_set, 1)
            pool.memset(ones[:, :], 1.0).then_inc(consts, 1)
            own(pool.memset(ident[:, :], 0.0))
            pool.affine_select(out=ident[:, :], in_=ident[:, :], compare_op=ALU.not_equal, fill=1.0, base=0,
                               pattern=[[-1, P]], channel_multiplier=1).then_inc(consts, 1)
            pool.iota(iota_i[:, :], pattern=[[1, SW]], base=0, channel_multiplier=0).then_inc(consts, 1)
            own(pool.memset(row0[:, :], 0.0))
            pool.memset(row0[0:1, :], 1.0).then_inc(consts, 1)
            pool.iota(lim_i[:, :], pattern=[[P, NI], [0, PER]], base=-P * (LATE - 1), channel_multiplier=0)\
                .then_inc(consts, 1)
            pool.iota(tid_i[:, :], pattern=[[P, NT]], base=1, channel_multiplier=1).then_inc(consts, 1)
            pool.iota(rank8_i[:, :], pattern=[[-1, EX]], base=EX, channel_multiplier=0).then_inc(consts, 1)
            own(pool.memset(upper[:, :], 1.0))
            pool.affine_select(out=upper[:, :], in_=upper[:, :], compare_op=ALU.is_gt, fill=0.0, base=0,
                               pattern=[[1, P]], channel_multiplier=-1).then_inc(consts, 1)
            pool.memset(ones_h[:, :], 1.0).then_inc(consts, 1)
            pool.memset(one8[:, :], 1.0).then_inc(consts, 1)
            pool.memset(eps_t[:, :], EPS).then_inc(consts, 1)
            pool.memset(zeros_h[:, :], 0.0).then_inc(consts, 1)
            wait_count(pool, sums_done, 1)
            pool.tensor_scalar(nmean[:, :], ssum[:, :], -1.0 / D, None, ALU.mult).then_inc(mean_ready, 1)
            wait_count(pool, ssq_done, 1)
            wait_count(pool, flag_ready, 1)
            pool.memset(accT[:, :, :], 0.0).then_inc(acc_zero, 1)

            wait_count(pool, g_stored, 7 * 16)

            def gather(s, j, done):
                pool.indirect_dma_start(rows[:, s, j * D:(j + 1) * D], None, g_dram[:, :],
                                        bass.IndirectOffsetOnAxis(idx[:, s, j:j + 1], 0)).then_inc(done, 16)

            general = pool.value_load(flag_i[0:1, 0:1], min_val=0, max_val=1)
            with pool.If(general != 0):
                with pool.Fori(0, NG) as n:
                    wait_count(pool, slow_idx, (n + 1) * 16)
                    wait_count(pool, slow_sum, n * NSW + 1)
                    for j in range(ET):
                        gather(0, j, slow_landed)
                wait_count(pool, slow_sum, NG * NSW + 1)

            def body(i):
                for s in range(PER):
                    wait_count(pool, idx_in[s], (i + 1) * 16)
                    if not (isinstance(i, int) and i == 0):
                        wait_count(pool, seg_done, i * PER + s - (PER - 1))
                    for j in range(ET):
                        gather(s, j, landed[s])

            body(0)
            with pool.Fori(1, NI) as i:
                body(i)

            wait_count(pool, tok_stored, NT * 16)

            def fetch(u, s):
                wait_count(pool, gi_in[s], (u + 1) * 16)
                pool.indirect_dma_start(trow[s], None, tok_dram[:, :],
                                        bass.IndirectOffsetOnAxis(gring[:, s:s + 1], 0)).then_inc(tok_in[s], 16)

            def scatter(u, s):
                wait_count(pool, si_in[s], (u + 1) * 16)
                wait_count(pool, o_ready, u * UN + s + 1)
                pool.indirect_dma_start(out[:, :], bass.IndirectOffsetOnAxis(sring[:, s:s + 1], 0), obuf[s], None,
                                        bounds_check=N - 1, oob_is_err=False).then_inc(stored[s], 16)

            for s in range(UN):
                fetch(0, s)
            with pool.Fori(1, NJ // UN) as u:
                for s in range(UN):
                    scatter(u - 1, s)
                    fetch(u, s)
            for s in range(UN):
                scatter(NJ // UN - 1, s)
            for s in range(UN):
                wait_count(pool, stored[s], 16 * (NJ // UN))

        @block.scalar
        def _(act):
            for dst_t, src_t in (
                (gw_sb[:, 0:KD, :], gnn_w1.rearrange("(k p) n -> p k n", p=P)),
                (gw_sb[:, KD:2 * KD, :], gnn_w2.rearrange("(k p) n -> p k n", p=P)),
                (gb_sb[:, :], gnn_b.partition_broadcast(P)),
                (w1_sb[:, :, :], w1.rearrange("(k p) n -> p k n", p=P)),
                (b1_sb[:, :], b1.rearrange("(c p) -> p c", p=P)),
                (wg_sb[:, :, :], wg.rearrange("(c p) e -> p c e", p=P)),
                (bg_sb[:, :], bg.partition_broadcast(P)),
            ):
                act.dma_start(dst_t, src_t).then_inc(weights_in, 16)
            act.wait_ge(x_in, 7 * 16)
            def reduce_row(q, t, **how):
                if q >= NJUNK:
                    act.wait_ge(act_own, q - NJUNK + 1)
                act.activation(junk[q % NJUNK], xs[:, t, :], **how).then_inc(act_own, 1)

            for t in range(NT):
                reduce_row(t, t, func=ACT.Copy, accum_out=ssum[:, t:t + 1])
            act.wait_ge(act_own, NT)
            act.sem_inc(sums_done, 1)
            act.wait_ge(mean_ready, 1)
            for t in range(NT):
                reduce_row(NT + t, t, func=ACT.Square, bias=nmean[:, t:t + 1], accum_out=ssq[:, t:t + 1])
            act.wait_ge(act_own, 2 * NT)
            act.sem_inc(ssq_done, 1)
            act.wait_ge(deg_read, 1)
            act.activation(deg[:, :], deg[:, :], ACT.Sqrt)
            act.activation(ssq[:, :], ssq[:, :], ACT.Sqrt).then_inc(roots, 1)
            act.wait_ge(scales, 1)
            for t in range(21):
                ins = act.activation(xs[:, t, :], xs[:, t, :], ACT.Identity, bias=gsb[:, t:t + 1],
                                     scale=gsc[:, t:t + 1])
                if t % 7 == 6:
                    ins.then_inc(g_act, 1)

            def tile_head(t, first):
                act.wait_ge(xt_in, (t + 1) * 16)
                if not first:
                    act.wait_ge(fu_t, t)
                act.activation(fu[:, 0, :], xin[:, :], ACT.Identity, bias=nb[:, bass.ds(t, 1)],
                               scale=rstd[:, bass.ds(t, 1)])
                act.activation(fu[:, 1, :], xin[:, :], ACT.Identity, bias=usb[:, bass.ds(t, 1)],
                               scale=usc[:, bass.ds(t, 1)]).then_inc(fu_ready, 1)

            def tile_rest(t, first):
                act.wait_ge(e_ready, t + 1)
                act.activation(sqj[:, :], emb2[:, :], ACT.Square, accum_out=ss[:, :]).then_inc(ss_ready, 1)
                act.wait_ge(ss_ready, t + 1)
                act.activation(nrm[:, :], ss[:, :], ACT.Sqrt).then_inc(nrm_ready, 1)
                act.wait_ge(var_ready, t + 1)
                act.activation(sd[:, :], mv[:, 1:2], ACT.Sqrt, bias=eps_t[:, :]).then_inc(sd_ready, 1)
                act.wait_ge(xn_t, t + 1)
                act.activation(xT[:, 0, :, :], bkL[:, 0:D].rearrange("p (k n) -> p k n", k=KD), ACT.Copy)\
                    .then_inc(xt_ready, 1)
                if not first:
                    act.wait_ge(lg_done, t)
                for c in range(KH):
                    b = c // 4
                    if c % 4 == 0:
                        act.wait_ge(h_done[b], t + 1)
                    ins = act.activation(hT[:, 0, c, :], bkH[b][:, (c % 4) * P:(c % 4 + 1) * P], ACT.Gelu,
                                         bias=b1_sb[:, c:c + 1])
                ins.then_inc(gelu_done, 1)

            act.wait_ge(weights_in, 7 * 16)
            act.wait_ge(consts, 12)

            def body(i):
                if not (isinstance(i, int) and i < LATE):
                    first = isinstance(i, int)
                    tile_head(i - LATE, first)
                    tile_rest(i - LATE, first)

            edge_loop(act, body)
            for t in (NT - 2, NT - 1):
                tile_head(t, False)
                tile_rest(t, False)

            act.wait_ge(exp_in, 1)
            act.activation(ra[:, :, :], ra[:, :, :], ACT.Exp).then_inc(exp_done, 1)

            def gelu_tile(u, s, first):
                j = u * UN + s
                for b in (0, 1):
                    hb = (bkH if s % 2 == 0 else bkA)[b]
                    act.wait_ge(h2_done, 2 * j + b + 1)
                    if not first and b == 0:
                        act.wait_ge(y_done, j - 1)
                    for c in range(4):
                        ins = act.activation(hT[:, s % 2, 4 * b + c, :], hb[:, c * P:(c + 1) * P], ACT.Gelu,
                                             bias=b1_sb[:, 4 * b + c:4 * b + c + 1])
                    ins.then_inc(gelu2, 1)

            for s in range(UN):
                gelu_tile(0, s, s < 2)
            with act.Fori(1, NJ // UN) as u:
                for s in range(UN):
                    gelu_tile(u, s, False)

        @block.vector
        def _(dve):
            own = Chain(dve, dve_own)
            dve.wait_ge(consts, 12)
            dve.tensor_copy(iota_f[:, :], iota_i[:, 0:P])
            dve.tensor_copy(limf[:, :], lim_i[:, :])
            dve.tensor_copy(tid[:, :], tid_i[:, :])
            dve.tensor_copy(rank8[:, :], rank8_i[:, :])
            own(dve.tensor_copy(iota_h[:, :], iota_i[:, 0:P]))
            dve.wait_ge(edges_in, 6 * 16)
            for k in (0, 1):
                dve.tensor_copy(nat_f[k], nat_i[k]).then_inc(nat_ready, 1)

            H = 4 * BR

            def split(banks, k, idx_out, f_out, lo_out, hi_out):
                dve.wait_ge(tables_t, k + 1)
                dve.tensor_copy(raw_i[:, 0:H], banks[0][:, 0:H])
                own(dve.tensor_copy(raw_i[:, H:NET], banks[1][:, 0:NET - H]))
                if idx_out is not None:
                    dve.tensor_scalar(idx_out, raw_i, 0, None, ALU.max)
                if f_out is not None:
                    dve.tensor_copy(f_out, raw_i)
                dve.tensor_scalar(part_i, raw_i, P - 1, None, ALU.bitwise_and)
                own(dve.tensor_scalar(part2_i, raw_i, 7, None, ALU.arith_shift_right))
                dve.tensor_copy(lo_out, part_i)
                own(dve.tensor_copy(hi_out, part2_i))

            split((bkT, bkE), 0, src_idx[:, :], None, slo, shi)

            def one_hots(half, j, lo, hi):
                dve.tensor_scalar(hoh[:, half, j, 0:P], iota_h[:, :], lo, None, ALU.is_equal)
                return dve.tensor_scalar(hoh[:, half, j, P:P + 64], iota_h[:, 0:64], hi, None, ALU.is_equal)

            with dve.Fori(0, NET // 16) as i:
                for half in (0, 1):
                    dve.wait_ge(hist_used, i * 2 + half + 1)
                    for j in range(8):
                        at = i * 16 + half * 8 + j
                        ins = one_hots(half, j, slo[:, bass.ds(at, 1)], shi[:, bass.ds(at, 1)])
                    ins.then_inc(hist_oh, 1)

            dve.wait_ge(hist_done, 1)
            own(dve.tensor_scalar(deg[:, :], bkC[:, 0:NT], 1.0, None, ALU.max))
            dve.wait_ge(ssq_done, 1)
            own(dve.tensor_scalar(ssq[:, :], ssq[:, :], 1.0 / D, EPS, ALU.mult, ALU.add))
            dve.sem_inc(deg_read, 1)
            dve.wait_ge(roots, 1)
            dve.reciprocal(rs[:, :], deg[:, :])
            own(dve.reciprocal(rstd[:, :], ssq[:, :]))
            own(dve.tensor_tensor(nb[:, :], nmean[:, :], rstd[:, :], ALU.mult))
            dve.tensor_tensor(gsc[:, :], rstd[:, :], rs[:, :], ALU.mult)
            dve.tensor_tensor(usc[:, :], rstd[:, :], deg[:, :], ALU.mult)
            dve.tensor_tensor(usb[:, :], nb[:, :], deg[:, :], ALU.mult)
            own(dve.tensor_tensor(gsb[:, :], nb[:, :], rs[:, :], ALU.mult))
            dve.sem_inc(scales, 1)
            for t in range(21, NT):
                ins = dve.tensor_scalar(xs[:, t, :], xs[:, t, :], gsc[:, t:t + 1], gsb[:, t:t + 1], ALU.mult, ALU.add)
                if t % 7 == 6:
                    ins.then_inc(g_dve, 1)

            dve.memset(dstf[:, NET:NET + ET], -1.0)
            dve.memset(dlo[:, NET:NET + ET], -1.0)
            dve.memset(dhi[:, NET:NET + ET], -1.0)
            dve.memset(rel[:, NET:NET + ET], -FAR)
            split((bkH[0], bkH[1]), 1, None, dstf[:, 0:NET], dlo[:, 0:NET], dhi[:, 0:NET])
            dve.sem_inc(dst_ready, 1)
            dve.wait_ge(base_bc, 1)
            own(dve.tensor_copy(basef[:, :], bkL[:, 0:NG]))
            dve.tensor_copy(base_i[:, :], basef[0:1, :])
            own(dve.tensor_tensor(rel[:, 0:NET].rearrange("p (n j) -> p n j", j=ET),
                                  dstf[:, 0:NET].rearrange("p (n j) -> p n j", j=ET),
                                  basef[:, :].unsqueeze(2).to_broadcast([P, NG, ET]), ALU.subtract))
            own(dve.tensor_scalar(viol, rel[:, 0:NET], 0.0, None, ALU.is_lt))
            own(dve.scalar_tensor_tensor(viol2, rel[:, 0:NET], float(WIN), viol, ALU.is_ge, ALU.add))
            own(dve.scalar_tensor_tensor(viol, dstf[:, 0:NET], 0.0, viol2, ALU.is_ge, ALU.mult))
            dve.tensor_tensor(viol2[:, 0:NG], basef[:, :], limf[:, :], ALU.is_lt)
            own(dve.tensor_reduce(small[:, 0:1], viol, AX.X, ALU.add))
            own(dve.tensor_reduce(small[:, 1:2], viol2[:, 0:NG], AX.X, ALU.add))
            dve.tensor_tensor(small[:, 2:3], small[:, 0:1], small[:, 1:2], ALU.add).then_inc(viol_ready, 1)
            dve.wait_ge(viol_sum, 1)
            own(dve.tensor_scalar(small[:, 3:4], bkL[:, 256:257], 1.0, None, ALU.min))
            own(dve.tensor_scalar(small[:, 4:5], small[:, 3:4], -FAR, None, ALU.mult))
            dve.tensor_copy(flag_i[:, :], small[0:1, 3:4])
            own(dve.tensor_scalar(rel[:, 0:NET], rel[:, 0:NET], small[:, 4:5], None, ALU.add))
            dve.sem_inc(flag_ready, 1)
            dve.wait_ge(acc_zero, 1)

            general = dve.value_load(flag_i[0:1, 0:1], min_val=0, max_val=1)
            dve.wait_ge(g_stored, 7 * 16)
            with dve.If(general != 0):
                dve.tensor_copy(slow_iota, iota_i[:, :]).then_inc(slow_added, 1)
                slow = Chain(dve, slow_own)
                SLOW_OWN = 4
                with dve.Fori(0, NG) as n:
                    dve.wait_ge(slow_hist_used, n + 1)
                    for j in range(ET):
                        ins = one_hots(0, j, dlo[:, bass.ds(n * ET + j, 1)], dhi[:, bass.ds(n * ET + j, 1)])
                    ins.then_inc(slow_hist, 1)
                    with dve.Fori(0, NSW) as w:
                        slow.at((n * NSW + w) * SLOW_OWN)
                        slow(dve.tensor_copy(small[:, 1:2], iota_i[:, bass.ds(w, 1)]))
                        slow(dve.tensor_scalar(small[:, 1:2], small[:, 1:2], -float(SW), None, ALU.mult))
                        slow(dve.tensor_scalar(small[:, 4:8], dstf[:, bass.ds(n * ET, ET)], small[:, 1:2], None,
                                               ALU.add))
                        for j in range(ET):
                            ins = dve.tensor_scalar(slow_oh[:, j, :], slow_iota, small[:, 4 + j:5 + j], None,
                                                    ALU.is_equal)
                        ins.then_inc(slow_oh_ready, 1)
                        dve.wait_ge(slow_sum, n * NSW + w + 2)
                        for h in range(KD):
                            a = accT[:, h, bass.ds(w * SW, SW)]
                            ins = dve.tensor_tensor(a, bkA[h][:, :], a, ALU.add)
                        slow(ins)
                        dve.sem_inc(slow_added, 1)
                        assert slow.k == SLOW_OWN
                dve.wait_ge(slow_hist_used, NG + 1)
            dve.sem_inc(acc_zero, 1)

            def windows(n, slot2):
                for j in range(ET):
                    ins = dve.tensor_scalar(woh[:, slot2, j, :], iota_f[:, 0:WIN], rel[:, bass.ds(n * ET + j, 1)],
                                            None, ALU.is_equal)
                ins.then_inc(oh_ready, 1)
                for j in range(ET):
                    ins = one_hots(slot2, j, dlo[:, bass.ds(n * ET + j, 1)], dhi[:, bass.ds(n * ET + j, 1)])
                ins.then_inc(ehist_oh, 1)

            def accumulate(n, s):
                base = dve.value_load(base_i[0:1, bass.ds(n, 1)], min_val=0, max_val=N - 1)
                a = accT[:, :, bass.ds(base, WIN)]
                dve.wait_ge(seg_done, n + 1)
                loop_own(dve.tensor_tensor(a, segp[s % 2], a, ALU.add))
                dve.sem_inc(seg_added, 1)

            loop_own = Chain(dve, edge_own)

            def piece0(t, first):
                dve.wait_ge(ehist_done, (t + LATE) * PER)
                loop_own(dve.tensor_scalar(reff[:, :], bkC[:, bass.ds(t, 1)], 0.5, rs[:, bass.ds(t, 1)],
                                           ALU.is_gt, ALU.mult))
                dve.sem_inc(cnt_read, 1)
                if not first:
                    dve.wait_ge(lg_done, t)
                    dve.tensor_tensor(logits[:, bass.ds(t - 1, 1), :], bkL[:, D:D + EX].unsqueeze(1), bg_sb[:, :].unsqueeze(1),
                                      ALU.add).then_inc(lg_read, 1)
                    dve.wait_ge(e_done, t)
                dve.wait_ge(fu_t, t + 1)
                g = accT[:, :, bass.ds(t * P, P)]
                fT = bkT[:, 0:D].rearrange("p (k n) -> p k n", k=KD)
                uT = bkT[:, D:2 * D].rearrange("p (k n) -> p k n", k=KD)
                dve.tensor_tensor(lT[:, 0:KD, :], uT, g, ALU.add)
                dve.tensor_tensor(lT[:, KD:2 * KD, :], fT, g, ALU.mult).then_inc(l_ready, 1)

            def piece1(t, first):
                dve.wait_ge(e_done, t + 1)
                loop_own(dve.scalar_tensor_tensor(emb[:, :], bkE[:, 0:D], reff[:, :], gb_sb[:, :], ALU.mult, ALU.add))
                dve.scalar_tensor_tensor(emb2[:, :], emb[:, :], 0.01, emb[:, :], ALU.mult, ALU.max)\
                    .then_inc(e_ready, 1)

            def piece2(t, first):
                dve.wait_ge(nrm_ready, t + 1)
                loop_own(dve.tensor_scalar(rn[:, :], nrm[:, :], 1e-12, None, ALU.max))
                loop_own(dve.reciprocal(rn[:, :], rn[:, :]))
                if not first:
                    dve.wait_ge(tok_stored, t * 16)
                x2 = xcat[:, 0:D]
                dve.scalar_tensor_tensor(x2, emb2[:, :], rn[:, :], xin[:, :], ALU.mult, ALU.add).then_inc(x2_ready, 1)
                dve.wait_ge(x2_ready, t + 1)
                loop_own(dve.bn_stats(st6[:, :], x2))
                dve.sem_inc(ticks, 1)
                dve.bn_aggr(mv[:, :], st6[:, :]).then_inc(var_ready, 1)
                dve.wait_ge(sd_ready, t + 1)
                loop_own(dve.reciprocal(rstd2[:, :], sd[:, :]))
                dve.tensor_scalar(xcat[:, D:2 * D], x2, mv[:, 0:1], rstd2[:, :], ALU.subtract, ALU.mult)\
                    .then_inc(xn_ready, 1)

            PIECES = (piece0, piece1, piece2)
            OWN_EDGE, OWN_TILE = PER, 6

            def body(i):
                tile = not (isinstance(i, int) and i < LATE)
                loop_own.at(i * OWN_EDGE + (i - LATE) * OWN_TILE if tile else i * OWN_EDGE)
                for s in range(PER):
                    n = i * PER + s
                    if not (isinstance(i, int) and n == 0):
                        dve.wait_ge(seg_done, n)
                        dve.wait_ge(ehist_done, n)
                    windows(n + 1, (s + 1) % 2)
                    if tile and s < 3:
                        PIECES[s](i - LATE, isinstance(i, int))
                    accumulate(n, s)
                assert loop_own.k == OWN_EDGE + (OWN_TILE if tile else 0)

            windows(0, 0)
            edge_loop(dve, body)
            loop_own.at(NI * OWN_EDGE + (NI - LATE) * OWN_TILE)
            for t in (NT - 2, NT - 1):
                dve.wait_ge(ehist_done, NG)
                loop_own(dve.tensor_scalar(reff[:, :], bkC[:, t:t + 1], 0.5, rs[:, t:t + 1], ALU.is_gt, ALU.mult))
                dve.wait_ge(lg_done, t)
                dve.tensor_tensor(logits[:, t - 1, :], bkL[:, D:D + EX], bg_sb[:, :], ALU.add).then_inc(lg_read, 1)
                dve.wait_ge(fu_t, t + 1)
                dve.wait_ge(e_done, t)
                g = accT[:, :, t * P:(t + 1) * P]
                dve.tensor_tensor(lT[:, 0:KD, :], bkT[:, D:2 * D].rearrange("p (k n) -> p k n", k=KD), g, ALU.add)
                dve.tensor_tensor(lT[:, KD:2 * KD, :], bkT[:, 0:D].rearrange("p (k n) -> p k n", k=KD), g, ALU.mult)\
                    .then_inc(l_ready, 1)
                piece1(t, False)
                piece2(t, False)
            dve.wait_ge(lg_done, NT)
            loop_own(dve.tensor_tensor(logits[:, NT - 1, :], bkL[:, D:D + EX], bg_sb[:, :], ALU.add))

            r = loop_own
            by_e = lambda a: a[:, :].unsqueeze(2).to_broadcast([P, NT, EX])
            by_t = lambda a: a[:, :].unsqueeze(1).to_broadcast([P, NT, EX])
            dve.memset(keep[:, :, 1:NT], 1.0)
            dve.memset(keep[:, :, 0:1], 0.0)
            r(dve.tensor_reduce(mx[:, :], logits[:, :, :], AX.X, ALU.max))
            dve.tensor_tensor(ra[:, :, :], logits[:, :, :], by_e(mx), ALU.subtract).then_inc(exp_in, 1)
            dve.wait_ge(exp_done, 1)
            r(dve.tensor_reduce(mx[:, :], ra[:, :, :], AX.X, ALU.add))
            dve.reciprocal(prob[:, :], mx[:, :])
            r(dve.tensor_scalar(rb[:, :, :], ra[:, :, :], 1.0, None, ALU.is_ge))
            r(dve.tensor_tensor(rb[:, :, :], rb[:, :, :], by_t(rank8), ALU.mult))
            r(dve.tensor_reduce(mx[:, :], rb[:, :, :], AX.X, ALU.max))
            r(dve.tensor_tensor(oneh[:, :, :], by_e(mx), by_t(rank8), ALU.is_equal))
            r(dve.tensor_scalar(valid[:, :], tid[:, :], float(N), None, ALU.is_le))
            r(dve.tensor_tensor(oneh[:, :, :], oneh[:, :, :], by_e(valid), ALU.mult))
            dve.tensor_copy(oneh_h[:, :, :], oneh[:, :, :]).then_inc(oneh_ready, 1)
            dve.wait_ge(ranks, 1)
            r(dve.tensor_copy(tot[:, :, :], bkE[:, 0:LE].rearrange("p (t e) -> p e t", e=EX)))
            r(dve.tensor_tensor_scan(cum[:, :, :].rearrange("p e t -> p (e t)"),
                                     keep[:, :, :].rearrange("p e t -> p (e t)"),
                                     tot[:, :, :].rearrange("p e t -> p (e t)"), 0.0, ALU.mult, ALU.add))
            r(dve.tensor_scalar(te[:, :], cum[:, :, NT - 1], float(P - 1), None, ALU.add))
            r(dve.tensor_copy(te_i[:, :], te[:, :]))
            r(dve.tensor_scalar(te_i[:, :], te_i[:, :], 7, None, ALU.arith_shift_right))
            r(dve.tensor_copy(te[:, :], te_i[:, :]))
            r(dve.tensor_tensor_scan(tinc[:, :], one8[:, :], te[:, :], 0.0, ALU.mult, ALU.add))
            r(dve.tensor_tensor(tstart[:, :], tinc[:, :], te[:, :], ALU.subtract))
            r(dve.tensor_scalar(tstart[:, :], tstart[:, :], float(P), None, ALU.mult))
            r(dve.tensor_tensor(cum[:, :, :], cum[:, :, :], tot[:, :, :], ALU.subtract))
            r(dve.tensor_tensor(cum[:, :, :], cum[:, :, :], tstart[:, :].unsqueeze(2).to_broadcast([P, EX, NT]), ALU.add))
            r(dve.tensor_tensor(rb[:, :, :], bkT[:, 0:LE].rearrange("p (t e) -> p t e", e=EX),
                                cum[:, :, :].rearrange("p e t -> p t e"), ALU.add))
            r(dve.tensor_tensor(rb[:, :, :], rb[:, :, :], oneh[:, :, :], ALU.mult))
            r(dve.tensor_reduce(pos[:, :], rb[:, :, :], AX.X, ALU.add))
            r(dve.tensor_scalar(valid[:, :], valid[:, :], -1.0, FAR, ALU.add, ALU.mult))
            r(dve.tensor_tensor(pos[:, :], pos[:, :], valid[:, :], ALU.add))
            r(dve.tensor_copy(pos_i[:, :], pos[:, :]))
            dve.tensor_scalar(plo_i[:, :], pos_i[:, :], P - 1, None, ALU.bitwise_and)
            r(dve.tensor_scalar(pos_i[:, :], pos_i[:, :], 7, None, ALU.arith_shift_right))
            dve.tensor_copy(plo[:, :], plo_i[:, :])
            r(dve.tensor_copy(phi[:, :], pos_i[:, :]))
            for t in range(NT):
                if t >= 2:
                    dve.wait_ge(pm_used, t - 1)
                dve.tensor_scalar(ploh[:, t % 2, :], iota_f[:, :], plo[:, t:t + 1], None, ALU.is_equal)
                dve.tensor_scalar(phoh[:, t % 2, 0, :], iota_f[:, 0:NJ], phi[:, t:t + 1], tid[:, t:t + 1],
                                  ALU.is_equal, ALU.mult)
                dve.tensor_scalar(phoh[:, t % 2, 1, :], iota_f[:, 0:NJ], phi[:, t:t + 1], prob[:, t:t + 1],
                                  ALU.is_equal, ALU.mult).then_inc(pm_oh, 1)
            iota_j = iota_f[0:1, 0:NJ].unsqueeze(2).to_broadcast([1, NJ, EX])
            r(dve.tensor_tensor(jx[:, :, :], iota_j, tinc[0:1, :].unsqueeze(1).to_broadcast([1, NJ, EX]), ALU.is_ge))
            r(dve.tensor_reduce(jexp[:, :], jx[:, :, :], AX.X, ALU.add))
            r(dve.tensor_scalar(jexp[:, :], jexp[:, :], float(EX - 1), None, ALU.min))
            r(dve.tensor_copy(jexp_i[:, :], jexp[:, :]))
            dve.wait_ge(pm_used, NT)
            r(dve.tensor_copy(slot[:, :, :], bkC[:, 0:2 * NJ].rearrange("p (a j) -> p a j", a=2)))
            r(dve.tensor_scalar(gidx[:, :], slot[:, 0, :], -1.0, 0.0, ALU.add, ALU.max))
            r(dve.tensor_scalar(sidf[:, :], slot[:, 0, :], 0.5, float(2 * N), ALU.is_lt, ALU.mult))
            r(dve.scalar_tensor_tensor(sidf[:, :], slot[:, 0, :], -1.0, sidf[:, :], ALU.add, ALU.add))
            r(dve.tensor_copy(sidx[:, :], sidf[:, :]))
            dve.sem_inc(slots_ready, 1)

            dve.wait_ge(bd_in, 16)

            def t_copy(j, s):
                dve.wait_ge(t2_done, j + 1)
                dve.tensor_copy(xT[:, s % 2, :, :], bkT2[s % 2][:, 0:D].rearrange("p (k n) -> p k n", k=KD))\
                    .then_inc(t2_read, 1)

            def finish(u, s):
                j = u * UN + s
                e = dve.value_load(jexp_i[0:1, bass.ds(j, 1)], min_val=0, max_val=EX - 1)
                dve.wait_ge(y_done, j + 1)
                if not (isinstance(j, int) and j == 0):
                    dve.wait_ge(o_ready, j)
                dve.tensor_tensor(yb, bkY[s % 2][:, 0:D], bd_sb[:, bass.ds(e * D, D)], ALU.add).then_inc(y_read, 1)
                dve.wait_ge(y_read, j + 1)
                if not (isinstance(u, int) and u == 0):
                    dve.wait_ge(stored[s], u * 16)
                dve.scalar_tensor_tensor(obuf[s], yb, slot[:, 1, bass.ds(j, 1)], trow[s][:, 0:D], ALU.mult, ALU.add)\
                    .then_inc(o_ready, 1)

            def steps(u, first, last):
                for s in range(UN):
                    if not (last and s == UN - 1):
                        t_copy(u * UN + s + 1, (s + 1) % UN)
                    if s:
                        finish(u, s - 1)
                    elif not first:
                        finish(u - 1, UN - 1)

            t_copy(0, 0)
            steps(0, True, False)
            steps(1, False, False)
            with dve.Fori(2, NJ // UN - 1) as u:
                steps(u, False, False)
            steps(NJ // UN - 1, False, True)
            finish(NJ // UN - 1, UN - 1)

        @block.tensor
        def _(pe):
            mm, tr = pe.matmul, pe.transpose
            pe.wait_ge(consts, 12)
            for k, banks in enumerate(((bkT, bkE), bkH)):
                pe.wait_ge(nat_ready, k + 1)
                for b in range(NB):
                    o = banks[b // 4][:, (b % 4) * BR:(b % 4 + 1) * BR]
                    ins = tr(o, nat_f[k][:, b, :], ident[0:BR, 0:BR])
                ins.then_inc(tables_t, 1)

            def count(half, j, stop=False):
                return mm(bkC[:, 0:64], hoh[:, half, j, 0:P], hoh[:, half, j, P:P + 64], start=False, stop=stop,
                          skip_group_check=True)

            def zero_counts():
                return mm(bkC[:, 0:64], zeros_h[:, :], zeros_h[:, 0:64], start=True, stop=True)

            zero_counts().then_inc(hist_used, 2)
            with pe.Fori(0, NET // 16) as i:
                for half in (0, 1):
                    pe.wait_ge(hist_oh, i * 2 + half + 1)
                    for j in range(8):
                        ins = count(half, j)
                    ins.then_inc(hist_used, 1)
            pe.wait_ge(hist_used, NET // 8 + 2)
            pe.sem_inc(hist_done, 1)
            pe.wait_ge(deg_read, 1)
            zero_counts()
            pe.wait_ge(dst_ready, 1)
            mm(bkL[:, 0:NG], row0[:, :], dstf[:, 0:NET:ET], start=True, stop=True).then_inc(base_bc, 1)
            pe.wait_ge(viol_ready, 1)
            mm(bkL[:, D:D + 1], ones[:, :], small[:, 2:3], start=True, stop=True).then_inc(viol_sum, 1)

            pe.wait_ge(flag_ready, 1)
            general = pe.value_load(flag_i[0:1, 0:1], min_val=0, max_val=1)
            with pe.If(general != 0):
                pe.sem_inc(slow_hist_used, 1)
                pe.sem_inc(slow_sum, 1)
                with pe.Fori(0, NG) as n:
                    pe.wait_ge(slow_hist, n + 1)
                    for j in range(ET):
                        ins = count(0, j)
                    ins.then_inc(slow_hist_used, 1)
                    wait_count(pe, slow_landed, (n + 1) * (ET * 16))
                    with pe.Fori(0, NSW) as w:
                        pe.wait_ge(slow_oh_ready, n * NSW + w + 1)
                        pe.wait_ge(slow_added, n * NSW + w + 1)
                        for h in range(KD):
                            for j in range(ET):
                                ins = mm(bkA[h][:, :], rows[:, 0, j * D + h * P:j * D + (h + 1) * P],
                                         slow_oh[:, j, :], start=j == 0, stop=j == ET - 1)
                        ins.then_inc(slow_sum, 1)
                pe.wait_ge(slow_added, NG * NSW + 1)

            pe.wait_ge(weights_in, 7 * 16)

            def segment(i, s):
                n = i * PER + s
                pe.wait_ge(landed[s], (i + 1) * (ET * 16))
                pe.wait_ge(oh_ready, n + 1)
                if not (isinstance(n, int) and n < 2):
                    pe.wait_ge(seg_added, n - 1)
                for h in range(KD):
                    for j in range(ET):
                        ins = mm(segp[s % 2][:, h, :], rows[:, s, j * D + h * P:j * D + (h + 1) * P],
                                 woh[:, s % 2, j, :], start=j == 0, stop=j == ET - 1)
                ins.then_inc(seg_done, 1)

            def in_degree(i, s):
                n = i * PER + s
                pe.wait_ge(ehist_oh, n + 1)
                for j in range(ET):
                    ins = count(s % 2, j)
                ins.then_inc(ehist_done, 1)

            def gates(t):
                pe.wait_ge(gelu_done, t + 1)
                for c in range(KH):
                    ins = mm(bkL[:, D:D + EX], hT[:, 0, c, :], wg_sb[:, c, :], start=c == 0, stop=c == KH - 1)
                ins.then_inc(lg_done, 1)

            def transpose_fu(t, first):
                pe.wait_ge(fu_ready, t + 1)
                if not first:
                    pe.wait_ge(l_ready, t)
                for a in range(2):
                    for k in range(KD):
                        q = a * KD + k
                        ins = tr(bkT[:, q * P:(q + 1) * P], fu[:, a, k * P:(k + 1) * P], ident[:, :])
                ins.then_inc(fu_t, 1)

            def embed(t, first):
                pe.wait_ge(l_ready, t + 1)
                if not first:
                    pe.wait_ge(e_ready, t)
                for q in range(2 * KD):
                    ins = mm(bkE[:, 0:D], lT[:, q, :], gw_sb[:, q, :], start=q == 0, stop=q == 2 * KD - 1)
                ins.then_inc(e_done, 1)

            def transpose_xn(t, first):
                pe.wait_ge(xn_ready, t + 1)
                if not first:
                    pe.wait_ge(lg_read, t)
                for k in range(KD):
                    ins = tr(bkL[:, k * P:(k + 1) * P], xcat[:, D + k * P:D + (k + 1) * P], ident[:, :])
                ins.then_inc(xn_t, 1)

            def hidden_bank(out_bank, xslot, b):
                for q in range(4):
                    c = 4 * b + q
                    for k in range(KD):
                        ins = mm(out_bank[:, q * P:(q + 1) * P], w1_sb[:, k, c * P:(c + 1) * P], xT[:, xslot, k, :],
                                 start=k == 0, stop=k == KD - 1)
                return ins

            def hidden(t, first):
                pe.wait_ge(xt_ready, t + 1)
                if not first:
                    pe.wait_ge(gelu_done, t)
                for b in (0, 1):
                    hidden_bank(bkH[b], 0, b).then_inc(h_done[b], 1)

            def body(i):
                tile = not (isinstance(i, int) and i < LATE)
                first = isinstance(i, int)
                t = i - LATE
                segment(i, 0)
                if tile:
                    pe.wait_ge(cnt_read, t + 1)
                in_degree(i, 0)
                if tile:
                    if not first:
                        gates(t - 1)
                    transpose_fu(t, first)
                segment(i, 1)
                in_degree(i, 1)
                if tile:
                    embed(t, first)
                segment(i, 2)
                in_degree(i, 2)
                if tile:
                    transpose_xn(t, first)
                segment(i, 3)
                in_degree(i, 3)
                if tile:
                    hidden(t, first)

            edge_loop(pe, body)
            for t in (NT - 2, NT - 1):
                gates(t - 1)
                transpose_fu(t, False)
                embed(t, False)
                transpose_xn(t, False)
                hidden(t, False)
            gates(NT - 1)

            pe.wait_ge(oneh_ready, 1)
            flat = oneh_h[:, :, :].rearrange("p t e -> p (t e)")
            mm(bkT[:, 0:LE], upper[:, :], flat, start=True, stop=True)
            mm(bkE[:, 0:LE], ones_h[:, :], flat, start=True, stop=True).then_inc(ranks, 1)
            for t in range(NT):
                pe.wait_ge(pm_oh, t + 1)
                mm(bkC[:, 0:2 * NJ], ploh[:, t % 2, :], phoh[:, t % 2, :, :].rearrange("p a j -> p (a j)"),
                   start=t == 0, stop=t == NT - 1).then_inc(pm_used, 1)

            pe.wait_ge(slots_ready, 1)
            pe.wait_ge(wd_in, 16)

            def transpose_tok(u, s, first):
                j = u * UN + s
                pe.wait_ge(tok_in[s], (u + 1) * 16)
                if not first:
                    pe.wait_ge(t2_read, j - 1)
                for k in range(KD):
                    ins = tr(bkT2[s % 2][:, k * P:(k + 1) * P], trow[s][:, D + k * P:D + (k + 1) * P], ident[:, :])
                ins.then_inc(t2_done, 1)

            def hidden2(u, s, first):
                j = u * UN + s
                pe.wait_ge(t2_read, j + 1)
                if not first:
                    pe.wait_ge(gelu2, 2 * (j - 1))
                for b in (0, 1):
                    hidden_bank((bkH, bkA)[s % 2][b], s % 2, b).then_inc(h2_done, 1)

            def expert(u, s, first):
                j = u * UN + s
                e = pe.value_load(jexp_i[0:1, bass.ds(j, 1)], min_val=0, max_val=EX - 1)
                pe.wait_ge(gelu2, 2 * (j + 1))
                if not first:
                    pe.wait_ge(y_read, j - 1)
                for c in range(KH):
                    ins = mm(bkY[s % 2][:, 0:D], hT[:, s % 2, c, :], big[:, bass.ds(e * (KH * D) + c * D, D)],
                             start=c == 0, stop=c == KH - 1)
                ins.then_inc(y_done, 1)

            def steps(u, first, last):
                for s in range(UN):
                    if s < UN - 1:
                        transpose_tok(u, s + 1, first and s + 1 < 2)
                    elif not last:
                        transpose_tok(u + 1, 0, False)
                    hidden2(u, s, first and s < 2)
                    if s:
                        expert(u, s - 1, first and s - 1 < 2)
                    elif not first:
                        expert(u - 1, UN - 1, False)

            transpose_tok(0, 0, True)
            steps(0, True, False)
            with pe.Fori(1, NJ // UN - 1) as u:
                steps(u, False, False)
            steps(NJ // UN - 1, False, True)
            expert(NJ // UN - 1, UN - 1, False)


def kernel(x, src, dst, L0_gnn_W1, L0_gnn_W2, L0_gnn_b, L0_ffn_W1, L0_ffn_b1, L0_ffn_Wg, L0_ffn_bg, L0_ffn_Wd,
           L0_ffn_bd):
    import numpy as np
    import concourse.bacc as bacc
    from concourse.bass_utils import run_bass_kernel_spmd

    nc = bacc.Bacc("TRN2", target_bir_lowering=False, num_devices=1)
    inputs = dict(x=x, src=src, dst=dst, gnn_w1=L0_gnn_W1, gnn_w2=L0_gnn_W2, gnn_b=L0_gnn_b, w1=L0_ffn_W1,
                  b1=L0_ffn_b1, wg=L0_ffn_Wg, bg=L0_ffn_bg, wd=L0_ffn_Wd, bd=L0_ffn_bd)
    arrays, args = {}, []
    for name, a in inputs.items():
        arrays[name] = np.ascontiguousarray(a)
        args.append(nc.dram_tensor(name, arrays[name].shape, mybir.dt.from_np(arrays[name].dtype),
                                   kind="ExternalInput").ap())
    args.append(nc.dram_tensor("out", (N, D), F32, kind="ExternalOutput").ap())
    build(nc, *args)
    r = run_bass_kernel_spmd(nc, [arrays], core_ids=[0])
    return r.results[0]["out"]
```

```python
from contextlib import ExitStack

import concourse.bass as bass
from concourse import mybir

F32 = mybir.dt.float32
BF16 = mybir.dt.bfloat16
F16 = mybir.dt.float16
I32 = mybir.dt.int32
ALU = mybir.AluOpType
ACT = mybir.ActivationFunctionType
AX = mybir.AxisListType

P = 128
N = 6250
D = 256
NE = 100000
HID = 1024
EX = 8
KD = D // P
KH = HID // P
NT = (N + P - 1) // P
LASTN = N - (NT - 1) * P
NLO = P
NHI = NT
HC = 4
ET = 4
GE = ET * P
NG = -(-NE // GE)
NET = NG * ET
WIN = 64
PER = 4
NI = NG // PER
LATE = 2
assert NI == NT and NI * PER == NG
SW = 512
NSW = -(-(N + WIN) // SW)
ACCW = NSW * SW
NB = 7
BR = NET // NB
FULLR = NE // P
RESTE = NE - FULLR * P
HR = NE // P
HT = NET // HC
NJ = (N + EX * (P - 1)) // P
UN = 4
assert NJ % UN == 0
EPS = 1e-5
FAR = 100000.0
GS = 2048.0
GC = 7


class Chain:

    def __init__(self, eng, sem):
        self.eng, self.sem, self.base, self.k = eng, sem, 0, 0

    def __call__(self, ins):
        ins.then_inc(self.sem, 1)
        self.k += 1
        self.eng.wait_ge(self.sem, self.base + self.k)

    def at(self, base):
        self.base, self.k = base, 0

    def count(self):
        return self.base + self.k


def build(nc, x, src, dst, gnn_w1, gnn_w2, gnn_b, w1, b1, wg, bg, wd, bd, out):
    ctx = ExitStack()
    with ctx:
        ctx.enter_context(nc.allow_non_contiguous_dma("small transposed bias loads"))

        def sb(name, shape, dt=F32):
            return ctx.enter_context(nc.sbuf_tensor(name, shape, dt))

        def bank(name):
            return ctx.enter_context(nc.psum_tensor(name, [P, 512], F32))

        def sem(name):
            return ctx.enter_context(nc.semaphore(name))

        g_dram = nc.dram_tensor("g_scratch", (NT * P, 2 * D), F16, kind="Internal").ap()
        tok_dram = nc.dram_tensor("tok_scratch", (NT * P, 2 * D), F32, kind="Internal").ap()

        accT = sb("accT", [P, KD, ACCW])
        big = sb("big", [P, EX * KH * D])
        wd_sb = big[:, :].rearrange("p (e c n) -> p (e c) n", e=EX, c=KH)
        xs = big[:, 0:NT * D].rearrange("p (t d) -> p t d", d=D)
        xg = big[:, 0:NT * D].bitcast(F16).rearrange("p (t a d) -> p t a d", t=NT, a=2)
        slow_oh = big[:, 0:ET * SW // 2].bitcast(F16).rearrange("p (j w) -> p j w", j=ET)
        slow_iota = big[:, ET * SW:ET * SW + SW]
        SO = NT * D
        hist_i = big[:, SO:SO + NET].bitcast(I32)
        part_i = big[:, SO + NET:SO + 2 * NET].bitcast(I32)
        hist_lo = big[:, SO + 2 * NET:SO + 2 * NET + NET // 2].bitcast(BF16)
        hist_hi = big[:, SO + 3 * NET:SO + 3 * NET + NET // 2].bitcast(BF16)
        work = sb("work", [P, PER * ET * D + 2 * KH * P])
        rows = work[:, 0:PER * ET * D].rearrange("p (s d) -> p s d", s=PER)
        rows_h = rows.bitcast(F16)
        gtmp = work[:, 0:3 * GC * D].rearrange("p (r t d) -> p r t d", r=3, t=GC)
        hT = work[:, PER * ET * D:].rearrange("p (b c n) -> p b c n", b=2, c=KH)
        w1_sb = sb("w1_sb", [P, KD, HID])
        gw_sb = sb("gw_sb", [P, 2 * KD, D])
        gb_sb = sb("gb_sb", [P, D])
        b1_sb = sb("b1_sb", [P, KH])
        wg_sb = sb("wg_sb", [P, KH, EX])
        bg_sb = sb("bg_sb", [P, EX])
        src_idx = sb("src_idx", [P, NET], I32)
        dstf = sb("dstf", [P, NET + ET])
        cnt_row = sb("cnt_row", [1, ACCW], BF16)
        cnt_t = sb("cnt_t", [1, P])
        rel = sb("rel", [P, NET + ET])
        acc0 = accT[:, 0, :]
        acc1 = accT[:, 1, :]
        nat = lambda k: work[0:BR, k * NB * P:(k + 1) * NB * P]
        nat_i = [nat(k).bitcast(I32).rearrange("p (b c) -> p b c", b=NB) for k in (0, 1)]
        nat_f = [nat(2 + k).rearrange("p (b c) -> p b c", b=NB) for k in (0, 1)]
        bins_lo = accT[:, :, :].rearrange("p h w -> p (h w)")[:, 0:NLO * HT // 2].bitcast(BF16)\
            .rearrange("p (b t) -> p b t", t=HT)
        bins_hi = work[:, 0:NHI * HT // 2].bitcast(BF16).rearrange("p (b t) -> p b t", t=HT)
        viol = acc1[:, 3 * NET:4 * NET]
        viol2 = acc1[:, 4 * NET:5 * NET]

        ident = sb("ident", [P, P])
        ones = sb("ones", [P, P])
        row0 = sb("row0", [P, P])
        upper = sb("upper", [P, P], BF16)
        ones_h = sb("ones_h", [P, P], BF16)
        iota_i = sb("iota_i", [P, SW], I32)
        iota_f = sb("iota_f", [P, P])
        lo_c = sb("lo_c", [P, HT], BF16)
        hi_c = sb("hi_c", [P, HT], BF16)
        lim_i = sb("lim_i", [P, NG], I32)
        limf = sb("limf", [P, NG])
        basef = sb("basef", [P, NG])
        base_i = sb("base_i", [1, NG], I32)
        flag_i = sb("flag_i", [1, 1], I32)
        small = sb("small", [P, 8])
        idx = sb("idx", [P, PER, ET], I32)
        ones_f = sb("ones_f", [P, 1], F16)
        woh = sb("woh", [P, 2, ET, WIN], F16)
        ssum = sb("ssum", [P, NT])
        nmean = sb("nmean", [P, NT])
        ssq = sb("ssq", [P, NT])
        rstd = sb("rstd", [P, NT])
        nb = sb("nb", [P, NT])
        deg = sb("deg", [P, NT])
        reffs = sb("reffs", [P, NT])
        rs = sb("rs", [P, NT])
        gsc = sb("gsc", [P, NT])
        gsb = sb("gsb", [P, NT])
        usc = sb("usc", [P, NT])
        usb = sb("usb", [P, NT])

        xin = sb("xin", [P, D])
        fu = sb("fu", [P, 2, D])
        lT = sb("lT", [P, 2 * KD, P])
        emb = sb("emb", [P, D])
        emb2 = sb("emb2", [P, D])
        sqj = sb("sqj", [P, D])
        xcat = sb("xcat", [P, 2 * D])
        xT = sb("xT", [P, 2, KD, P])
        junk = [xin[:, :], emb[:, :], emb2[:, :], sqj[:, :]]
        NJUNK = len(junk)
        reff = sb("reff", [P, 1])
        ss = sb("ss", [P, 1])
        rn = sb("rn", [P, 1])
        nrm = sb("nrm", [P, 1])
        sd = sb("sd", [P, 1])
        eps_t = sb("eps_t", [P, 1])
        st6 = sb("st6", [P, 6])
        mv = sb("mv", [P, 2])
        rstd2 = sb("rstd2", [P, 1])
        logits = sb("logits", [P, NT, EX])

        bd_sb = acc1[:, 0:EX * D]
        LE = NT * EX
        carved = [0]

        def carve(n, dt=F32):
            at = carved[0]
            carved[0] += n
            assert carved[0] <= ACCW
            return acc0[:, at:at + n] if dt == F32 else acc0[:, at:at + n].bitcast(dt)

        te_view = lambda a: a.rearrange("p (t e) -> p t e", e=EX)
        et_view = lambda a: a.rearrange("p (e t) -> p e t", e=EX)
        ra, rb, oneh = te_view(carve(LE)), te_view(carve(LE)), te_view(carve(LE))
        oneh_h = sb("oneh_h", [P, NT, EX], BF16)
        tot, cum, keep = et_view(carve(LE)), et_view(carve(LE)), et_view(carve(LE))
        mx, prob, pos, plo, phi, valid = (carve(NT) for _ in range(6))
        pos_i, plo_i = carve(NT, I32), carve(NT, I32)
        tid_i = sb("tid_i", [P, NT], I32)
        tid = sb("tid", [P, NT])
        rank8_i = sb("rank8_i", [P, EX], I32)
        rank8 = sb("rank8", [P, EX])
        te, tinc, tstart = carve(EX), carve(EX), carve(EX)
        te_i = carve(EX, I32)
        one8 = sb("one8", [P, EX])
        zeros_h = sb("zeros_h", [P, P], BF16)
        jx = carve(NJ * EX)[0:1, :].rearrange("p (j e) -> p j e", e=EX)
        jexp = carve(NJ)[0:1, :]
        jexp_i = carve(NJ, I32)[0:1, :]
        ploh = carve(2 * P).rearrange("p (b n) -> p b n", b=2)
        phoh = carve(4 * NJ).rearrange("p (b a j) -> p b a j", b=2, a=2)
        slot = carve(2 * NJ).rearrange("p (a j) -> p a j", a=2)
        gidx, sidx = carve(NJ, I32), carve(NJ, I32)
        sidf = carve(NJ)
        gring = sb("gring", [P, UN], I32)
        sring = sb("sring", [P, UN], I32)
        trow = [rows[:, s, 0:2 * D] for s in range(UN)]
        obuf = [rows[:, s, 2 * D:3 * D] for s in range(UN)]
        yb = rows[:, 0, 3 * D:4 * D]

        bkA = [bank("bkA0"), bank("bkA1")]
        bkC = bank("bkC")
        bkT = bank("bkT")
        bkE = bank("bkE")
        bkH = [bank("bkH0"), bank("bkH1")]
        bkL = bank("bkL")
        bkT2 = (bkT, bkL)
        bkY = (bkE, bkC)
        segc = [b[0:1, KD * WIN:(KD + 1) * WIN] for b in bkA]
        segp = [b[:, 0:KD * WIN].rearrange("p (h w) -> p h w", h=KD) for b in bkA]

        pads_set = sem("pads_set"); edges_in = sem("edges_in"); x_in = sem("x_in"); weights_in = sem("weights_in")
        consts = sem("consts"); pool_own = sem("pool_own"); dve_own = sem("dve_own")
        nat_ready = sem("nat_ready"); tables_t = sem("tables_t"); tables_read = sem("tables_read")
        sums_done = sem("sums_done"); mean_ready = sem("mean_ready"); ssq_done = sem("ssq_done"); scales = sem("scales")
        hist_oh = sem("hist_oh"); hist_used = sem("hist_used"); hist_in = sem("hist_in")
        deg_read = sem("deg_read"); slow_own = sem("slow_own"); act_own = sem("act_own"); hist_own = sem("hist_own"); edge_own = sem("edge_own")
        g_f32 = sem("g_f32"); g_hi = sem("g_hi"); g_lo = sem("g_lo"); g_stored = sem("g_stored"); acc_zero = sem("acc_zero")
        dst_ready = sem("dst_ready"); base_bc = sem("base_bc"); viol_ready = sem("viol_ready"); viol_sum = sem("viol_sum")
        flag_ready = sem("flag_ready")
        slow_idx = sem("slow_idx"); slow_landed = sem("slow_landed"); slow_oh_ready = sem("slow_oh_ready")
        slow_sum = sem("slow_sum"); slow_added = sem("slow_added")
        idx_in = [sem(f"idx_in{s}") for s in range(PER)]
        landed = [sem(f"landed{s}") for s in range(PER)]
        oh_ready = sem("oh_ready"); seg_done = sem("seg_done"); seg_added = sem("seg_added")
        xt_in = sem("xt_in"); fu_ready = sem("fu_ready"); fu_t = sem("fu_t"); l_ready = sem("l_ready")
        e_done = sem("e_done"); e_ready = sem("e_ready"); ss_ready = sem("ss_ready"); nrm_ready = sem("nrm_ready"); var_ready = sem("var_ready"); sd_ready = sem("sd_ready"); roots = sem("roots"); x2_ready = sem("x2_ready")
        xn_ready = sem("xn_ready"); xn_t = sem("xn_t"); xt_ready = sem("xt_ready")
        h_done = [sem("h_done0"), sem("h_done1")]; gelu_done = sem("gelu_done")
        lg_done = sem("lg_done"); lg_read = sem("lg_read"); tok_stored = sem("tok_stored"); wd_in = sem("wd_in"); bd_in = sem("bd_in")
        exp_in = sem("exp_in"); exp_done = sem("exp_done"); oneh_ready = sem("oneh_ready"); ranks = sem("ranks")
        pm_oh = sem("pm_oh"); pm_used = sem("pm_used"); slots_ready = sem("slots_ready")
        gi_in = [sem(f"gi_in{s}") for s in range(UN)]
        si_in = [sem(f"si_in{s}") for s in range(UN)]
        tok_in = [sem(f"tok_in{s}") for s in range(UN)]
        stored = [sem(f"stored{s}") for s in range(UN)]
        t2_done = sem("t2_done"); t2_read = sem("t2_read"); h2_done = sem("h2_done"); gelu2 = sem("gelu2")
        y_done = sem("y_done"); y_read = sem("y_read"); o_ready = sem("o_ready"); slots_used = sem("slots_used")

        ticks = sem("ticks")

        def wait_count(eng, s, value):
            eng.wait_ge(s, value)
            if not isinstance(value, int):
                eng.sem_inc(ticks, 1)

        block = ctx.enter_context(nc.Block())

        SEG1 = LATE + 2

        def edge_loop(eng, body):
            for i in range(SEG1):
                body(i)
            with eng.Fori(SEG1, NI) as i:
                body(i)

        @block.sync
        def _(sp):
            sp.wait_ge(pads_set, 4)
            for k, e in enumerate((src, dst)):
                full = (NB - 1) * BR
                sp.dma_start(nat_i[k][:, 0:NB - 1, :],
                             e[0:full * P].rearrange("(b p c) -> p b c", p=BR, c=P)).then_inc(edges_in, 16)
                sp.dma_start(nat_i[k][0:FULLR - full, NB - 1, :],
                             e[full * P:FULLR * P].rearrange("(p c) -> p c", c=P)).then_inc(edges_in, 16)
                sp.dma_start(nat_i[k][FULLR - full:FULLR - full + 1, NB - 1, 0:RESTE],
                             e[FULLR * P:NE].rearrange("(p c) -> p c", p=1)).then_inc(edges_in, 16)
            sp.dma_start(hist_i[:, 0:HR], src[0:P * HR].rearrange("(p c) -> p c", p=P)).then_inc(hist_in, 16)
            sp.dma_start(hist_i[0:NE - P * HR, HR:HR + 1], src[P * HR:NE].rearrange("(p c) -> p c", c=1))\
                .then_inc(hist_in, 16)
            for c in range(6):
                sp.dma_start(xs[:, 8 * c:8 * c + 8, :],
                             x[8 * c * P:8 * (c + 1) * P, :].rearrange("(t p) d -> p t d", p=P)).then_inc(x_in, 16)
            sp.dma_start(xs[0:LASTN, NT - 1, :], x[(NT - 1) * P:N, :]).then_inc(x_in, 16)

            for c in range(7):
                sp.wait_ge(g_lo, c + 1)
                sp.dma_start(g_dram[GC * c * P:GC * (c + 1) * P, :].rearrange("(t p) d -> p t d", p=P),
                             xg[:, GC * c:GC * (c + 1), :, :].rearrange("p t a d -> p t (a d)")).then_inc(g_stored, 16)

            sp.wait_ge(flag_ready, 1)
            general = sp.value_load(flag_i[0:1, 0:1], min_val=0, max_val=1)
            with sp.If(general != 0):
                with sp.Fori(0, NG) as n:
                    sp.wait_ge(slow_sum, n * NSW + 1)
                    sp.dma_start(idx[:, 0, :], src_idx[:, bass.ds(n * ET, ET)]).then_inc(slow_idx, 16)
                sp.wait_ge(slow_landed, NG * ET * 16)

            for s in range(PER):
                sp.dma_start(idx[:, s, :], src_idx[:, s * ET:(s + 1) * ET]).then_inc(idx_in[s], 16)
            sp.dma_start(xin[:, :], x[0:P, :]).then_inc(xt_in, 16)
            sp.wait_ge(g_stored, 7 * 16)
            sp.wait_ge(acc_zero, 2)
            sp.dma_start(wd_sb, wd.rearrange("e (c p) n -> p (e c) n", p=P)).then_inc(wd_in, 16)

            def ahead(i, last):
                for s in range(PER):
                    if not last:
                        sp.wait_ge(landed[s], (i + 1) * (ET * 16))
                        sp.dma_start(idx[:, s, :], src_idx[:, bass.ds((i + 1) * (PER * ET) + s * ET, ET)])\
                          .then_inc(idx_in[s], 16)
                    if s == 2:
                        store(i)

            def store(i):
                if isinstance(i, int) and i < LATE:
                    return
                t = i - LATE
                sp.wait_ge(x2_ready, t + 1)
                sp.dma_start(xin[:, :], x[bass.ds((t + 1) * P, P), :]).then_inc(xt_in, 16)
                sp.wait_ge(xn_ready, t + 1)
                sp.dma_start(tok_dram[bass.ds(t * P, P), :], xcat[:, :]).then_inc(tok_stored, 16)

            for i in range(SEG1):
                ahead(i, False)
            with sp.Fori(SEG1, NI - 1) as i:
                ahead(i, False)
            ahead(NI - 1, True)
            t = NT - 2
            sp.wait_ge(x2_ready, t + 1)
            sp.dma_start(xin[0:LASTN, :], x[(NT - 1) * P:N, :]).then_inc(xt_in, 16)
            for t in (NT - 2, NT - 1):
                sp.wait_ge(xn_ready, t + 1)
                sp.dma_start(tok_dram[t * P:(t + 1) * P, :], xcat[:, :]).then_inc(tok_stored, 16)

            sp.dma_start(bd_sb, bd.rearrange("e n -> (e n)").partition_broadcast(P)).then_inc(bd_in, 16)

            sp.wait_ge(slots_ready, 1)

            def rings(u, s, first):
                j = u * UN + s
                if not first:
                    sp.wait_ge(tok_in[s], u * 16)
                sp.dma_start(gring[:, s:s + 1], gidx[:, bass.ds(j, 1)]).then_inc(gi_in[s], 16)
                if not first:
                    sp.wait_ge(stored[s], u * 16)
                sp.dma_start(sring[:, s:s + 1], sidx[:, bass.ds(j, 1)]).then_inc(si_in[s], 16)

            for s in range(UN):
                rings(0, s, True)
            with sp.Fori(1, NJ // UN) as u:
                for s in range(UN):
                    rings(u, s, False)

        @block.gpsimd
        def _(pool):
            own = Chain(pool, pool_own)
            pool.memset(nat_i[0][:, NB - 1, :], -1).then_inc(pads_set, 1)
            pool.memset(nat_i[1][:, NB - 1, :], -1).then_inc(pads_set, 1)
            pool.memset(hist_i[:, HR:NET], -1).then_inc(pads_set, 1)
            pool.memset(xs[:, NT - 1, :], 0.0).then_inc(pads_set, 1)
            pool.memset(ones[:, :], 1.0).then_inc(consts, 1)
            own(pool.memset(ident[:, :], 0.0))
            pool.affine_select(out=ident[:, :], in_=ident[:, :], compare_op=ALU.not_equal, fill=1.0, base=0,
                               pattern=[[-1, P]], channel_multiplier=1).then_inc(consts, 1)
            pool.iota(iota_i[:, :], pattern=[[1, SW]], base=0, channel_multiplier=0).then_inc(consts, 1)
            own(pool.memset(row0[:, :], 0.0))
            pool.memset(row0[0:1, :], 1.0).then_inc(consts, 1)
            pool.iota(lim_i[:, :], pattern=[[P, NI], [0, PER]], base=-P * (LATE - 1), channel_multiplier=0)\
                .then_inc(consts, 1)
            pool.iota(tid_i[:, :], pattern=[[P, NT]], base=1, channel_multiplier=1).then_inc(consts, 1)
            pool.iota(rank8_i[:, :], pattern=[[-1, EX]], base=EX, channel_multiplier=0).then_inc(consts, 1)
            own(pool.memset(upper[:, :], 1.0))
            pool.affine_select(out=upper[:, :], in_=upper[:, :], compare_op=ALU.is_gt, fill=0.0, base=0,
                               pattern=[[1, P]], channel_multiplier=-1).then_inc(consts, 1)
            pool.memset(ones_h[:, :], 1.0).then_inc(consts, 1)
            pool.memset(one8[:, :], 1.0).then_inc(consts, 1)
            pool.memset(eps_t[:, :], EPS).then_inc(consts, 1)
            pool.memset(ones_f[:, :], 1.0).then_inc(consts, 1)
            pool.memset(zeros_h[:, :], 0.0).then_inc(consts, 1)
            wait_count(pool, sums_done, 1)
            pool.tensor_scalar(nmean[:, :], ssum[:, :], -1.0 / D, None, ALU.mult).then_inc(mean_ready, 1)
            wait_count(pool, ssq_done, 1)
            wait_count(pool, flag_ready, 1)
            pool.memset(cnt_row[:, :], 0.0)
            pool.memset(accT[:, :, :], 0.0).then_inc(acc_zero, 1)

            wait_count(pool, g_stored, 7 * 16)

            def gather(s, j, done):
                pool.indirect_dma_start(rows_h[:, s, j * 2 * D:(j + 1) * 2 * D], None, g_dram[:, :],
                                        bass.IndirectOffsetOnAxis(idx[:, s, j:j + 1], 0)).then_inc(done, 16)

            general = pool.value_load(flag_i[0:1, 0:1], min_val=0, max_val=1)
            with pool.If(general != 0):
                with pool.Fori(0, NG) as n:
                    wait_count(pool, slow_idx, (n + 1) * 16)
                    wait_count(pool, slow_sum, n * NSW + 1)
                    for j in range(ET):
                        gather(0, j, slow_landed)
                wait_count(pool, slow_sum, NG * NSW + 1)

            def body(i):
                for s in range(PER):
                    wait_count(pool, idx_in[s], (i + 1) * 16)
                    if not (isinstance(i, int) and i == 0):
                        wait_count(pool, seg_done, i * PER + s - (PER - 1))
                    for j in range(ET):
                        gather(s, j, landed[s])

            body(0)
            with pool.Fori(1, NI) as i:
                body(i)

            wait_count(pool, tok_stored, NT * 16)

            def fetch(u, s):
                wait_count(pool, gi_in[s], (u + 1) * 16)
                pool.indirect_dma_start(trow[s], None, tok_dram[:, :],
                                        bass.IndirectOffsetOnAxis(gring[:, s:s + 1], 0)).then_inc(tok_in[s], 16)

            def scatter(u, s):
                wait_count(pool, si_in[s], (u + 1) * 16)
                wait_count(pool, o_ready, u * UN + s + 1)
                pool.indirect_dma_start(out[:, :], bass.IndirectOffsetOnAxis(sring[:, s:s + 1], 0), obuf[s], None,
                                        bounds_check=N - 1, oob_is_err=False).then_inc(stored[s], 16)

            for s in range(UN):
                fetch(0, s)
            with pool.Fori(1, NJ // UN) as u:
                for s in range(UN):
                    scatter(u - 1, s)
                    fetch(u, s)
            for s in range(UN):
                scatter(NJ // UN - 1, s)
            for s in range(UN):
                wait_count(pool, stored[s], 16 * (NJ // UN))

        @block.scalar
        def _(act):
            for dst_t, src_t in (
                (gw_sb[:, 0:KD, :], gnn_w1.rearrange("(k p) n -> p k n", p=P)),
                (gw_sb[:, KD:2 * KD, :], gnn_w2.rearrange("(k p) n -> p k n", p=P)),
                (gb_sb[:, :], gnn_b.partition_broadcast(P)),
                (w1_sb[:, :, :], w1.rearrange("(k p) n -> p k n", p=P)),
                (b1_sb[:, :], b1.rearrange("(c p) -> p c", p=P)),
                (wg_sb[:, :, :], wg.rearrange("(c p) e -> p c e", p=P)),
                (bg_sb[:, :], bg.partition_broadcast(P)),
            ):
                act.dma_start(dst_t, src_t).then_inc(weights_in, 16)
            act.wait_ge(x_in, 7 * 16)
            def reduce_row(q, t, **how):
                if q >= NJUNK:
                    act.wait_ge(act_own, q - NJUNK + 1)
                act.activation(junk[q % NJUNK], xs[:, t, :], **how).then_inc(act_own, 1)

            for t in range(NT):
                reduce_row(t, t, func=ACT.Copy, accum_out=ssum[:, t:t + 1])
            act.wait_ge(act_own, NT)
            act.sem_inc(sums_done, 1)
            act.wait_ge(mean_ready, 1)
            for t in range(NT):
                reduce_row(NT + t, t, func=ACT.Square, bias=nmean[:, t:t + 1], accum_out=ssq[:, t:t + 1])
            act.wait_ge(act_own, 2 * NT)
            act.sem_inc(ssq_done, 1)
            act.wait_ge(deg_read, 1)
            act.activation(deg[:, :], deg[:, :], ACT.Sqrt)
            act.activation(ssq[:, :], ssq[:, :], ACT.Sqrt).then_inc(roots, 1)
            act.wait_ge(scales, 1)
            for t in range(NT):
                c = t // GC
                if t % GC == 0 and c >= 3:
                    act.wait_ge(g_lo, c - 2)
                ins = act.activation(gtmp[:, c % 3, t % GC, :], xs[:, t, :], ACT.Identity, bias=gsb[:, t:t + 1],
                                     scale=gsc[:, t:t + 1])
                if t % GC == GC - 1:
                    ins.then_inc(g_f32, 1)

            def tile_head(t, first=False):
                act.wait_ge(xt_in, (t + 1) * 16)
                if not first:
                    act.wait_ge(fu_t, t)
                at = bass.ds(t, 1)
                act.activation(fu[:, 0, :], xin[:, :], ACT.Identity, bias=nb[:, at], scale=rstd[:, at])
                act.activation(fu[:, 1, :], xin[:, :], ACT.Identity, bias=usb[:, at], scale=usc[:, at])\
                    .then_inc(fu_ready, 1)

            def tile_gelu(t, first):
                if not first:
                    act.wait_ge(lg_done, t)
                for c in range(KH):
                    b = c // 4
                    if c % 4 == 0:
                        act.wait_ge(h_done[b], t + 1)
                    ins = act.activation(hT[:, 0, c, :], bkH[b][:, (c % 4) * P:(c % 4 + 1) * P], ACT.Gelu,
                                         bias=b1_sb[:, c:c + 1])
                ins.then_inc(gelu_done, 1)

            def tile_norms(t):
                act.wait_ge(e_ready, t + 1)
                act.activation(sqj[:, :], emb2[:, :], ACT.Square, accum_out=ss[:, :]).then_inc(ss_ready, 1)
                act.wait_ge(ss_ready, t + 1)
                act.activation(nrm[:, :], ss[:, :], ACT.Sqrt).then_inc(nrm_ready, 1)
                act.wait_ge(var_ready, t + 1)
                act.activation(sd[:, :], mv[:, 1:2], ACT.Sqrt, bias=eps_t[:, :]).then_inc(sd_ready, 1)
                act.wait_ge(xn_t, t + 1)
                act.activation(xT[:, 0, :, :], bkL[:, 0:D].rearrange("p (k n) -> p k n", k=KD), ACT.Copy)\
                    .then_inc(xt_ready, 1)

            act.wait_ge(weights_in, 7 * 16)
            act.wait_ge(consts, 13)
            tile_head(0, True)

            def body(i):
                if isinstance(i, int) and i < LATE:
                    return
                t = i - LATE
                if not (isinstance(t, int) and t == 0):
                    tile_gelu(t - 1, isinstance(t, int) and t == 1)
                tile_norms(t)
                tile_head(t + 1)

            edge_loop(act, body)
            for t in (NT - 2, NT - 1):
                tile_gelu(t - 1, False)
                tile_norms(t)
                if t < NT - 1:
                    tile_head(t + 1)
            tile_gelu(NT - 1, False)

            act.wait_ge(exp_in, 1)
            act.activation(ra[:, :, :], ra[:, :, :], ACT.Exp).then_inc(exp_done, 1)

            def gelu_tile(u, s, first):
                j = u * UN + s
                for b in (0, 1):
                    hb = (bkH if s % 2 == 0 else bkA)[b]
                    act.wait_ge(h2_done, 2 * j + b + 1)
                    if not first and b == 0:
                        act.wait_ge(y_done, j - 1)
                    for c in range(4):
                        ins = act.activation(hT[:, s % 2, 4 * b + c, :], hb[:, c * P:(c + 1) * P], ACT.Gelu,
                                             bias=b1_sb[:, 4 * b + c:4 * b + c + 1])
                    ins.then_inc(gelu2, 1)

            for s in range(UN):
                gelu_tile(0, s, s < 2)
            with act.Fori(1, NJ // UN) as u:
                for s in range(UN):
                    gelu_tile(u, s, False)

        @block.vector
        def _(dve):
            own = Chain(dve, dve_own)
            dve.wait_ge(consts, 13)
            dve.tensor_copy(iota_f[:, :], iota_i[:, 0:P])
            dve.tensor_copy(limf[:, :], lim_i[:, :])
            dve.tensor_copy(tid[:, :], tid_i[:, :])
            dve.tensor_copy(rank8[:, :], rank8_i[:, :])
            dve.wait_ge(hist_in, 2 * 16)
            own(dve.tensor_scalar(part_i, hist_i, P - 1, None, ALU.bitwise_and))
            own(dve.tensor_copy(hist_lo, part_i))
            own(dve.tensor_scalar(part_i, hist_i, 7, None, ALU.arith_shift_right))
            own(dve.tensor_copy(hist_hi, part_i))
            dve.wait_ge(edges_in, 6 * 16)
            for k in (0, 1):
                dve.tensor_copy(nat_f[k], nat_i[k]).then_inc(nat_ready, 1)

            H = 4 * BR

            def table(banks, k, out_t, least):
                dve.wait_ge(tables_t, k + 1)
                dve.tensor_scalar(out_t[:, 0:H], banks[0][:, 0:H], least, None, ALU.max)
                own(dve.tensor_scalar(out_t[:, H:NET], banks[1][:, 0:NET - H], least, None, ALU.max))

            table((bkT, bkE), 0, src_idx, 0.0)
            table(bkH, 1, dstf, -1.0)
            dve.memset(rel[:, NET:NET + ET], -FAR)
            dve.sem_inc(dst_ready, 1)

            chunk_own = Chain(dve, hist_own)
            with dve.Fori(0, HC) as c:
                chunk_own.at(c * 2)
                dve.wait_ge(hist_used, c + 1)
                chunk_own(dve.tensor_copy(lo_c[:, :], hist_lo[:, bass.ds(c * HT, HT)]))
                chunk_own(dve.tensor_copy(hi_c[:, :], hist_hi[:, bass.ds(c * HT, HT)]))
                for q in range(NHI):
                    dve.tensor_scalar(bins_hi[:, q, :], hi_c[:, :], float(q), None, ALU.is_equal)
                for q in range(NLO):
                    ins = dve.tensor_scalar(bins_lo[:, q, :], lo_c[:, :], float(q), None, ALU.is_equal)
                ins.then_inc(hist_oh, 1)

            dve.wait_ge(hist_used, HC + 1)
            own(dve.tensor_scalar(deg[:, :], bkC[:, 0:NT], 1.0, None, ALU.max))
            dve.wait_ge(ssq_done, 1)
            own(dve.tensor_scalar(ssq[:, :], ssq[:, :], 1.0 / D, EPS, ALU.mult, ALU.add))
            dve.sem_inc(deg_read, 1)
            dve.wait_ge(roots, 1)
            dve.reciprocal(rs[:, :], deg[:, :])
            own(dve.reciprocal(rstd[:, :], ssq[:, :]))
            own(dve.tensor_tensor(nb[:, :], nmean[:, :], rstd[:, :], ALU.mult))
            own(dve.tensor_scalar(reffs[:, :], rs[:, :], GS, None, ALU.mult))
            dve.tensor_tensor(gsc[:, :], rstd[:, :], reffs[:, :], ALU.mult)
            own(dve.tensor_tensor(gsb[:, :], nb[:, :], reffs[:, :], ALU.mult))
            dve.sem_inc(scales, 1)
            own(dve.tensor_scalar(deg[:, :], deg[:, :], GS, None, ALU.mult))
            dve.tensor_tensor(usc[:, :], rstd[:, :], deg[:, :], ALU.mult)
            dve.tensor_tensor(usb[:, :], nb[:, :], deg[:, :], ALU.mult)
            dve.tensor_scalar(reffs[:, :], rs[:, :], 1.0 / GS, None, ALU.mult)
            for c in range(NT // GC):
                dve.wait_ge(g_f32, c + 1)
                dve.tensor_copy(xg[:, GC * c:GC * (c + 1), 0, :], gtmp[:, c % 3, :, :]).then_inc(g_hi, 1)
                dve.wait_ge(g_hi, c + 1)
                dve.tensor_tensor(xg[:, GC * c:GC * (c + 1), 1, :], gtmp[:, c % 3, :, :],
                                  xg[:, GC * c:GC * (c + 1), 0, :], ALU.subtract).then_inc(g_lo, 1)

            dve.wait_ge(base_bc, 1)
            own(dve.tensor_copy(basef[:, :], bkL[:, 0:NG]))
            dve.tensor_copy(base_i[:, :], basef[0:1, :])
            own(dve.tensor_tensor(rel[:, 0:NET].rearrange("p (n j) -> p n j", j=ET),
                                  dstf[:, 0:NET].rearrange("p (n j) -> p n j", j=ET),
                                  basef[:, :].unsqueeze(2).to_broadcast([P, NG, ET]), ALU.subtract))
            own(dve.tensor_scalar(viol, rel[:, 0:NET], 0.0, None, ALU.is_lt))
            own(dve.scalar_tensor_tensor(viol2, rel[:, 0:NET], float(WIN), viol, ALU.is_ge, ALU.add))
            own(dve.scalar_tensor_tensor(viol, dstf[:, 0:NET], 0.0, viol2, ALU.is_ge, ALU.mult))
            dve.tensor_tensor(viol2[:, 0:NG], basef[:, :], limf[:, :], ALU.is_lt)
            own(dve.tensor_reduce(small[:, 0:1], viol, AX.X, ALU.add))
            own(dve.tensor_reduce(small[:, 1:2], viol2[:, 0:NG], AX.X, ALU.add))
            dve.tensor_tensor(small[:, 2:3], small[:, 0:1], small[:, 1:2], ALU.add).then_inc(viol_ready, 1)
            dve.wait_ge(viol_sum, 1)
            own(dve.tensor_scalar(small[:, 3:4], bkL[:, 256:257], 1.0, None, ALU.min))
            own(dve.tensor_scalar(small[:, 4:5], small[:, 3:4], -FAR, None, ALU.mult))
            dve.tensor_copy(flag_i[:, :], small[0:1, 3:4])
            own(dve.tensor_scalar(rel[:, 0:NET], rel[:, 0:NET], small[:, 4:5], None, ALU.add))
            dve.sem_inc(flag_ready, 1)
            dve.wait_ge(acc_zero, 1)

            general = dve.value_load(flag_i[0:1, 0:1], min_val=0, max_val=1)
            dve.wait_ge(g_stored, 7 * 16)
            with dve.If(general != 0):
                dve.tensor_copy(slow_iota, iota_i[:, :]).then_inc(slow_added, 1)
                slow = Chain(dve, slow_own)
                SLOW_OWN = 4
                with dve.Fori(0, NG) as n:
                    with dve.Fori(0, NSW) as w:
                        slow.at((n * NSW + w) * SLOW_OWN)
                        slow(dve.tensor_copy(small[:, 1:2], iota_i[:, bass.ds(w, 1)]))
                        slow(dve.tensor_scalar(small[:, 1:2], small[:, 1:2], -float(SW), None, ALU.mult))
                        slow(dve.tensor_scalar(small[:, 4:8], dstf[:, bass.ds(n * ET, ET)], small[:, 1:2], None,
                                               ALU.add))
                        for j in range(ET):
                            ins = dve.tensor_scalar(slow_oh[:, j, :], slow_iota, small[:, 4 + j:5 + j], None,
                                                    ALU.is_equal)
                        ins.then_inc(slow_oh_ready, 1)
                        dve.wait_ge(slow_sum, n * NSW + w + 2)
                        for h in range(KD):
                            a = accT[:, h, bass.ds(w * SW, SW)]
                            ins = dve.tensor_tensor(a, bkA[h][:, :], a, ALU.add)
                        a = cnt_row[:, bass.ds(w * SW, SW)]
                        slow(dve.tensor_tensor(a, bkC[0:1, :], a, ALU.add))
                        dve.sem_inc(slow_added, 1)
                        assert slow.k == SLOW_OWN
            dve.sem_inc(acc_zero, 1)

            def windows(n, slot2):
                dve.tensor_tensor(woh[:, slot2, :, :], iota_f[:, 0:WIN].unsqueeze(1).to_broadcast([P, ET, WIN]),
                                  rel[:, bass.ds(n * ET, ET)].unsqueeze(2).to_broadcast([P, ET, WIN]),
                                  ALU.is_equal).then_inc(oh_ready, 1)

            def accumulate(n, s):
                base = dve.value_load(base_i[0:1, bass.ds(n, 1)], min_val=0, max_val=N - 1)
                a = accT[:, :, bass.ds(base, WIN)]
                c = cnt_row[:, bass.ds(base, WIN)]
                dve.wait_ge(seg_done, n + 1)
                dve.tensor_tensor(a, segp[s % 2], a, ALU.add)
                loop_own(dve.tensor_tensor(c, segc[s % 2], c, ALU.add))
                dve.sem_inc(seg_added, 1)

            loop_own = Chain(dve, edge_own)

            def piece0(t, first):
                if not first:
                    dve.wait_ge(e_done, t)
                dve.tensor_copy(cnt_t[:, :], cnt_row[:, bass.ds(t * P, P)])
                dve.wait_ge(fu_t, t + 1)
                g = accT[:, :, bass.ds(t * P, P)]
                fT = bkT[:, 0:D].rearrange("p (k n) -> p k n", k=KD)
                uT = bkT[:, D:2 * D].rearrange("p (k n) -> p k n", k=KD)
                dve.tensor_tensor(lT[:, 0:KD, :], uT, g, ALU.add)
                dve.tensor_tensor(lT[:, KD:2 * KD, :], fT, g, ALU.mult).then_inc(l_ready, 1)
                dve.wait_ge(l_ready, t + 1)

            def piece1(t, first):
                dve.wait_ge(e_done, t + 1)
                loop_own(dve.tensor_scalar(reff[:, :], bkE[:, D:D + 1], 0.5, reffs[:, bass.ds(t, 1)], ALU.is_gt, ALU.mult))
                loop_own(dve.scalar_tensor_tensor(emb[:, :], bkE[:, 0:D], reff[:, :], gb_sb[:, :], ALU.mult, ALU.add))
                dve.scalar_tensor_tensor(emb2[:, :], emb[:, :], 0.01, emb[:, :], ALU.mult, ALU.max)\
                    .then_inc(e_ready, 1)

            def piece2(t, first):
                dve.wait_ge(nrm_ready, t + 1)
                loop_own(dve.tensor_scalar(rn[:, :], nrm[:, :], 1e-12, None, ALU.max))
                loop_own(dve.reciprocal(rn[:, :], rn[:, :]))
                if not first:
                    dve.wait_ge(tok_stored, t * 16)
                x2 = xcat[:, 0:D]
                dve.scalar_tensor_tensor(x2, emb2[:, :], rn[:, :], xin[:, :], ALU.mult, ALU.add).then_inc(x2_ready, 1)
                dve.wait_ge(x2_ready, t + 1)
                loop_own(dve.bn_stats(st6[:, :], x2))
                dve.sem_inc(ticks, 1)
                dve.bn_aggr(mv[:, :], st6[:, :]).then_inc(var_ready, 1)
                dve.wait_ge(sd_ready, t + 1)
                loop_own(dve.reciprocal(rstd2[:, :], sd[:, :]))
                dve.tensor_scalar(xcat[:, D:2 * D], x2, mv[:, 0:1], rstd2[:, :], ALU.subtract, ALU.mult)\
                    .then_inc(xn_ready, 1)

            def piece3(t, first):
                if not first:
                    dve.wait_ge(lg_done, t)
                    dve.tensor_tensor(logits[:, bass.ds(t - 1, 1), :], bkC[:, 0:EX].unsqueeze(1),
                                      bg_sb[:, :].unsqueeze(1), ALU.add).then_inc(lg_read, 1)

            PIECES = (piece0, piece1, piece2, piece3)
            OWN_EDGE, OWN_TILE = PER, 6

            def body(i):
                tile = not (isinstance(i, int) and i < LATE)
                loop_own.at(i * OWN_EDGE + (i - LATE) * OWN_TILE if tile else i * OWN_EDGE)
                for s in range(PER):
                    n = i * PER + s
                    if not (isinstance(i, int) and n == 0):
                        dve.wait_ge(seg_done, n)
                    windows(n + 1, (s + 1) % 2)
                    accumulate(n, s)
                    if tile:
                        PIECES[s](i - LATE, isinstance(i, int) and i == LATE)
                assert loop_own.k == OWN_EDGE + (OWN_TILE if tile else 0)

            windows(0, 0)
            edge_loop(dve, body)
            loop_own.at(NI * OWN_EDGE + (NI - LATE) * OWN_TILE)
            for t in (NT - 2, NT - 1):
                for piece in PIECES:
                    piece(t, False)
            dve.wait_ge(lg_done, NT)
            loop_own(dve.tensor_tensor(logits[:, NT - 1, :], bkC[:, 0:EX], bg_sb[:, :], ALU.add))

            r = loop_own
            by_e = lambda a: a[:, :].unsqueeze(2).to_broadcast([P, NT, EX])
            by_t = lambda a: a[:, :].unsqueeze(1).to_broadcast([P, NT, EX])
            dve.memset(keep[:, :, 1:NT], 1.0)
            dve.memset(keep[:, :, 0:1], 0.0)
            r(dve.tensor_reduce(mx[:, :], logits[:, :, :], AX.X, ALU.max))
            dve.tensor_tensor(ra[:, :, :], logits[:, :, :], by_e(mx), ALU.subtract).then_inc(exp_in, 1)
            dve.wait_ge(exp_done, 1)
            r(dve.tensor_reduce(mx[:, :], ra[:, :, :], AX.X, ALU.add))
            dve.reciprocal(prob[:, :], mx[:, :])
            r(dve.tensor_scalar(rb[:, :, :], ra[:, :, :], 1.0, None, ALU.is_ge))
            r(dve.tensor_tensor(rb[:, :, :], rb[:, :, :], by_t(rank8), ALU.mult))
            r(dve.tensor_reduce(mx[:, :], rb[:, :, :], AX.X, ALU.max))
            r(dve.tensor_tensor(oneh[:, :, :], by_e(mx), by_t(rank8), ALU.is_equal))
            r(dve.tensor_scalar(valid[:, :], tid[:, :], float(N), None, ALU.is_le))
            r(dve.tensor_tensor(oneh[:, :, :], oneh[:, :, :], by_e(valid), ALU.mult))
            dve.tensor_copy(oneh_h[:, :, :], oneh[:, :, :]).then_inc(oneh_ready, 1)
            dve.wait_ge(ranks, 1)
            r(dve.tensor_copy(tot[:, :, :], bkE[:, 0:LE].rearrange("p (t e) -> p e t", e=EX)))
            r(dve.tensor_tensor_scan(cum[:, :, :].rearrange("p e t -> p (e t)"),
                                     keep[:, :, :].rearrange("p e t -> p (e t)"),
                                     tot[:, :, :].rearrange("p e t -> p (e t)"), 0.0, ALU.mult, ALU.add))
            r(dve.tensor_scalar(te[:, :], cum[:, :, NT - 1], float(P - 1), None, ALU.add))
            r(dve.tensor_copy(te_i[:, :], te[:, :]))
            r(dve.tensor_scalar(te_i[:, :], te_i[:, :], 7, None, ALU.arith_shift_right))
            r(dve.tensor_copy(te[:, :], te_i[:, :]))
            r(dve.tensor_tensor_scan(tinc[:, :], one8[:, :], te[:, :], 0.0, ALU.mult, ALU.add))
            r(dve.tensor_tensor(tstart[:, :], tinc[:, :], te[:, :], ALU.subtract))
            r(dve.tensor_scalar(tstart[:, :], tstart[:, :], float(P), None, ALU.mult))
            r(dve.tensor_tensor(cum[:, :, :], cum[:, :, :], tot[:, :, :], ALU.subtract))
            r(dve.tensor_tensor(cum[:, :, :], cum[:, :, :], tstart[:, :].unsqueeze(2).to_broadcast([P, EX, NT]), ALU.add))
            r(dve.tensor_tensor(rb[:, :, :], bkT[:, 0:LE].rearrange("p (t e) -> p t e", e=EX),
                                cum[:, :, :].rearrange("p e t -> p t e"), ALU.add))
            r(dve.tensor_tensor(rb[:, :, :], rb[:, :, :], oneh[:, :, :], ALU.mult))
            r(dve.tensor_reduce(pos[:, :], rb[:, :, :], AX.X, ALU.add))
            r(dve.tensor_scalar(valid[:, :], valid[:, :], -1.0, FAR, ALU.add, ALU.mult))
            r(dve.tensor_tensor(pos[:, :], pos[:, :], valid[:, :], ALU.add))
            r(dve.tensor_copy(pos_i[:, :], pos[:, :]))
            dve.tensor_scalar(plo_i[:, :], pos_i[:, :], P - 1, None, ALU.bitwise_and)
            r(dve.tensor_scalar(pos_i[:, :], pos_i[:, :], 7, None, ALU.arith_shift_right))
            dve.tensor_copy(plo[:, :], plo_i[:, :])
            r(dve.tensor_copy(phi[:, :], pos_i[:, :]))
            for t in range(NT):
                if t >= 2:
                    dve.wait_ge(pm_used, t - 1)
                dve.tensor_scalar(ploh[:, t % 2, :], iota_f[:, :], plo[:, t:t + 1], None, ALU.is_equal)
                dve.tensor_scalar(phoh[:, t % 2, 0, :], iota_f[:, 0:NJ], phi[:, t:t + 1], tid[:, t:t + 1],
                                  ALU.is_equal, ALU.mult)
                dve.tensor_scalar(phoh[:, t % 2, 1, :], iota_f[:, 0:NJ], phi[:, t:t + 1], prob[:, t:t + 1],
                                  ALU.is_equal, ALU.mult).then_inc(pm_oh, 1)
            iota_j = iota_f[0:1, 0:NJ].unsqueeze(2).to_broadcast([1, NJ, EX])
            r(dve.tensor_tensor(jx[:, :, :], iota_j, tinc[0:1, :].unsqueeze(1).to_broadcast([1, NJ, EX]), ALU.is_ge))
            r(dve.tensor_reduce(jexp[:, :], jx[:, :, :], AX.X, ALU.add))
            r(dve.tensor_scalar(jexp[:, :], jexp[:, :], float(EX - 1), None, ALU.min))
            r(dve.tensor_copy(jexp_i[:, :], jexp[:, :]))
            dve.wait_ge(pm_used, NT)
            r(dve.tensor_copy(slot[:, :, :], bkC[:, 0:2 * NJ].rearrange("p (a j) -> p a j", a=2)))
            r(dve.tensor_scalar(gidx[:, :], slot[:, 0, :], -1.0, 0.0, ALU.add, ALU.max))
            r(dve.tensor_scalar(sidf[:, :], slot[:, 0, :], 0.5, float(2 * N), ALU.is_lt, ALU.mult))
            r(dve.scalar_tensor_tensor(sidf[:, :], slot[:, 0, :], -1.0, sidf[:, :], ALU.add, ALU.add))
            r(dve.tensor_copy(sidx[:, :], sidf[:, :]))
            dve.sem_inc(slots_ready, 1)

            dve.wait_ge(bd_in, 16)

            def t_copy(j, s):
                dve.wait_ge(t2_done, j + 1)
                dve.tensor_copy(xT[:, s % 2, :, :], bkT2[s % 2][:, 0:D].rearrange("p (k n) -> p k n", k=KD))\
                    .then_inc(t2_read, 1)

            def finish(u, s):
                j = u * UN + s
                e = dve.value_load(jexp_i[0:1, bass.ds(j, 1)], min_val=0, max_val=EX - 1)
                dve.wait_ge(y_done, j + 1)
                if not (isinstance(j, int) and j == 0):
                    dve.wait_ge(o_ready, j)
                dve.tensor_tensor(yb, bkY[s % 2][:, 0:D], bd_sb[:, bass.ds(e * D, D)], ALU.add).then_inc(y_read, 1)
                dve.wait_ge(y_read, j + 1)
                if not (isinstance(u, int) and u == 0):
                    dve.wait_ge(stored[s], u * 16)
                dve.scalar_tensor_tensor(obuf[s], yb, slot[:, 1, bass.ds(j, 1)], trow[s][:, 0:D], ALU.mult, ALU.add)\
                    .then_inc(o_ready, 1)

            def steps(u, first, last):
                for s in range(UN):
                    if not (last and s == UN - 1):
                        t_copy(u * UN + s + 1, (s + 1) % UN)
                    if s:
                        finish(u, s - 1)
                    elif not first:
                        finish(u - 1, UN - 1)

            t_copy(0, 0)
            steps(0, True, False)
            steps(1, False, False)
            with dve.Fori(2, NJ // UN - 1) as u:
                steps(u, False, False)
            steps(NJ // UN - 1, False, True)
            finish(NJ // UN - 1, UN - 1)

        @block.tensor
        def _(pe):
            mm, tr = pe.matmul, pe.transpose
            pe.wait_ge(consts, 13)
            for k, banks in enumerate(((bkT, bkE), bkH)):
                pe.wait_ge(nat_ready, k + 1)
                for b in range(NB):
                    o = banks[b // 4][:, (b % 4) * BR:(b % 4 + 1) * BR]
                    ins = tr(o, nat_f[k][:, b, :], ident[0:BR, 0:BR])
                ins.then_inc(tables_t, 1)

            mm(bkC[:, 0:NHI], zeros_h[:, :], zeros_h[:, 0:NHI], start=True, stop=True).then_inc(hist_used, 1)
            with pe.Fori(0, HC) as c:
                pe.wait_ge(hist_oh, c + 1)
                for t in range(HT):
                    ins = mm(bkC[:, 0:NHI], bins_lo[:, :, t], bins_hi[:, :, t], start=False, stop=False,
                             skip_group_check=True)
                ins.then_inc(hist_used, 1)
            pe.wait_ge(dst_ready, 1)
            mm(bkL[:, 0:NG], row0[:, :], dstf[:, 0:NET:ET], start=True, stop=True).then_inc(base_bc, 1)
            pe.wait_ge(viol_ready, 1)
            mm(bkL[:, D:D + 1], ones[:, :], small[:, 2:3], start=True, stop=True).then_inc(viol_sum, 1)

            pe.wait_ge(flag_ready, 1)
            general = pe.value_load(flag_i[0:1, 0:1], min_val=0, max_val=1)
            with pe.If(general != 0):
                pe.sem_inc(slow_sum, 1)
                with pe.Fori(0, NG) as n:
                    wait_count(pe, slow_landed, (n + 1) * (ET * 16))
                    with pe.Fori(0, NSW) as w:
                        pe.wait_ge(slow_oh_ready, n * NSW + w + 1)
                        pe.wait_ge(slow_added, n * NSW + w + 1)
                        for h in range(KD):
                            for j in range(ET):
                                for a in (0, 1):
                                    at = (2 * j + a) * D + h * P
                                    mm(bkA[h][:, :], rows_h[:, 0, at:at + P], slow_oh[:, j, :], start=j + a == 0,
                                       stop=j + a == ET)
                        for j in range(ET):
                            ins = mm(bkC[0:1, :], ones_f[:, :], slow_oh[:, j, :], start=j == 0, stop=j == ET - 1)
                        ins.then_inc(slow_sum, 1)
                pe.wait_ge(slow_added, NG * NSW + 1)

            pe.wait_ge(weights_in, 7 * 16)

            def segment(i, s):
                n = i * PER + s
                pe.wait_ge(landed[s], (i + 1) * (ET * 16))
                pe.wait_ge(oh_ready, n + 1)
                if not (isinstance(n, int) and n < 2):
                    pe.wait_ge(seg_added, n - 1)
                for h in range(KD):
                    for j in range(ET):
                        for a in (0, 1):
                            at = (2 * j + a) * D + h * P
                            mm(segp[s % 2][:, h, :], rows_h[:, s, at:at + P], woh[:, s % 2, j, :], start=j + a == 0,
                               stop=j + a == ET)
                for j in range(ET):
                    ins = mm(segc[s % 2], ones_f[:, :], woh[:, s % 2, j, :], start=j == 0, stop=j == ET - 1)
                ins.then_inc(seg_done, 1)

            def gates(t):
                pe.wait_ge(gelu_done, t + 1)
                if not (isinstance(t, int) and t == 0):
                    pe.wait_ge(lg_read, t)
                for c in range(KH):
                    ins = mm(bkC[:, 0:EX], hT[:, 0, c, :], wg_sb[:, c, :], start=c == 0, stop=c == KH - 1)
                ins.then_inc(lg_done, 1)

            def transpose_fu(t, first):
                pe.wait_ge(fu_ready, t + 1)
                if not first:
                    pe.wait_ge(l_ready, t)
                for a in range(2):
                    for k in range(KD):
                        q = a * KD + k
                        ins = tr(bkT[:, q * P:(q + 1) * P], fu[:, a, k * P:(k + 1) * P], ident[:, :])
                ins.then_inc(fu_t, 1)

            def embed(t, first):
                pe.wait_ge(l_ready, t + 1)
                if not first:
                    pe.wait_ge(e_ready, t)
                mm(bkE[:, D:D + 1], cnt_t[:, :], ones[0:1, 0:1], start=True, stop=True)
                for q in range(2 * KD):
                    ins = mm(bkE[:, 0:D], lT[:, q, :], gw_sb[:, q, :], start=q == 0, stop=q == 2 * KD - 1)
                ins.then_inc(e_done, 1)

            def transpose_xn(t, first):
                pe.wait_ge(xn_ready, t + 1)
                if not first:
                    pe.wait_ge(xt_ready, t)
                for k in range(KD):
                    ins = tr(bkL[:, k * P:(k + 1) * P], xcat[:, D + k * P:D + (k + 1) * P], ident[:, :])
                ins.then_inc(xn_t, 1)

            def hidden_bank(out_bank, xslot, b):
                for q in range(4):
                    c = 4 * b + q
                    for k in range(KD):
                        ins = mm(out_bank[:, q * P:(q + 1) * P], w1_sb[:, k, c * P:(c + 1) * P], xT[:, xslot, k, :],
                                 start=k == 0, stop=k == KD - 1)
                return ins

            def hidden(t):
                pe.wait_ge(xt_ready, t + 1)
                if not (isinstance(t, int) and t == 0):
                    pe.wait_ge(gelu_done, t)
                for b in (0, 1):
                    hidden_bank(bkH[b], 0, b).then_inc(h_done[b], 1)

            def body(i):
                tile = not (isinstance(i, int) and i < LATE)
                first = isinstance(i, int) and i == LATE
                t = i - LATE
                segment(i, 0)
                if tile:
                    transpose_fu(t, first)
                    if not first:
                        hidden(t - 1)
                segment(i, 1)
                if tile:
                    embed(t, first)
                segment(i, 2)
                if tile and not first:
                    gates(t - 1)
                segment(i, 3)
                if tile:
                    transpose_xn(t, first)

            edge_loop(pe, body)
            for t in (NT - 2, NT - 1):
                transpose_fu(t, False)
                hidden(t - 1)
                embed(t, False)
                gates(t - 1)
                transpose_xn(t, False)
            hidden(NT - 1)
            gates(NT - 1)

            pe.wait_ge(oneh_ready, 1)
            flat = oneh_h[:, :, :].rearrange("p t e -> p (t e)")
            mm(bkT[:, 0:LE], upper[:, :], flat, start=True, stop=True)
            mm(bkE[:, 0:LE], ones_h[:, :], flat, start=True, stop=True).then_inc(ranks, 1)
            for t in range(NT):
                pe.wait_ge(pm_oh, t + 1)
                mm(bkC[:, 0:2 * NJ], ploh[:, t % 2, :], phoh[:, t % 2, :, :].rearrange("p a j -> p (a j)"),
                   start=t == 0, stop=t == NT - 1).then_inc(pm_used, 1)

            pe.wait_ge(slots_ready, 1)
            pe.wait_ge(wd_in, 16)

            def transpose_tok(u, s, first):
                j = u * UN + s
                pe.wait_ge(tok_in[s], (u + 1) * 16)
                if not first:
                    pe.wait_ge(t2_read, j - 1)
                for k in range(KD):
                    ins = tr(bkT2[s % 2][:, k * P:(k + 1) * P], trow[s][:, D + k * P:D + (k + 1) * P], ident[:, :])
                ins.then_inc(t2_done, 1)

            def hidden2(u, s, first):
                j = u * UN + s
                pe.wait_ge(t2_read, j + 1)
                if not first:
                    pe.wait_ge(gelu2, 2 * (j - 1))
                for b in (0, 1):
                    hidden_bank((bkH, bkA)[s % 2][b], s % 2, b).then_inc(h2_done, 1)

            def expert(u, s, first):
                j = u * UN + s
                e = pe.value_load(jexp_i[0:1, bass.ds(j, 1)], min_val=0, max_val=EX - 1)
                pe.wait_ge(gelu2, 2 * (j + 1))
                if not first:
                    pe.wait_ge(y_read, j - 1)
                for c in range(KH):
                    ins = mm(bkY[s % 2][:, 0:D], hT[:, s % 2, c, :], big[:, bass.ds(e * (KH * D) + c * D, D)],
                             start=c == 0, stop=c == KH - 1)
                ins.then_inc(y_done, 1)

            def steps(u, first, last):
                for s in range(UN):
                    if s < UN - 1:
                        transpose_tok(u, s + 1, first and s + 1 < 2)
                    elif not last:
                        transpose_tok(u + 1, 0, False)
                    hidden2(u, s, first and s < 2)
                    if s:
                        expert(u, s - 1, first and s - 1 < 2)
                    elif not first:
                        expert(u - 1, UN - 1, False)

            transpose_tok(0, 0, True)
            steps(0, True, False)
            with pe.Fori(1, NJ // UN - 1) as u:
                steps(u, False, False)
            steps(NJ // UN - 1, False, True)
            expert(NJ // UN - 1, UN - 1, False)


def kernel(x, src, dst, L0_gnn_W1, L0_gnn_W2, L0_gnn_b, L0_ffn_W1, L0_ffn_b1, L0_ffn_Wg, L0_ffn_bg, L0_ffn_Wd,
           L0_ffn_bd):
    import numpy as np
    import concourse.bacc as bacc
    from concourse.bass_utils import run_bass_kernel_spmd

    nc = bacc.Bacc("TRN2", target_bir_lowering=False, num_devices=1)
    inputs = dict(x=x, src=src, dst=dst, gnn_w1=L0_gnn_W1, gnn_w2=L0_gnn_W2, gnn_b=L0_gnn_b, w1=L0_ffn_W1,
                  b1=L0_ffn_b1, wg=L0_ffn_Wg, bg=L0_ffn_bg, wd=L0_ffn_Wd, bd=L0_ffn_bd)
    arrays, args = {}, []
    for name, a in inputs.items():
        arrays[name] = np.ascontiguousarray(a)
        args.append(nc.dram_tensor(name, arrays[name].shape, mybir.dt.from_np(arrays[name].dtype),
                                   kind="ExternalInput").ap())
    args.append(nc.dram_tensor("out", (N, D), F32, kind="ExternalOutput").ap())
    build(nc, *args)
    r = run_bass_kernel_spmd(nc, [arrays], core_ids=[0])
    return r.results[0]["out"]
```

```python
from contextlib import ExitStack

import concourse.bass as bass
from concourse import mybir

F32 = mybir.dt.float32
BF16 = mybir.dt.bfloat16
F16 = mybir.dt.float16
I32 = mybir.dt.int32
ALU = mybir.AluOpType
ACT = mybir.ActivationFunctionType
AX = mybir.AxisListType

P = 128
N = 6250
D = 256
NE = 100000
HID = 1024
EX = 8
KD = D // P
KH = HID // P
NT = (N + P - 1) // P
LASTN = N - (NT - 1) * P
NLO = P
NHI = NT
HC = 4
ET = 4
GE = ET * P
NG = -(-NE // GE)
NET = NG * ET
WIN = 64
PER = 4
NI = NG // PER
LATE = 2
assert NI == NT and NI * PER == NG
SW = 512
NSW = -(-(N + WIN) // SW)
ACCW = NSW * SW
NB = 7
BR = NET // NB
FULLR = NE // P
RESTE = NE - FULLR * P
HR = NE // P
HT = NET // HC
NJ = (N + EX * (P - 1)) // P
UN = 4
WC = 4
WI = EX * KH // WC
assert NJ % UN == 0
EPS = 1e-5
FAR = 100000.0
GS = 2048.0
GC = 7
PS = 1024.0


class Chain:

    def __init__(self, eng, sem):
        self.eng, self.sem, self.base, self.k = eng, sem, 0, 0

    def __call__(self, ins):
        ins.then_inc(self.sem, 1)
        self.k += 1
        self.eng.wait_ge(self.sem, self.base + self.k)

    def at(self, base):
        self.base, self.k = base, 0

    def count(self):
        return self.base + self.k


def build(nc, x, src, dst, gnn_w1, gnn_w2, gnn_b, w1, b1, wg, bg, wd, bd, out):
    ctx = ExitStack()
    with ctx:
        ctx.enter_context(nc.allow_non_contiguous_dma("small transposed bias loads"))

        def sb(name, shape, dt=F32):
            return ctx.enter_context(nc.sbuf_tensor(name, shape, dt))

        def bank(name):
            return ctx.enter_context(nc.psum_tensor(name, [P, 512], F32))

        def sem(name):
            return ctx.enter_context(nc.semaphore(name))

        g_dram = nc.dram_tensor("g_scratch", (NT * P, 2 * D), F16, kind="Internal").ap()
        tok_dram = nc.dram_tensor("tok_scratch", (NT * P, 2 * D), F32, kind="Internal").ap()

        accT = sb("accT", [P, KD, ACCW])
        big = sb("big", [P, EX * KH * D])
        wd_sb = big[:, :].rearrange("p (e c n) -> p (e c) n", e=EX, c=KH)
        xs = big[:, 0:NT * D].rearrange("p (t d) -> p t d", d=D)
        slow_oh = big[:, 0:ET * SW // 2].bitcast(F16).rearrange("p (j w) -> p j w", j=ET)
        slow_iota = big[:, ET * SW:ET * SW + SW]
        SO = NT * D
        hist_i = big[:, SO:SO + NET].bitcast(I32)
        part_i = big[:, SO + NET:SO + 2 * NET].bitcast(I32)
        hist_lo = big[:, SO + 2 * NET:SO + 2 * NET + NET // 2].bitcast(BF16)
        hist_hi = big[:, SO + 3 * NET:SO + 3 * NET + NET // 2].bitcast(BF16)
        WORK = PER * ET * D + 2 * KH * P
        arena = sb("arena", [P, WORK + KD * HID + 2 * KD * D + 2 * KD * P])
        work = arena[:, 0:WORK]
        rows = work[:, 0:PER * ET * D].rearrange("p (s d) -> p s d", s=PER)
        rows_h = rows.bitcast(F16)
        gout = work[:, 0:3 * GC * D].bitcast(F16).rearrange("p (r t a d) -> p r t a d", r=3, t=GC, a=2)
        hT = work[:, PER * ET * D:PER * ET * D + KH * P].rearrange("p (c n) -> p c n", c=KH)
        hT_last = work[:, PER * ET * D + KH * P:].rearrange("p (c n) -> p c n", c=KH)
        wtmp = work[:, PER * ET * D + KH * P:]
        wtmp_h = wtmp.bitcast(F16).rearrange("p (c a n) -> p c a n", c=WC, a=2)
        hs = work[:, PER * ET * D:].bitcast(F16).rearrange("p (b a n) -> p b a n", b=2, a=2)
        w1_sb = arena[:, WORK:WORK + KD * HID].rearrange("p (k n) -> p k n", k=KD)
        AT = WORK + KD * HID
        gw_sb = arena[:, AT:AT + 2 * KD * D].rearrange("p (k n) -> p k n", k=2 * KD)
        gw_flat = arena[:, AT:AT + 2 * KD * D]
        AT += 2 * KD * D
        xT = arena[:, AT:AT + 2 * KD * P].rearrange("p (b k n) -> p b k n", b=2, k=KD)
        gb_sb = sb("gb_sb", [P, D])
        b1_sb = sb("b1_sb", [P, KH])
        wg_sb = sb("wg_sb", [P, KH, EX])
        bg_sb = sb("bg_sb", [P, EX])
        src_idx = sb("src_idx", [P, NET], I32)
        dstf = sb("dstf", [P, NET + ET])
        cnt_row = sb("cnt_row", [1, ACCW], BF16)
        cnt_t = sb("cnt_t", [1, P])
        rel = sb("rel", [P, NET + ET])
        acc0 = accT[:, 0, :]
        acc1 = accT[:, 1, :]
        nat = lambda k: work[0:BR, k * NB * P:(k + 1) * NB * P]
        nat_i = [nat(k).bitcast(I32).rearrange("p (b c) -> p b c", b=NB) for k in (0, 1)]
        nat_f = [nat(2 + k).rearrange("p (b c) -> p b c", b=NB) for k in (0, 1)]
        bins_lo = accT[:, :, :].rearrange("p h w -> p (h w)")[:, 0:NLO * HT // 2].bitcast(BF16)\
            .rearrange("p (b t) -> p b t", t=HT)
        bins_hi = arena[:, 0:2 * (NHI * HT // 2)].bitcast(BF16).rearrange("p (s b t) -> p s b t", s=2, t=HT)
        viol = big[:, SO:SO + NET]
        viol2 = big[:, SO + NET:SO + 2 * NET]

        ident = sb("ident", [P, P])
        ones = sb("ones", [P, P])
        row0 = sb("row0", [P, P])
        upper = sb("upper", [P, P], BF16)
        ones_h = sb("ones_h", [P, P], BF16)
        iota_i = sb("iota_i", [P, SW], I32)
        iota_f = sb("iota_f", [P, P])
        lo_c = sb("lo_c", [P, HT], BF16)
        hi_c = sb("hi_c", [P, HT], BF16)
        lim_i = sb("lim_i", [P, NG], I32)
        limf = sb("limf", [P, NG])
        basef = sb("basef", [P, NG])
        base_i = sb("base_i", [1, NG], I32)
        flag_i = sb("flag_i", [1, 1], I32)
        small = sb("small", [P, 8])
        idx = sb("idx", [P, PER, ET], I32)
        ones_f = sb("ones_f", [P, 1], F16)
        woh = sb("woh", [P, 2, ET, WIN], F16)
        ssum = sb("ssum", [P, NT])
        nmean = sb("nmean", [P, NT])
        ssq = sb("ssq", [P, NT])
        rstd = sb("rstd", [P, NT])
        nb = sb("nb", [P, NT])
        deg = sb("deg", [P, NT])
        reffs = sb("reffs", [P, NT])
        rs = sb("rs", [P, NT])
        gsc = sb("gsc", [P, NT])
        usc = sb("usc", [P, NT])
        usb = sb("usb", [P, NT])

        xin = sb("xin", [P, D])
        fu = sb("fu", [P, 2, D])
        lT = sb("lT", [P, 2 * KD, P])
        emb = sb("emb", [P, D])
        emb2 = sb("emb2", [P, D])
        sqj = sb("sqj", [P, D])
        xcat = sb("xcat", [P, 2 * D])
        junk = [xin[:, :], emb[:, :], emb2[:, :], sqj[:, :]]
        NJUNK = len(junk)
        reff = sb("reff", [P, 1])
        ss = sb("ss", [P, 1])
        rn = sb("rn", [P, 1])
        nrm = sb("nrm", [P, 1])
        sd = sb("sd", [P, 1])
        eps_t = sb("eps_t", [P, 1])
        st6 = sb("st6", [P, 6])
        mv = sb("mv", [P, 2])
        rstd2 = sb("rstd2", [P, 1])
        logits = sb("logits", [P, NT, EX])
        lgT = sb("lgT", [EX, P])

        wmax = sb("wmax", [P, WI])
        wsum = sb("wsum", [P, 4])
        bound = sb("bound", [P, 4])
        pow2 = sb("pow2", [P, 4])
        scale = sb("scale", [P, 4])
        inv = sb("inv", [P, 2])
        ident_h = sb("ident_h", [P, P], F16)
        bd_sb = acc1[:, 0:EX * D]
        w1h = acc1[:, EX * D:EX * D + KD * HID].bitcast(F16).rearrange("p (a k n) -> p a k n", a=2, k=KD)
        hf = acc1[:, EX * D + KD * HID:EX * D + KD * HID + 2 * KH * P].rearrange("p (b n) -> p b n", b=2)
        bigh = big[:, :].bitcast(F16)
        xTh = xT[:, :, :, :].rearrange("p b k n -> p b (k n)").bitcast(F16)\
            .rearrange("p b (q n) -> p b q n", q=2 * KD)
        LE = NT * EX
        carved = [0]

        def carve(n, dt=F32):
            at = carved[0]
            carved[0] += n
            assert carved[0] <= ACCW
            return acc0[:, at:at + n] if dt == F32 else acc0[:, at:at + n].bitcast(dt)

        te_view = lambda a: a.rearrange("p (t e) -> p t e", e=EX)
        et_view = lambda a: a.rearrange("p (e t) -> p e t", e=EX)
        ra, rb, oneh = te_view(carve(LE)), te_view(carve(LE)), te_view(carve(LE))
        oneh_h = sb("oneh_h", [P, NT, EX], BF16)
        tot, cum, keep = et_view(carve(LE)), et_view(carve(LE)), et_view(carve(LE))
        mx, prob, pos, plo, phi, valid = (carve(NT) for _ in range(6))
        pos_i, plo_i = carve(NT, I32), carve(NT, I32)
        tid_i = sb("tid_i", [P, NT], I32)
        tid = sb("tid", [P, NT])
        vals = sb("vals", [P, NT, 4], F16)
        rank8_i = sb("rank8_i", [P, EX], I32)
        rank8 = sb("rank8", [P, EX])
        te, tinc, tstart = carve(EX), carve(EX), carve(EX)
        te_i = carve(EX, I32)
        one8 = sb("one8", [P, EX])
        zeros_h = sb("zeros_h", [P, P], BF16)
        jx = carve(NJ * EX)[0:1, :].rearrange("p (j e) -> p j e", e=EX)
        jexp = carve(NJ)[0:1, :]
        jexp_i = carve(NJ, I32)[0:1, :]
        SC = 4 * GC
        lo_oh = [carve(SC * P // 2).bitcast(F16).rearrange("p (t n) -> p t n", n=P),
                 acc1[:, EX * D + KD * HID:EX * D + KD * HID + (NT - SC) * P // 2].bitcast(F16)
                 .rearrange("p (t n) -> p t n", n=P)]
        lo_at = lambda t: (lo_oh[0], t) if t < SC else (lo_oh[1], t - SC)
        PC = 4
        hi_view = lambda a, q: a[:, q * (GC * NJ // 2):(q + 1) * (GC * NJ // 2)].bitcast(F16)\
            .rearrange("p (t j) -> p t j", t=GC)
        hi_own = carve((NT // GC - PC) * GC * NJ // 2)
        hi_oh = [hi_view(gw_flat, c) for c in range(PC)] + [hi_view(hi_own, c) for c in range(NT // GC - PC)]
        hi_val = work[:, 0:NT * 4 * NJ // 2].bitcast(F16).rearrange("p (t a j) -> p t a j", t=NT, a=4)
        slot = carve(2 * NJ).rearrange("p (a j) -> p a j", a=2)
        gidx, sidx = carve(NJ, I32), carve(NJ, I32)
        sidf = carve(NJ)
        gring = sb("gring", [P, UN], I32)
        sring = sb("sring", [P, UN], I32)
        trow = [rows[:, s, 0:2 * D] for s in range(UN)]
        trow_h = [rows_h[:, s, 2 * D:4 * D] for s in range(UN)]
        obuf = [rows[:, s, 2 * D:3 * D] for s in range(UN)]
        yb = rows[:, 0, 3 * D:4 * D]

        bkA = [bank("bkA0"), bank("bkA1")]
        bkC = bank("bkC")
        bkT = bank("bkT")
        bkE = bank("bkE")
        bkH = [bank("bkH0"), bank("bkH1")]
        bkL = bank("bkL")
        bkT2 = (bkT, bkL)
        bkY = (bkE, bkC)
        segc = [b[0:1, KD * WIN:(KD + 1) * WIN] for b in bkA]
        segp = [b[:, 0:KD * WIN].rearrange("p (h w) -> p h w", h=KD) for b in bkA]

        pads_set = sem("pads_set"); edges_in = sem("edges_in"); x_in = sem("x_in"); weights_in = sem("weights_in")
        consts = sem("consts"); pool_own = sem("pool_own"); dve_own = sem("dve_own")
        nat_ready = sem("nat_ready"); tables_t = sem("tables_t")
        centred = sem("centred")
        sums_done = sem("sums_done"); mean_ready = sem("mean_ready"); sd_x = sem("sd_x"); scales = sem("scales")
        hist_oh = sem("hist_oh"); hist_used = sem("hist_used"); hist_in = sem("hist_in")
        deg_read = sem("deg_read"); slow_own = sem("slow_own"); act_own = sem("act_own"); hist_own = sem("hist_own")
        edge_own = sem("edge_own")
        g_hi_dve = sem("g_hi_dve"); g_hi = sem("g_hi"); g_lo = sem("g_lo")
        g_stored = [sem(f"g_stored{s}") for s in range(3)]; acc_zero = sem("acc_zero")
        dst_ready = sem("dst_ready"); base_bc = sem("base_bc"); viol_ready = sem("viol_ready")
        viol_sum = sem("viol_sum")
        flag_ready = sem("flag_ready")
        slow_idx = sem("slow_idx"); slow_landed = sem("slow_landed"); slow_oh_ready = sem("slow_oh_ready")
        slow_sum = sem("slow_sum"); slow_added = sem("slow_added")
        idx_in = [sem(f"idx_in{s}") for s in range(PER)]
        landed = [sem(f"landed{s}") for s in range(PER)]
        oh_ready = sem("oh_ready"); seg_done = sem("seg_done"); seg_added = sem("seg_added")
        xt_in = sem("xt_in"); x_again = sem("x_again"); fu_ready = sem("fu_ready"); fu_t = sem("fu_t")
        l_ready = sem("l_ready")
        e_done = sem("e_done"); e_ready = sem("e_ready"); ss_ready = sem("ss_ready"); nrm_ready = sem("nrm_ready")
        var_ready = sem("var_ready"); sd_ready = sem("sd_ready"); roots = sem("roots"); x2_ready = sem("x2_ready")
        xn_ready = sem("xn_ready"); xn_t = sem("xn_t"); xt_ready = sem("xt_ready")
        h_done = [sem("h_done0"), sem("h_done1")]; gelu_done = sem("gelu_done")
        lgt_done = sem("lgt_done"); lgt_read = sem("lgt_read"); lg_done = sem("lg_done"); lg_read = sem("lg_read")
        tok_stored = sem("tok_stored"); wd_in = sem("wd_in"); bd_in = sem("bd_in")
        exp_in = sem("exp_in"); exp_done = sem("exp_done"); oneh_ready = sem("oneh_ready"); ranks = sem("ranks")
        hi_ready = sem("hi_ready"); lo_ready = sem("lo_ready"); val_pool = sem("val_pool"); val_dve = sem("val_dve")
        pm_used = sem("pm_used"); slots_ready = sem("slots_ready")
        gi_in = [sem(f"gi_in{s}") for s in range(UN)]
        si_in = [sem(f"si_in{s}") for s in range(UN)]
        tok_in = [sem(f"tok_in{s}") for s in range(UN)]
        stored = [sem(f"stored{s}") for s in range(UN)]
        t2_done = sem("t2_done"); t2_read = sem("t2_read"); h2_done = sem("h2_done"); gelu2 = sem("gelu2")
        row_ready = sem("row_ready"); norm_hi = sem("norm_hi"); max_ready = sem("max_ready"); max_sum = sem("max_sum")
        scales_set = sem("scales_set"); wd_max = sem("wd_max"); wd_split = sem("wd_split"); w1_hi = sem("w1_hi")
        w1_split = sem("w1_split"); h_hi = sem("h_hi"); h_split = sem("h_split")
        y_done = sem("y_done"); y_read = sem("y_read"); o_ready = sem("o_ready")

        ticks = sem("ticks")

        def wait_count(eng, s, value):
            eng.wait_ge(s, value)
            if not isinstance(value, int):
                eng.sem_inc(ticks, 1)

        block = ctx.enter_context(nc.Block())

        STORES = [len(range(q, NT // GC, 3)) for q in range(3)]

        SEG1 = LATE + 3
        WD0 = SEG1 + 1
        WD1 = WD0 + WI
        assert WD1 + WI < NI

        def edge_loop(eng, body, at_wd1=None):
            for i in range(SEG1):
                body(i)
            if at_wd1 is None:
                with eng.Fori(SEG1, NI) as i:
                    body(i)
            else:
                with eng.Fori(SEG1, WD1) as i:
                    body(i)
                at_wd1()
                with eng.Fori(WD1, NI) as i:
                    body(i)

        def has_gates(t):
            return not (isinstance(t, int) and t < 2)

        def times_values(eng, c):
            ts = slice(c * GC, (c + 1) * GC)
            return eng.tensor_tensor(hi_val[:, ts, :, :], hi_oh[c].unsqueeze(2).to_broadcast([P, GC, 4, NJ]),
                                     vals[:, ts, :].unsqueeze(3).to_broadcast([P, GC, 4, NJ]), ALU.mult)

        @block.sync
        def _(sp):
            sp.wait_ge(pads_set, 4)
            for k, e in enumerate((src, dst)):
                full = (NB - 1) * BR
                sp.dma_start(nat_i[k][:, 0:NB - 1, :],
                             e[0:full * P].rearrange("(b p c) -> p b c", p=BR, c=P)).then_inc(edges_in, 16)
                sp.dma_start(nat_i[k][0:FULLR - full, NB - 1, :],
                             e[full * P:FULLR * P].rearrange("(p c) -> p c", c=P)).then_inc(edges_in, 16)
                sp.dma_start(nat_i[k][FULLR - full:FULLR - full + 1, NB - 1, 0:RESTE],
                             e[FULLR * P:NE].rearrange("(p c) -> p c", p=1)).then_inc(edges_in, 16)
            sp.dma_start(hist_i[:, 0:HR], src[0:P * HR].rearrange("(p c) -> p c", p=P)).then_inc(hist_in, 16)
            sp.dma_start(hist_i[0:NE - P * HR, HR:HR + 1], src[P * HR:NE].rearrange("(p c) -> p c", c=1))\
                .then_inc(hist_in, 16)
            for c in range(6):
                sp.dma_start(xs[:, 8 * c:8 * c + 8, :],
                             x[8 * c * P:8 * (c + 1) * P, :].rearrange("(t p) d -> p t d", p=P)).then_inc(x_in, 16)
            sp.dma_start(xs[0:LASTN, NT - 1, :], x[(NT - 1) * P:N, :]).then_inc(x_in, 16)

            for c in range(7):
                sp.wait_ge(g_lo, c + 1)
                sp.dma_start(g_dram[GC * c * P:GC * (c + 1) * P, :].rearrange("(t p) d -> p t d", p=P),
                             gout[:, c % 3, :, :, :].rearrange("p t a d -> p t (a d)")).then_inc(g_stored[c % 3], 16)

            sp.wait_ge(flag_ready, 1)
            general = sp.value_load(flag_i[0:1, 0:1], min_val=0, max_val=1)
            with sp.If(general != 0):
                with sp.Fori(0, NG) as n:
                    sp.wait_ge(slow_sum, n * NSW + 1)
                    sp.dma_start(idx[:, 0, :], src_idx[:, bass.ds(n * ET, ET)]).then_inc(slow_idx, 16)
                sp.wait_ge(slow_landed, NG * ET * 16)

            for s in range(PER):
                sp.dma_start(idx[:, s, :], src_idx[:, s * ET:(s + 1) * ET]).then_inc(idx_in[s], 16)
            sp.dma_start(xin[:, :], x[0:P, :]).then_inc(xt_in, 16)
            sp.dma_start(xcat[:, 0:D], x[0:P, :]).then_inc(x_again, 16)
            for q in range(3):
                sp.wait_ge(g_stored[q], STORES[q] * 16)
            sp.wait_ge(acc_zero, 2)
            wd_chunks = wd.rearrange("e (c p) n -> p (e c) n", p=P)

            def ahead(i, last):
                t = i - LATE
                tile = not (isinstance(i, int) and t < 0)
                for s in range(PER):
                    if not last:
                        sp.wait_ge(landed[s], (i + 1) * (ET * 16))
                        sp.dma_start(idx[:, s, :], src_idx[:, bass.ds((i + 1) * (PER * ET) + s * ET, ET)])\
                          .then_inc(idx_in[s], 16)
                    if s == 0 and tile:
                        sp.wait_ge(fu_ready, t + 1)
                        sp.dma_start(xin[:, :], x[bass.ds((t + 1) * P, P), :]).then_inc(xt_in, 16)
                    if s == 1 and tile and not (isinstance(t, int) and t == 0):
                        store_row(t - 1)
                        sp.dma_start(xcat[:, 0:D], x[bass.ds(t * P, P), :]).then_inc(x_again, 16)

            def store_row(t):
                sp.wait_ge(row_ready, t + 1)
                sp.dma_start(tok_dram[bass.ds(t * P, P), :], xcat[:, :]).then_inc(tok_stored, 16)
                sp.wait_ge(tok_stored, (t + 1) * 16)

            for i in range(SEG1):
                ahead(i, False)
            with sp.Fori(SEG1, SEG1 + WI) as i:
                at = bass.ds((i - SEG1) * WC, WC)
                sp.dma_start(wd_sb[:, at, :], wd_chunks[:, at, :]).then_inc(wd_in, 16)
                ahead(i, False)
            with sp.Fori(SEG1 + WI, NI - 1) as i:
                ahead(i, False)
            ahead(NI - 1, True)
            sp.wait_ge(fu_ready, NT - 1)
            sp.dma_start(xin[0:LASTN, :], x[(NT - 1) * P:N, :]).then_inc(xt_in, 16)
            store_row(NT - 3)
            sp.dma_start(xcat[:, 0:D], x[(NT - 2) * P:(NT - 1) * P, :]).then_inc(x_again, 16)
            store_row(NT - 2)
            sp.dma_start(xcat[0:LASTN, 0:D], x[(NT - 1) * P:N, :]).then_inc(x_again, 16)
            store_row(NT - 1)

            sp.dma_start(bd_sb, bd.rearrange("e n -> (e n)").partition_broadcast(P)).then_inc(bd_in, 16)

            sp.wait_ge(slots_ready, 1)

            def rings(u, s, first):
                j = u * UN + s
                if not first:
                    sp.wait_ge(tok_in[s], u * 16)
                sp.dma_start(gring[:, s:s + 1], gidx[:, bass.ds(j, 1)]).then_inc(gi_in[s], 16)
                if not first:
                    sp.wait_ge(stored[s], u * 16)
                sp.dma_start(sring[:, s:s + 1], sidx[:, bass.ds(j, 1)]).then_inc(si_in[s], 16)

            for s in range(UN):
                rings(0, s, True)
            with sp.Fori(1, NJ // UN) as u:
                for s in range(UN):
                    rings(u, s, False)

        @block.gpsimd
        def _(pool):
            own = Chain(pool, pool_own)
            pool.memset(nat_i[0][:, NB - 1, :], -1).then_inc(pads_set, 1)
            pool.memset(nat_i[1][:, NB - 1, :], -1).then_inc(pads_set, 1)
            pool.memset(hist_i[:, HR:NET], -1).then_inc(pads_set, 1)
            pool.memset(xs[:, NT - 1, :], 0.0).then_inc(pads_set, 1)
            pool.memset(ones[:, :], 1.0).then_inc(consts, 1)
            own(pool.memset(ident[:, :], 0.0))
            pool.affine_select(out=ident[:, :], in_=ident[:, :], compare_op=ALU.not_equal, fill=1.0, base=0,
                               pattern=[[-1, P]], channel_multiplier=1).then_inc(consts, 1)
            pool.iota(iota_i[:, :], pattern=[[1, SW]], base=0, channel_multiplier=0).then_inc(consts, 1)
            own(pool.memset(row0[:, :], 0.0))
            pool.memset(row0[0:1, :], 1.0).then_inc(consts, 1)
            pool.iota(lim_i[:, :], pattern=[[P, NI], [0, PER]], base=-P * (LATE - 1), channel_multiplier=0)\
                .then_inc(consts, 1)
            pool.iota(tid_i[:, :], pattern=[[P, NT]], base=1, channel_multiplier=1).then_inc(consts, 1)
            pool.iota(rank8_i[:, :], pattern=[[-1, EX]], base=EX, channel_multiplier=0).then_inc(consts, 1)
            own(pool.memset(upper[:, :], 1.0))
            pool.affine_select(out=upper[:, :], in_=upper[:, :], compare_op=ALU.is_gt, fill=0.0, base=0,
                               pattern=[[1, P]], channel_multiplier=-1).then_inc(consts, 1)
            pool.memset(ones_h[:, :], 1.0).then_inc(consts, 1)
            pool.memset(one8[:, :], 1.0).then_inc(consts, 1)
            pool.memset(eps_t[:, :], EPS).then_inc(consts, 1)
            pool.memset(ones_f[:, :], 1.0).then_inc(consts, 1)
            pool.memset(zeros_h[:, :], 0.0).then_inc(consts, 1)
            wait_count(pool, sums_done, 1)
            pool.tensor_scalar(nmean[:, :], ssum[:, :], -1.0 / D, None, ALU.mult).then_inc(mean_ready, 1)
            pool.memset(cnt_row[:, :], 0.0)
            wait_count(pool, hist_used, HC + 1)
            pool.memset(accT[:, :, :], 0.0).then_inc(acc_zero, 1)

            wait_count(pool, flag_ready, 1)
            for q in range(3):
                wait_count(pool, g_stored[q], STORES[q] * 16)

            def gather(s, j, done):
                pool.indirect_dma_start(rows_h[:, s, j * 2 * D:(j + 1) * 2 * D], None, g_dram[:, :],
                                        bass.IndirectOffsetOnAxis(idx[:, s, j:j + 1], 0)).then_inc(done, 16)

            general = pool.value_load(flag_i[0:1, 0:1], min_val=0, max_val=1)
            with pool.If(general != 0):
                with pool.Fori(0, NG) as n:
                    wait_count(pool, slow_idx, (n + 1) * 16)
                    wait_count(pool, slow_sum, n * NSW + 1)
                    for j in range(ET):
                        gather(0, j, slow_landed)
                wait_count(pool, slow_sum, NG * NSW + 1)

            def body(i):
                for s in range(PER):
                    wait_count(pool, idx_in[s], (i + 1) * 16)
                    if not (isinstance(i, int) and i == 0):
                        wait_count(pool, seg_done, i * PER + s - (PER - 1))
                    for j in range(ET):
                        gather(s, j, landed[s])

            body(0)
            with pool.Fori(1, NI) as i:
                body(i)

            wait_count(pool, l_ready, NT)
            w1_flat = w1_sb[:, :, :].rearrange("p k n -> p (k n)")
            w1_parts = w1h.rearrange("p a k n -> p a (k n)")
            wait_count(pool, scales_set, 1)
            w1_scaled = hf.rearrange("p b n -> p (b n)")
            pool.tensor_scalar(w1_scaled, w1_flat, scale[:, 1:2], None, ALU.mult).then_inc(w1_hi, 1)
            wait_count(pool, w1_hi, 1)
            pool.tensor_copy(w1_parts[:, 0, :], w1_scaled).then_inc(w1_hi, 1)
            wait_count(pool, w1_hi, 2)
            pool.tensor_tensor(w1_parts[:, 1, :], w1_scaled, w1_parts[:, 0, :], ALU.subtract).then_inc(w1_split, 1)

            for c in range(PC):
                wait_count(pool, hi_ready, c + 1)
                times_values(pool, c).then_inc(val_pool, 1)

            wait_count(pool, tok_stored, NT * 16)

            def fetch(u, s):
                wait_count(pool, gi_in[s], (u + 1) * 16)
                pool.indirect_dma_start(trow[s], None, tok_dram[:, :],
                                        bass.IndirectOffsetOnAxis(gring[:, s:s + 1], 0)).then_inc(tok_in[s], 16)

            def scatter(u, s):
                wait_count(pool, si_in[s], (u + 1) * 16)
                wait_count(pool, o_ready, u * UN + s + 1)
                pool.indirect_dma_start(out[:, :], bass.IndirectOffsetOnAxis(sring[:, s:s + 1], 0), obuf[s], None,
                                        bounds_check=N - 1, oob_is_err=False).then_inc(stored[s], 16)

            for s in range(UN):
                fetch(0, s)
            with pool.Fori(1, NJ // UN) as u:
                for s in range(UN):
                    scatter(u - 1, s)
                    fetch(u, s)
            for s in range(UN):
                scatter(NJ // UN - 1, s)
            for s in range(UN):
                wait_count(pool, stored[s], 16 * (NJ // UN))

        @block.scalar
        def _(act):
            act.wait_ge(x_in, 7 * 16)
            def reduce_row(q, t, **how):
                if q >= NJUNK:
                    act.wait_ge(act_own, q - NJUNK + 1)
                act.activation(junk[q % NJUNK], xs[:, t, :], **how).then_inc(act_own, 1)

            for t in range(NT):
                reduce_row(t, t, func=ACT.Copy, accum_out=ssum[:, t:t + 1])
            act.wait_ge(act_own, NT)
            act.sem_inc(sums_done, 1)
            act.wait_ge(mean_ready, 1)
            for t in range(NT):
                reduce_row(NT + t, t, func=ACT.Square, bias=nmean[:, t:t + 1], accum_out=ssq[:, t:t + 1])
            act.wait_ge(act_own, 2 * NT)
            for t in range(NT):
                ins = act.activation(xs[:, t, :], xs[:, t, :], ACT.Identity, bias=nmean[:, t:t + 1])
            ins.then_inc(centred, 1)
            act.wait_ge(centred, 1)
            act.wait_ge(consts, 13)
            act.activation(ssq[:, :], ssq[:, :], ACT.Sqrt, bias=eps_t[:, :], scale=1.0 / D).then_inc(sd_x, 1)
            act.wait_ge(deg_read, 1)
            act.activation(deg[:, :], deg[:, :], ACT.Sqrt).then_inc(roots, 1)
            act.wait_ge(scales, 1)
            for c in range(NT // GC):
                if c >= 3:
                    act.wait_ge(g_stored[c % 3], 16 * (c // 3))
                for q in range(GC - 1):
                    t = c * GC + q
                    ins = act.activation(gout[:, c % 3, q, 0, :], xs[:, t, :], ACT.Copy, scale=gsc[:, t:t + 1])
                ins.then_inc(g_hi, 1)
            act.wait_ge(hist_used, HC + 1)
            for dst_t, src_t in (
                (gw_sb[:, 0:KD, :], gnn_w1.rearrange("(k p) n -> p k n", p=P)),
                (gw_sb[:, KD:2 * KD, :], gnn_w2.rearrange("(k p) n -> p k n", p=P)),
                (gb_sb[:, :], gnn_b.partition_broadcast(P)),
                (w1_sb[:, :, :], w1.rearrange("(k p) n -> p k n", p=P)),
                (b1_sb[:, :], b1.rearrange("(c p) -> p c", p=P)),
                (wg_sb[:, :, :], wg.rearrange("(c p) e -> p c e", p=P)),
                (bg_sb[:, :], bg.partition_broadcast(P)),
            ):
                act.dma_start(dst_t, src_t).then_inc(weights_in, 16)

            def tile_head(t, first=False):
                act.wait_ge(xt_in, (t + 1) * 16)
                if not first:
                    act.wait_ge(fu_t, t)
                at = bass.ds(t, 1)
                act.activation(fu[:, 0, :], xin[:, :], ACT.Identity, bias=nb[:, at], scale=rstd[:, at])
                act.activation(fu[:, 1, :], xin[:, :], ACT.Identity, bias=usb[:, at], scale=usc[:, at])\
                    .then_inc(fu_ready, 1)

            def tile_gelu(t, first, banks=bkH, out_t=hT):
                if not first and out_t is hT:
                    act.wait_ge(lgt_done, t)
                for c in range(KH):
                    b = c // 4
                    if c % 4 == 0:
                        act.wait_ge(h_done[b], t + 1)
                    ins = act.activation(out_t[:, c, :], banks[b][:, (c % 4) * P:(c % 4 + 1) * P], ACT.Gelu,
                                         bias=b1_sb[:, c:c + 1])
                ins.then_inc(gelu_done, 1)

            def tile_norms(t):
                act.wait_ge(e_ready, t + 1)
                act.activation(sqj[:, :], emb2[:, :], ACT.Square, accum_out=ss[:, :]).then_inc(ss_ready, 1)
                act.wait_ge(ss_ready, t + 1)
                act.activation(nrm[:, :], ss[:, :], ACT.Sqrt).then_inc(nrm_ready, 1)
                act.wait_ge(var_ready, t + 1)
                act.activation(sd[:, :], mv[:, 1:2], ACT.Sqrt, bias=eps_t[:, :]).then_inc(sd_ready, 1)

            def tile_xt(t):
                act.wait_ge(xn_t, t + 1)
                act.activation(xT[:, 0, :, :], bkL[:, 0:D].rearrange("p (k n) -> p k n", k=KD), ACT.Copy)\
                    .then_inc(xt_ready, 1)

            act.wait_ge(weights_in, 7 * 16)
            act.wait_ge(consts, 13)
            tile_head(0, True)

            def body(i):
                if isinstance(i, int) and i < LATE:
                    return
                t = i - LATE
                begun = not (isinstance(t, int) and t == 0)
                if begun:
                    tile_xt(t - 1)
                tile_head(t + 1)
                tile_norms(t)
                if begun:
                    tile_gelu(t - 1, isinstance(t, int) and t == 1)

            edge_loop(act, body)
            tile_xt(NT - 3)
            tile_head(NT - 1)
            tile_norms(NT - 2)
            tile_gelu(NT - 3, False)
            tile_xt(NT - 2)
            tile_norms(NT - 1)
            tile_xt(NT - 1)
            tile_gelu(NT - 2, False)
            tile_gelu(NT - 1, False, bkA, hT_last)

            act.wait_ge(exp_in, 1)
            act.activation(ra[:, :, :], ra[:, :, :], ACT.Exp).then_inc(exp_done, 1)

            def t_copy(j, s):
                act.wait_ge(t2_done, j + 1)
                act.activation(xTh[:, s % 2, :, :], bkT2[s % 2][:, :].rearrange("p (q n) -> p q n", q=2 * KD),
                               ACT.Copy).then_inc(t2_read, 1)

            def gelu_tile(j, s, first):
                for b in (0, 1):
                    hb = (bkH if s % 2 == 0 else bkA)[b]
                    act.wait_ge(h2_done, 2 * j + b + 1)
                    if not first and b == 0:
                        act.wait_ge(h_split, 2 * (j - 1))
                    for c in range(4 * b, 4 * b + 4):
                        ins = act.activation(hf[:, s % 2, c * P:(c + 1) * P], hb[:, (c % 4) * P:(c % 4 + 1) * P],
                                             ACT.Gelu, bias=b1_sb[:, c:c + 1], scale=inv[:, 0:1])
                    ins.then_inc(gelu2, 1)

            def steps(u, first, last):
                for s in range(UN):
                    if not (last and s == UN - 1):
                        t_copy(u * UN + s + 1, s + 1)
                    gelu_tile(u * UN + s, s, first and s < 2)

            act.wait_ge(scales_set, 1)
            t_copy(0, 0)
            steps(0, True, False)
            with act.Fori(1, NJ // UN - 1) as u:
                steps(u, False, False)
            steps(NJ // UN - 1, False, True)

        @block.vector
        def _(dve):
            own = Chain(dve, dve_own)
            dve.wait_ge(consts, 13)
            dve.tensor_copy(iota_f[:, :], iota_i[:, 0:P])
            dve.tensor_copy(ident_h[:, :], ident[:, :])
            dve.tensor_copy(limf[:, :], lim_i[:, :])
            dve.tensor_copy(tid[:, :], tid_i[:, :])
            dve.tensor_copy(rank8[:, :], rank8_i[:, :])
            own(dve.tensor_copy(vals[:, :, 0], tid_i[:, :]))
            dve.tensor_tensor(vals[:, :, 1], tid[:, :], vals[:, :, 0], ALU.subtract)
            dve.wait_ge(hist_in, 2 * 16)
            own(dve.tensor_scalar(part_i, hist_i, P - 1, None, ALU.bitwise_and))
            own(dve.tensor_copy(hist_lo, part_i))
            own(dve.tensor_scalar(part_i, hist_i, 7, None, ALU.arith_shift_right))
            own(dve.tensor_copy(hist_hi, part_i))
            dve.wait_ge(edges_in, 6 * 16)
            for k in (0, 1):
                dve.tensor_copy(nat_f[k], nat_i[k]).then_inc(nat_ready, 1)

            H = 4 * BR

            def table(banks, k, out_t, least):
                dve.wait_ge(tables_t, k + 1)
                dve.tensor_scalar(out_t[:, 0:H], banks[0][:, 0:H], least, None, ALU.max)
                own(dve.tensor_scalar(out_t[:, H:NET], banks[1][:, 0:NET - H], least, None, ALU.max))

            table((bkT, bkE), 0, src_idx, 0.0)
            table(bkH, 1, dstf, -1.0)
            dve.memset(rel[:, NET:NET + ET], -FAR)
            dve.sem_inc(dst_ready, 1)

            dve.wait_ge(base_bc, 1)
            own(dve.tensor_copy(basef[:, :], bkL[:, 0:NG]))
            dve.tensor_copy(base_i[:, :], basef[0:1, :])

            chunk_own = Chain(dve, hist_own)
            HIST_OWN = 6
            def hist_chunk(c, half):
                chunk_own.at(c * HIST_OWN)
                chunk_own(dve.tensor_copy(lo_c[:, :], hist_lo[:, bass.ds(c * HT, HT)]))
                chunk_own(dve.tensor_copy(hi_c[:, :], hist_hi[:, bass.ds(c * HT, HT)]))
                for q in range(NHI):
                    dve.tensor_scalar(bins_hi[:, half, q, :], hi_c[:, :], float(q), None, ALU.is_equal)
                dve.wait_ge(hist_used, c + 1)
                for q in range(NLO):
                    ins = dve.tensor_scalar(bins_lo[:, q, :], lo_c[:, :], float(q), None, ALU.is_equal)
                ins.then_inc(hist_oh, 1)
                at, d = bass.ds(c * HT, HT), dstf[:, bass.ds(c * HT, HT)]
                rc, v, v2 = rel[:, at], viol[:, at], viol2[:, at]
                chunk_own(dve.tensor_tensor(rc.rearrange("p (n j) -> p n j", j=ET),
                                            d.rearrange("p (n j) -> p n j", j=ET),
                                            basef[:, bass.ds(c * (HT // ET), HT // ET)].unsqueeze(2)
                                            .to_broadcast([P, HT // ET, ET]), ALU.subtract))
                chunk_own(dve.tensor_scalar(v, rc, 0.0, None, ALU.is_lt))
                chunk_own(dve.scalar_tensor_tensor(v2, rc, float(WIN), v, ALU.is_ge, ALU.add))
                chunk_own(dve.scalar_tensor_tensor(v, d, 0.0, v2, ALU.is_ge, ALU.mult))
                assert chunk_own.k == HIST_OWN

            with dve.Fori(0, HC // 2) as c:
                hist_chunk(2 * c, 0)
                hist_chunk(2 * c + 1, 1)

            dve.tensor_tensor(viol2[:, 0:NG], basef[:, :], limf[:, :], ALU.is_lt)
            own(dve.tensor_reduce(small[:, 0:1], viol, AX.X, ALU.add))
            dve.wait_ge(hist_used, HC + 1)
            own(dve.tensor_scalar(deg[:, :], bkC[:, 0:NT], 1.0, None, ALU.max))
            dve.sem_inc(deg_read, 1)
            dve.wait_ge(sd_x, 1)
            dve.wait_ge(roots, 1)
            dve.reciprocal(rs[:, :], deg[:, :])
            own(dve.reciprocal(rstd[:, :], ssq[:, :]))
            own(dve.tensor_tensor(gsc[:, :], rs[:, :], rstd[:, :], ALU.mult))
            own(dve.tensor_scalar(gsc[:, :], gsc[:, :], GS, None, ALU.mult))
            dve.sem_inc(scales, 1)
            dve.tensor_tensor(nb[:, :], nmean[:, :], rstd[:, :], ALU.mult)
            own(dve.tensor_scalar(deg[:, :], deg[:, :], GS, None, ALU.mult))
            dve.tensor_tensor(usc[:, :], rstd[:, :], deg[:, :], ALU.mult)
            dve.tensor_tensor(usb[:, :], nb[:, :], deg[:, :], ALU.mult)
            dve.tensor_scalar(reffs[:, :], rs[:, :], 1.0 / GS, None, ALU.mult)
            own(dve.tensor_reduce(small[:, 1:2], viol2[:, 0:NG], AX.X, ALU.add))
            dve.tensor_tensor(small[:, 2:3], small[:, 0:1], small[:, 1:2], ALU.add).then_inc(viol_ready, 1)
            dve.wait_ge(centred, 1)
            for c in range(NT // GC):
                if c >= 3:
                    dve.wait_ge(g_stored[c % 3], 16 * (c // 3))
                t = c * GC + GC - 1
                dve.tensor_scalar(gout[:, c % 3, GC - 1, 0, :], xs[:, t, :], gsc[:, t:t + 1], None, ALU.mult)\
                    .then_inc(g_hi_dve, 1)
                dve.wait_ge(g_hi, c + 1)
                dve.wait_ge(g_hi_dve, c + 1)
                for q in range(GC):
                    t = c * GC + q
                    ins = dve.scalar_tensor_tensor(gout[:, c % 3, q, 1, :], xs[:, t, :], gsc[:, t:t + 1],
                                                   gout[:, c % 3, q, 0, :], ALU.mult, ALU.subtract)
                ins.then_inc(g_lo, 1)

            dve.wait_ge(viol_sum, 1)
            own(dve.tensor_scalar(small[:, 3:4], bkL[:, 256:257], 1.0, None, ALU.min))
            own(dve.tensor_scalar(small[:, 4:5], small[:, 3:4], -FAR, None, ALU.mult))
            dve.tensor_copy(flag_i[:, :], small[0:1, 3:4])
            own(dve.tensor_scalar(rel[:, 0:NET], rel[:, 0:NET], small[:, 4:5], None, ALU.add))
            dve.sem_inc(flag_ready, 1)
            dve.wait_ge(acc_zero, 1)

            general = dve.value_load(flag_i[0:1, 0:1], min_val=0, max_val=1)
            for q in range(3):
                dve.wait_ge(g_stored[q], STORES[q] * 16)
            with dve.If(general != 0):
                dve.tensor_copy(slow_iota, iota_i[:, :]).then_inc(slow_added, 1)
                slow = Chain(dve, slow_own)
                SLOW_OWN = 4
                with dve.Fori(0, NG) as n:
                    with dve.Fori(0, NSW) as w:
                        slow.at((n * NSW + w) * SLOW_OWN)
                        slow(dve.tensor_copy(small[:, 1:2], iota_i[:, bass.ds(w, 1)]))
                        slow(dve.tensor_scalar(small[:, 1:2], small[:, 1:2], -float(SW), None, ALU.mult))
                        slow(dve.tensor_scalar(small[:, 4:8], dstf[:, bass.ds(n * ET, ET)], small[:, 1:2], None,
                                               ALU.add))
                        for j in range(ET):
                            ins = dve.tensor_scalar(slow_oh[:, j, :], slow_iota, small[:, 4 + j:5 + j], None,
                                                    ALU.is_equal)
                        ins.then_inc(slow_oh_ready, 1)
                        dve.wait_ge(slow_sum, n * NSW + w + 2)
                        for h in range(KD):
                            a = accT[:, h, bass.ds(w * SW, SW)]
                            ins = dve.tensor_tensor(a, bkA[h][:, :], a, ALU.add)
                        a = cnt_row[:, bass.ds(w * SW, SW)]
                        slow(dve.tensor_tensor(a, bkC[0:1, :], a, ALU.add))
                        dve.sem_inc(slow_added, 1)
                        assert slow.k == SLOW_OWN
            dve.sem_inc(acc_zero, 1)

            def windows(n, slot2):
                dve.tensor_tensor(woh[:, slot2, :, :], iota_f[:, 0:WIN].unsqueeze(1).to_broadcast([P, ET, WIN]),
                                  rel[:, bass.ds(n * ET, ET)].unsqueeze(2).to_broadcast([P, ET, WIN]),
                                  ALU.is_equal).then_inc(oh_ready, 1)

            def accumulate(n, s):
                base = dve.value_load(base_i[0:1, bass.ds(n, 1)], min_val=0, max_val=N - 1)
                a = accT[:, :, bass.ds(base, WIN)]
                c = cnt_row[:, bass.ds(base, WIN)]
                dve.wait_ge(seg_done, n + 1)
                dve.tensor_tensor(a, segp[s % 2], a, ALU.add)
                loop_own(dve.tensor_tensor(c, segc[s % 2], c, ALU.add))
                dve.sem_inc(seg_added, 1)

            loop_own = Chain(dve, edge_own)

            def left_operands(t, first):
                if not first:
                    dve.wait_ge(e_done, t)
                dve.tensor_copy(cnt_t[:, :], cnt_row[:, bass.ds(t * P, P)])
                dve.wait_ge(fu_t, t + 1)
                g = accT[:, :, bass.ds(t * P, P)]
                fT = bkT[:, 0:D].rearrange("p (k n) -> p k n", k=KD)
                uT = bkT[:, D:2 * D].rearrange("p (k n) -> p k n", k=KD)
                dve.tensor_tensor(lT[:, 0:KD, :], uT, g, ALU.add)
                dve.tensor_tensor(lT[:, KD:2 * KD, :], fT, g, ALU.mult).then_inc(l_ready, 1)
                dve.wait_ge(l_ready, t + 1)

            def embedding(t, first):
                dve.wait_ge(e_done, t + 1)
                loop_own(dve.tensor_scalar(reff[:, :], bkE[:, D:D + 1], 0.5, reffs[:, bass.ds(t, 1)], ALU.is_gt,
                                           ALU.mult))
                loop_own(dve.scalar_tensor_tensor(emb[:, :], bkE[:, 0:D], reff[:, :], gb_sb[:, :], ALU.mult, ALU.add))
                if not first:
                    dve.wait_ge(xn_t, t)
                dve.scalar_tensor_tensor(emb2[:, :], emb[:, :], 0.01, emb[:, :], ALU.mult, ALU.max)\
                    .then_inc(e_ready, 1)

            def tile_norm(t):
                dve.wait_ge(nrm_ready, t + 1)
                loop_own(dve.tensor_scalar(rn[:, :], nrm[:, :], 1e-12, None, ALU.max))
                loop_own(dve.reciprocal(rn[:, :], rn[:, :]))
                dve.wait_ge(x_again, (t + 1) * 16)
                x2 = xcat[:, 0:D]
                dve.scalar_tensor_tensor(x2, emb2[:, :], rn[:, :], x2, ALU.mult, ALU.add).then_inc(x2_ready, 1)
                dve.wait_ge(x2_ready, t + 1)
                loop_own(dve.bn_stats(st6[:, :], x2))
                dve.sem_inc(ticks, 1)
                dve.bn_aggr(mv[:, :], st6[:, :]).then_inc(var_ready, 1)
                dve.wait_ge(sd_ready, t + 1)
                loop_own(dve.reciprocal(rstd2[:, :], sd[:, :]))
                xn, parts = emb2[:, :], xcat[:, D:2 * D].bitcast(F16)
                dve.tensor_scalar(xn, x2, mv[:, 0:1], rstd2[:, :], ALU.subtract, ALU.mult).then_inc(xn_ready, 1)
                dve.wait_ge(xn_ready, t + 1)
                dve.tensor_scalar(parts[:, 0:D], xn, GS, None, ALU.mult).then_inc(norm_hi, 1)
                dve.wait_ge(norm_hi, t + 1)
                dve.scalar_tensor_tensor(parts[:, D:2 * D], xn, GS, parts[:, 0:D], ALU.mult, ALU.subtract)\
                    .then_inc(row_ready, 1)

            def take_transposed(t):
                dve.wait_ge(lgt_done, t + 1)
                dve.tensor_copy(lgT[:, :], bkC[0:EX, 0:P]).then_inc(lgt_read, 1)

            def take_logits(t):
                dve.wait_ge(lg_done, t + 1)
                dve.tensor_tensor(logits[:, bass.ds(t, 1), :], bkC[:, P:P + EX].unsqueeze(1), bg_sb[:, :].unsqueeze(1),
                                  ALU.add).then_inc(lg_read, 1)

            OWN_EDGE, OWN_TILE = PER, 6

            def body(i, extra=None):
                tile = not (isinstance(i, int) and i < LATE)
                loop_own.at(i * OWN_EDGE + (i - LATE) * OWN_TILE if tile else i * OWN_EDGE)
                for s in range(PER):
                    n = i * PER + s
                    if not (isinstance(i, int) and n == 0):
                        dve.wait_ge(seg_done, n)
                    windows(n + 1, (s + 1) % 2)
                    accumulate(n, s)
                    t, first = i - LATE, isinstance(i, int) and i == LATE
                    if tile and s == 0:
                        left_operands(t, first)
                    elif tile and s == 1:
                        if extra is not None:
                            extra(i)
                        embedding(t, first)
                    elif tile and s == 2:
                        if has_gates(t):
                            take_transposed(t - 2)
                        tile_norm(t)
                    elif tile and has_gates(t):
                        take_logits(t - 2)
                assert loop_own.k == OWN_EDGE + (OWN_TILE if tile else 0)

            def wd_max_piece(i):
                dve.wait_ge(wd_in, (i - WD0 + 1) * 16)
                dve.tensor_reduce(wmax[:, bass.ds(i - WD0, 1)], big[:, bass.ds((i - WD0) * (WC * D), WC * D)],
                                  AX.X, ALU.max, apply_absolute_value=True).then_inc(wd_max, 1)

            def set_scales():
                dve.wait_ge(wd_max, WI)
                dve.tensor_reduce(wsum[:, 0:1], wmax[:, :], AX.X, ALU.max)
                dve.tensor_reduce(wsum[:, 1:2], w1_sb[:, :, :].rearrange("p k n -> p (k n)"), AX.X, ALU.max,
                                  apply_absolute_value=True)
                dve.tensor_reduce(wsum[:, 2:3], b1_sb[:, :], AX.X, ALU.max, apply_absolute_value=True)\
                    .then_inc(max_ready, 1)
                dve.wait_ge(max_sum, 1)
                own(dve.tensor_scalar(bound[:, 0:3], bkT[:, 0:3], 1e-30, None, ALU.max))
                own(dve.scalar_tensor_tensor(bound[:, 3:4], bound[:, 1:2], float(D), bound[:, 2:3], ALU.mult, ALU.add))
                own(dve.tensor_scalar(pow2[:, :].bitcast(I32), bound[:, :].bitcast(I32), 0x7F800000, None,
                                      ALU.bitwise_and))
                own(dve.reciprocal(scale[:, :], pow2[:, :]))
                own(dve.tensor_scalar(scale[:, :], scale[:, :], 2.0 ** 14, None, ALU.mult))
                dve.tensor_scalar(inv[:, 0:1], pow2[:, 1:2], 2.0 ** -14 / GS, None, ALU.mult)
                own(dve.tensor_scalar(inv[:, 1:2], pow2[:, 0:1], 2.0 ** -28, None, ALU.mult))
                own(dve.tensor_scalar(inv[:, 1:2], inv[:, 1:2], pow2[:, 3:4], None, ALU.mult))
                dve.sem_inc(scales_set, 1)

            wd_own = Chain(dve, wd_split)
            WD_OWN = 3

            def wd_split_piece(i):
                q = i - WD1
                piece = big[:, bass.ds(q * (WC * D), WC * D)]
                rows4 = piece.rearrange("p (c n) -> p c n", c=WC)
                wd_own.at(q * WD_OWN)
                wd_own(dve.tensor_scalar(wtmp_h[:, :, 0, :], rows4, scale[:, 0:1], None, ALU.mult))
                wd_own(dve.scalar_tensor_tensor(wtmp_h[:, :, 1, :], rows4, scale[:, 0:1], wtmp_h[:, :, 0, :], ALU.mult,
                                                ALU.subtract))
                dve.sem_inc(ticks, 1)
                wd_own(dve.tensor_copy(piece, wtmp))

            windows(0, 0)
            for i in range(WD0):
                body(i)
            with dve.Fori(WD0, WD1) as i:
                body(i, wd_max_piece)
            set_scales()
            with dve.Fori(WD1, WD1 + WI) as i:
                body(i, wd_split_piece)
            with dve.Fori(WD1 + WI, NI) as i:
                body(i)
            loop_own.at(NI * OWN_EDGE + (NI - LATE) * OWN_TILE)
            left_operands(NT - 2, False)
            embedding(NT - 2, False)
            left_operands(NT - 1, False)
            take_transposed(NT - 4)
            take_logits(NT - 4)
            tile_norm(NT - 2)
            embedding(NT - 1, False)
            take_transposed(NT - 3)
            take_logits(NT - 3)
            tile_norm(NT - 1)
            for t in (NT - 2, NT - 1):
                take_transposed(t)
                take_logits(t)
            dve.wait_ge(lg_read, NT)

            r = loop_own
            by_e = lambda a: a[:, :].unsqueeze(2).to_broadcast([P, NT, EX])
            by_t = lambda a: a[:, :].unsqueeze(1).to_broadcast([P, NT, EX])
            dve.memset(keep[:, :, 1:NT], 1.0)
            dve.memset(keep[:, :, 0:1], 0.0)
            r(dve.tensor_reduce(mx[:, :], logits[:, :, :], AX.X, ALU.max))
            dve.tensor_tensor(ra[:, :, :], logits[:, :, :], by_e(mx), ALU.subtract).then_inc(exp_in, 1)
            dve.wait_ge(exp_done, 1)
            r(dve.tensor_reduce(mx[:, :], ra[:, :, :], AX.X, ALU.add))
            r(dve.reciprocal(prob[:, :], mx[:, :]))
            r(dve.tensor_scalar(vals[:, :, 2], prob[:, :], PS, None, ALU.mult))
            dve.scalar_tensor_tensor(vals[:, :, 3], prob[:, :], PS, vals[:, :, 2], ALU.mult, ALU.subtract)
            r(dve.tensor_scalar(rb[:, :, :], ra[:, :, :], 1.0, None, ALU.is_ge))
            r(dve.tensor_tensor(rb[:, :, :], rb[:, :, :], by_t(rank8), ALU.mult))
            r(dve.tensor_reduce(mx[:, :], rb[:, :, :], AX.X, ALU.max))
            r(dve.tensor_tensor(oneh[:, :, :], by_e(mx), by_t(rank8), ALU.is_equal))
            r(dve.tensor_scalar(valid[:, :], tid[:, :], float(N), None, ALU.is_le))
            r(dve.tensor_tensor(oneh[:, :, :], oneh[:, :, :], by_e(valid), ALU.mult))
            dve.tensor_copy(oneh_h[:, :, :], oneh[:, :, :]).then_inc(oneh_ready, 1)
            dve.wait_ge(ranks, 1)
            r(dve.tensor_copy(tot[:, :, :], bkE[:, 0:LE].rearrange("p (t e) -> p e t", e=EX)))
            r(dve.tensor_tensor_scan(cum[:, :, :].rearrange("p e t -> p (e t)"),
                                     keep[:, :, :].rearrange("p e t -> p (e t)"),
                                     tot[:, :, :].rearrange("p e t -> p (e t)"), 0.0, ALU.mult, ALU.add))
            r(dve.tensor_scalar(te[:, :], cum[:, :, NT - 1], float(P - 1), None, ALU.add))
            r(dve.tensor_copy(te_i[:, :], te[:, :]))
            r(dve.tensor_scalar(te_i[:, :], te_i[:, :], 7, None, ALU.arith_shift_right))
            r(dve.tensor_copy(te[:, :], te_i[:, :]))
            r(dve.tensor_tensor_scan(tinc[:, :], one8[:, :], te[:, :], 0.0, ALU.mult, ALU.add))
            r(dve.tensor_tensor(tstart[:, :], tinc[:, :], te[:, :], ALU.subtract))
            r(dve.tensor_scalar(tstart[:, :], tstart[:, :], float(P), None, ALU.mult))
            r(dve.tensor_tensor(cum[:, :, :], cum[:, :, :], tot[:, :, :], ALU.subtract))
            r(dve.tensor_tensor(cum[:, :, :], cum[:, :, :], tstart[:, :].unsqueeze(2).to_broadcast([P, EX, NT]),
                                ALU.add))
            r(dve.tensor_tensor(rb[:, :, :], bkT[:, 0:LE].rearrange("p (t e) -> p t e", e=EX),
                                cum[:, :, :].rearrange("p e t -> p t e"), ALU.add))
            r(dve.tensor_tensor(rb[:, :, :], rb[:, :, :], oneh[:, :, :], ALU.mult))
            r(dve.tensor_reduce(pos[:, :], rb[:, :, :], AX.X, ALU.add))
            r(dve.tensor_scalar(valid[:, :], valid[:, :], -1.0, FAR, ALU.add, ALU.mult))
            r(dve.tensor_tensor(pos[:, :], pos[:, :], valid[:, :], ALU.add))
            r(dve.tensor_copy(pos_i[:, :], pos[:, :]))
            dve.tensor_scalar(plo_i[:, :], pos_i[:, :], P - 1, None, ALU.bitwise_and)
            r(dve.tensor_scalar(pos_i[:, :], pos_i[:, :], 7, None, ALU.arith_shift_right))
            dve.tensor_copy(plo[:, :], plo_i[:, :])
            r(dve.tensor_copy(phi[:, :], pos_i[:, :]))
            def high_bits(c):
                return dve.tensor_tensor(hi_oh[c], iota_f[:, 0:NJ].unsqueeze(1).to_broadcast([P, GC, NJ]),
                                         phi[:, c * GC:(c + 1) * GC].unsqueeze(2).to_broadcast([P, GC, NJ]),
                                         ALU.is_equal)

            for c in range(PC):
                high_bits(c).then_inc(hi_ready, 1)
            for c in range(NT // GC):
                part, at = lo_at(c * GC)
                if c * GC == SC:
                    dve.wait_ge(w1_split, 1)
                dve.tensor_tensor(part[:, at:at + GC, :], iota_f[:, :].unsqueeze(1).to_broadcast([P, GC, P]),
                                  plo[:, c * GC:(c + 1) * GC].unsqueeze(2).to_broadcast([P, GC, P]), ALU.is_equal)\
                    .then_inc(lo_ready, 1)
            for c in range(PC, NT // GC):
                r(high_bits(c))
                times_values(dve, c).then_inc(val_dve, 1)
            iota_j = iota_f[0:1, 0:NJ].unsqueeze(2).to_broadcast([1, NJ, EX])
            r(dve.tensor_tensor(jx[:, :, :], iota_j, tinc[0:1, :].unsqueeze(1).to_broadcast([1, NJ, EX]), ALU.is_ge))
            r(dve.tensor_reduce(jexp[:, :], jx[:, :, :], AX.X, ALU.add))
            r(dve.tensor_scalar(jexp[:, :], jexp[:, :], float(EX - 1), None, ALU.min))
            r(dve.tensor_copy(jexp_i[:, :], jexp[:, :]))
            dve.wait_ge(pm_used, 1)
            parts = bkC[:, 0:4 * NJ].rearrange("p (a h j) -> p a h j", a=2, h=2)
            r(dve.tensor_copy(slot[:, :, :], parts[:, :, 0, :]))
            r(dve.tensor_tensor(slot[:, :, :], slot[:, :, :], parts[:, :, 1, :], ALU.add))
            dve.tensor_scalar(slot[:, 1, :], slot[:, 1, :], 1.0 / PS, None, ALU.mult)
            r(dve.tensor_scalar(gidx[:, :], slot[:, 0, :], -1.0, 0.0, ALU.add, ALU.max))
            r(dve.tensor_scalar(sidf[:, :], slot[:, 0, :], 0.5, float(2 * N), ALU.is_lt, ALU.mult))
            r(dve.scalar_tensor_tensor(sidf[:, :], slot[:, 0, :], -1.0, sidf[:, :], ALU.add, ALU.add))
            r(dve.tensor_copy(sidx[:, :], sidf[:, :]))
            dve.sem_inc(slots_ready, 1)

            dve.wait_ge(bd_in, 16)

            def split(u, s, first):
                j = u * UN + s
                for b in (0, 1):
                    half = slice(b * (KH * P // 2), (b + 1) * (KH * P // 2))
                    hi, lo = hs[:, s % 2, 0, half], hs[:, s % 2, 1, half]
                    dve.wait_ge(gelu2, 2 * j + b + 1)
                    if not first and b == 0:
                        dve.wait_ge(y_done, j - 1)
                    dve.tensor_scalar(hi, hf[:, s % 2, half], scale[:, 3:4], None, ALU.mult).then_inc(h_hi, 1)
                    dve.wait_ge(h_hi, 2 * j + b + 1)
                    dve.scalar_tensor_tensor(lo, hf[:, s % 2, half], scale[:, 3:4], hi, ALU.mult, ALU.subtract)\
                        .then_inc(h_split, 1)

            def finish(u, s):
                j = u * UN + s
                e = dve.value_load(jexp_i[0:1, bass.ds(j, 1)], min_val=0, max_val=EX - 1)
                dve.wait_ge(y_done, j + 1)
                if not (isinstance(j, int) and j == 0):
                    dve.wait_ge(o_ready, j)
                dve.scalar_tensor_tensor(yb, bkY[s % 2][:, 0:D], inv[:, 1:2], bd_sb[:, bass.ds(e * D, D)], ALU.mult,
                                         ALU.add).then_inc(y_read, 1)
                dve.wait_ge(y_read, j + 1)
                if not (isinstance(u, int) and u == 0):
                    dve.wait_ge(stored[s], u * 16)
                dve.scalar_tensor_tensor(obuf[s], yb, slot[:, 1, bass.ds(j, 1)], trow[s][:, 0:D], ALU.mult, ALU.add)\
                    .then_inc(o_ready, 1)

            def steps(u, first):
                for s in range(UN):
                    split(u, s, first and s < 2)
                    if s:
                        finish(u, s - 1)
                    elif not first:
                        finish(u - 1, UN - 1)

            steps(0, True)
            steps(1, False)
            with dve.Fori(2, NJ // UN) as u:
                steps(u, False)
            finish(NJ // UN - 1, UN - 1)

        @block.tensor
        def _(pe):
            mm, tr = pe.matmul, pe.transpose
            pe.wait_ge(consts, 13)
            for k, banks in enumerate(((bkT, bkE), bkH)):
                pe.wait_ge(nat_ready, k + 1)
                for b in range(NB):
                    o = banks[b // 4][:, (b % 4) * BR:(b % 4 + 1) * BR]
                    ins = tr(o, nat_f[k][:, b, :], ident[0:BR, 0:BR])
                ins.then_inc(tables_t, 1)

            pe.wait_ge(dst_ready, 1)
            mm(bkL[:, 0:NG], row0[:, :], dstf[:, 0:NET:ET], start=True, stop=True).then_inc(base_bc, 1)
            mm(bkC[:, 0:NHI], zeros_h[:, :], zeros_h[:, 0:NHI], start=True, stop=True).then_inc(hist_used, 1)
            with pe.Fori(0, HC // 2) as c:
                for half in (0, 1):
                    pe.wait_ge(hist_oh, 2 * c + half + 1)
                    for t in range(HT):
                        ins = mm(bkC[:, 0:NHI], bins_lo[:, :, t], bins_hi[:, half, :, t], start=False, stop=False,
                                 skip_group_check=True)
                    ins.then_inc(hist_used, 1)
            pe.wait_ge(viol_ready, 1)
            mm(bkL[:, D:D + 1], ones[:, :], small[:, 2:3], start=True, stop=True).then_inc(viol_sum, 1)

            pe.wait_ge(flag_ready, 1)
            general = pe.value_load(flag_i[0:1, 0:1], min_val=0, max_val=1)
            with pe.If(general != 0):
                pe.sem_inc(slow_sum, 1)
                with pe.Fori(0, NG) as n:
                    wait_count(pe, slow_landed, (n + 1) * (ET * 16))
                    with pe.Fori(0, NSW) as w:
                        pe.wait_ge(slow_oh_ready, n * NSW + w + 1)
                        pe.wait_ge(slow_added, n * NSW + w + 1)
                        for h in range(KD):
                            for j in range(ET):
                                for a in (0, 1):
                                    at = (2 * j + a) * D + h * P
                                    mm(bkA[h][:, :], rows_h[:, 0, at:at + P], slow_oh[:, j, :], start=j + a == 0,
                                       stop=j + a == ET)
                        for j in range(ET):
                            ins = mm(bkC[0:1, :], ones_f[:, :], slow_oh[:, j, :], start=j == 0, stop=j == ET - 1)
                        ins.then_inc(slow_sum, 1)
                pe.wait_ge(slow_added, NG * NSW + 1)

            pe.wait_ge(weights_in, 7 * 16)

            def segment(i, s):
                n = i * PER + s
                pe.wait_ge(landed[s], (i + 1) * (ET * 16))
                pe.wait_ge(oh_ready, n + 1)
                if not (isinstance(n, int) and n < 2):
                    pe.wait_ge(seg_added, n - 1)
                for h in range(KD):
                    for j in range(ET):
                        for a in (0, 1):
                            at = (2 * j + a) * D + h * P
                            mm(segp[s % 2][:, h, :], rows_h[:, s, at:at + P], woh[:, s % 2, j, :], start=j + a == 0,
                               stop=j + a == ET)
                for j in range(ET):
                    ins = mm(segc[s % 2], ones_f[:, :], woh[:, s % 2, j, :], start=j == 0, stop=j == ET - 1)
                ins.then_inc(seg_done, 1)

            def gates(t, hid=hT):
                pe.wait_ge(gelu_done, t + 1)
                if not (isinstance(t, int) and t == 0):
                    pe.wait_ge(lg_read, t)
                for c in range(KH):
                    ins = mm(bkC[0:EX, 0:P], wg_sb[:, c, :], hid[:, c, :], start=c == 0, stop=c == KH - 1)
                ins.then_inc(lgt_done, 1)

            def gates_back(t):
                wait_count(pe, lgt_read, t + 1)
                tr(bkC[:, P:P + EX], lgT[:, :], ident[0:EX, 0:EX]).then_inc(lg_done, 1)

            def transpose_fu(t, first):
                pe.wait_ge(fu_ready, t + 1)
                if not first:
                    pe.wait_ge(l_ready, t)
                for a in range(2):
                    for k in range(KD):
                        q = a * KD + k
                        ins = tr(bkT[:, q * P:(q + 1) * P], fu[:, a, k * P:(k + 1) * P], ident[:, :])
                ins.then_inc(fu_t, 1)

            def embed(t, first):
                pe.wait_ge(l_ready, t + 1)
                if not first:
                    pe.wait_ge(e_ready, t)
                mm(bkE[:, D:D + 1], cnt_t[:, :], ones[0:1, 0:1], start=True, stop=True)
                for q in range(2 * KD):
                    ins = mm(bkE[:, 0:D], lT[:, q, :], gw_sb[:, q, :], start=q == 0, stop=q == 2 * KD - 1)
                ins.then_inc(e_done, 1)

            def transpose_xn(t):
                pe.wait_ge(xn_ready, t + 1)
                if not (isinstance(t, int) and t == 0):
                    pe.wait_ge(xt_ready, t)
                for k in range(KD):
                    ins = tr(bkL[:, k * P:(k + 1) * P], emb2[:, k * P:(k + 1) * P], ident[:, :])
                ins.then_inc(xn_t, 1)

            def hidden_bank(out_bank, b):
                for q in range(4):
                    c = 4 * b + q
                    for k in range(KD):
                        ins = mm(out_bank[:, q * P:(q + 1) * P], w1_sb[:, k, c * P:(c + 1) * P], xT[:, 0, k, :],
                                 start=k == 0, stop=k == KD - 1)
                return ins

            def hidden(t, banks=bkH):
                pe.wait_ge(xt_ready, t + 1)
                if banks is bkH and not (isinstance(t, int) and t == 0):
                    pe.wait_ge(gelu_done, t)
                for b in (0, 1):
                    hidden_bank(banks[b], b).then_inc(h_done[b], 1)

            def body(i):
                tile = not (isinstance(i, int) and i < LATE)
                first = isinstance(i, int) and i == LATE
                t = i - LATE
                segment(i, 0)
                if tile:
                    transpose_fu(t, first)
                    if not first:
                        transpose_xn(t - 1)
                segment(i, 1)
                if tile:
                    embed(t, first)
                segment(i, 2)
                if tile and has_gates(t):
                    gates(t - 2)
                if tile and not first:
                    hidden(t - 1)
                segment(i, 3)
                if tile and has_gates(t):
                    gates_back(t - 2)

            def sum_maxima():
                pe.wait_ge(max_ready, 1)
                mm(bkT[:, 0:3], ones[:, :], wsum[:, 0:3], start=True, stop=True).then_inc(max_sum, 1)
                pe.wait_ge(scales_set, 1)

            edge_loop(pe, body, sum_maxima)
            transpose_fu(NT - 2, False)
            transpose_xn(NT - 3)
            embed(NT - 2, False)
            transpose_fu(NT - 1, False)
            gates(NT - 4)
            gates_back(NT - 4)
            hidden(NT - 3)
            embed(NT - 1, False)
            transpose_xn(NT - 2)
            gates(NT - 3)
            gates_back(NT - 3)
            hidden(NT - 2)
            transpose_xn(NT - 1)
            pe.wait_ge(seg_added, NG)
            hidden(NT - 1, bkA)
            gates(NT - 2)
            gates_back(NT - 2)
            gates(NT - 1, hT_last)
            gates_back(NT - 1)

            pe.wait_ge(oneh_ready, 1)
            flat = oneh_h[:, :, :].rearrange("p t e -> p (t e)")
            mm(bkT[:, 0:LE], upper[:, :], flat, start=True, stop=True)
            mm(bkE[:, 0:LE], ones_h[:, :], flat, start=True, stop=True).then_inc(ranks, 1)
            for t in range(NT):
                if t % GC == 0:
                    c = t // GC
                    pe.wait_ge(lo_ready, c + 1)
                    if c < PC:
                        pe.wait_ge(val_pool, c + 1)
                    else:
                        pe.wait_ge(val_dve, c - PC + 1)
                part, at = lo_at(t)
                ins = mm(bkC[:, 0:4 * NJ], part[:, at, :], hi_val[:, t, :, :].rearrange("p a j -> p (a j)"),
                         start=t == 0, stop=t == NT - 1)
            ins.then_inc(pm_used, 1)

            PRODUCTS = ((0, 0), (0, 1), (1, 0))
            pe.wait_ge(slots_ready, 1)
            pe.wait_ge(wd_split, WI * 3)
            pe.wait_ge(w1_split, 1)

            def transpose_tok(u, s, first):
                j = u * UN + s
                pe.wait_ge(tok_in[s], (u + 1) * 16)
                if not first:
                    pe.wait_ge(t2_read, j - 1)
                for q in range(2 * KD):
                    ins = mm(bkT2[s % 2][:, q * P:(q + 1) * P], trow_h[s][:, q * P:(q + 1) * P], ident_h[:, :],
                             start=True, stop=True)
                ins.then_inc(t2_done, 1)

            def hidden2(u, s, first):
                j = u * UN + s
                pe.wait_ge(t2_read, j + 1)
                if not first:
                    pe.wait_ge(gelu2, 2 * (j - 1))
                for b in (0, 1):
                    for q in range(4):
                        c = 4 * b + q
                        for n, (k, wpart, xpart) in enumerate((k, wp, xp) for k in range(KD) for wp, xp in PRODUCTS):
                            ins = mm((bkH, bkA)[s % 2][b][:, q * P:(q + 1) * P], w1h[:, wpart, k, c * P:(c + 1) * P],
                                     xTh[:, s % 2, xpart * KD + k, :], start=n == 0, stop=n == KD * len(PRODUCTS) - 1)
                    ins.then_inc(h2_done, 1)

            def expert(u, s, first):
                j = u * UN + s
                e = pe.value_load(jexp_i[0:1, bass.ds(j, 1)], min_val=0, max_val=EX - 1)
                pe.wait_ge(h_split, 2 * (j + 1))
                if not first:
                    pe.wait_ge(y_read, j - 1)
                for c in range(KH):
                    for n, (hpart, wpart) in enumerate(PRODUCTS):
                        ins = mm(bkY[s % 2][:, 0:D], hs[:, s % 2, hpart, c * P:(c + 1) * P],
                                 bigh[:, bass.ds(e * (2 * KH * D) + (2 * c + wpart) * D, D)],
                                 start=c + n == 0, stop=c == KH - 1 and n == len(PRODUCTS) - 1)
                ins.then_inc(y_done, 1)

            def steps(u, first, last):
                for s in range(UN):
                    if s < UN - 1:
                        transpose_tok(u, s + 1, first and s + 1 < 2)
                    elif not last:
                        transpose_tok(u + 1, 0, False)
                    hidden2(u, s, first and s < 2)
                    if s:
                        expert(u, s - 1, first and s - 1 < 2)
                    elif not first:
                        expert(u - 1, UN - 1, False)

            transpose_tok(0, 0, True)
            steps(0, True, False)
            with pe.Fori(1, NJ // UN - 1) as u:
                steps(u, False, False)
            steps(NJ // UN - 1, False, True)
            expert(NJ // UN - 1, UN - 1, False)


def kernel(x, src, dst, L0_gnn_W1, L0_gnn_W2, L0_gnn_b, L0_ffn_W1, L0_ffn_b1, L0_ffn_Wg, L0_ffn_bg, L0_ffn_Wd,
           L0_ffn_bd):
    import numpy as np
    import concourse.bacc as bacc
    from concourse.bass_utils import run_bass_kernel_spmd

    nc = bacc.Bacc("TRN2", target_bir_lowering=False, num_devices=1)
    inputs = dict(x=x, src=src, dst=dst, gnn_w1=L0_gnn_W1, gnn_w2=L0_gnn_W2, gnn_b=L0_gnn_b, w1=L0_ffn_W1,
                  b1=L0_ffn_b1, wg=L0_ffn_Wg, bg=L0_ffn_bg, wd=L0_ffn_Wd, bd=L0_ffn_bd)
    arrays, args = {}, []
    for name, a in inputs.items():
        arrays[name] = np.ascontiguousarray(a)
        args.append(nc.dram_tensor(name, arrays[name].shape, mybir.dt.from_np(arrays[name].dtype),
                                   kind="ExternalInput").ap())
    args.append(nc.dram_tensor("out", (N, D), F32, kind="ExternalOutput").ap())
    build(nc, *args)
    r = run_bass_kernel_spmd(nc, [arrays], core_ids=[0])
    return r.results[0]["out"]
```
